# Optimizing a Trainium2 kernel written in Bass

```python
import numpy as np
import jax
import jax.numpy as jnp

def _softmax(x, axis=-1):
    return jax.nn.softmax(x, axis=axis)

def _gelu(x):
    return jax.nn.gelu(x, approximate=True)

def _silu(x):
    return jax.nn.silu(x)

def _sigmoid(x):
    return jax.nn.sigmoid(x)

def _layernorm(x, axis=-1, eps=1e-05):
    m = jnp.mean(x, axis=axis, keepdims=True)
    v = jnp.var(x, axis=axis, keepdims=True)
    return (x - m) / jnp.sqrt(v + eps)

def _scatter_add(tgt, idx, src, axis=0):
    return tgt.at[idx].add(src)

def _segment_sum(src, seg, n):
    return jax.ops.segment_sum(src, seg, n)
kernel_name = 'mk_macaron_d2_jaxref_r8_97e4b3'

def setup_inputs(seed: int=0):
    np.random.seed(seed)
    _w = jnp.asarray

    def _L0_attn_setup():
        import jax, jax.numpy as jnp
        from jax import lax
        import numpy as np
        B, T, C = (8, 256, 128)
        ATT_SCALE = 1.0
        LN_EPS = 1e-05

        def _layernorm(x, g, b):
            mu = jnp.mean(x, axis=-1, keepdims=True)
            var = jnp.mean(jnp.square(x - mu), axis=-1, keepdims=True)
            return (x - mu) * lax.rsqrt(var + LN_EPS) * g + b

        def _wkv_scan(k, v, td):
            kT = jnp.swapaxes(k, 0, 1)
            vT = jnp.swapaxes(v, 0, 1)

            def step(carry, kv):
                num, den = carry
                kt, vt = kv
                den = den * td + kt
                num = num * td + kt * vt
                return ((num, den), num / (den + 1e-08))
            z = jnp.zeros((k.shape[0], k.shape[2]), dtype=k.dtype)
            _, wkvT = lax.scan(step, (z, z), (kT, vT))
            return jnp.swapaxes(wkvT, 0, 1)

        def _reference_tuple_inner(x, time_decay, time_mix_k, time_mix_v, time_mix_r, Wk, Wv, Wr, Wo, ln_g, ln_b):
            x = _layernorm(x, ln_g, ln_b)
            last_x = jnp.pad(x[:, :-1], ((0, 0), (1, 0), (0, 0)))
            k = (x * time_mix_k + last_x * (1.0 - time_mix_k)) @ Wk.T
            v = (x * time_mix_v + last_x * (1.0 - time_mix_v)) @ Wv.T
            r = (x * time_mix_r + last_x * (1.0 - time_mix_r)) @ Wr.T
            k = k * ATT_SCALE
            td = jnp.exp(time_decay)
            wkv = _wkv_scan(jnp.exp(k), v, td)
            out = jax.nn.sigmoid(r) * wkv @ Wo.T
            new_state = x[:, -1:]
            return (out, new_state)
        key = jax.random.key(seed)
        ks = jax.random.split(key, 10)
        scale = 1.0 / np.sqrt(C)
        x = jax.random.normal(ks[0], (B, T, C), dtype=jnp.float32)
        Wk = jax.random.normal(ks[1], (C, C), dtype=jnp.float32) * scale
        Wv = jax.random.normal(ks[2], (C, C), dtype=jnp.float32) * scale
        Wr = jax.random.normal(ks[3], (C, C), dtype=jnp.float32) * scale
        Wo = jax.random.normal(ks[4], (C, C), dtype=jnp.float32) * scale
        decay_init = jnp.linspace(0.1, 0.45, C, dtype=jnp.float32)
        time_decay = jnp.log(decay_init / (1.0 - decay_init))
        time_mix_k = jax.random.uniform(ks[5], (1, 1, C), dtype=jnp.float32) * 0.375
        time_mix_v = jax.random.uniform(ks[6], (1, 1, C), dtype=jnp.float32) * 0.5
        time_mix_r = jax.random.uniform(ks[7], (1, 1, C), dtype=jnp.float32) * 0.375
        ln_g = jnp.ones((C,), dtype=jnp.float32)
        ln_b = jnp.zeros((C,), dtype=jnp.float32)
        return {'x': x, 'time_decay': time_decay, 'time_mix_k': time_mix_k, 'time_mix_v': time_mix_v, 'time_mix_r': time_mix_r, 'Wk': Wk, 'Wv': Wv, 'Wr': Wr, 'Wo': Wo, 'ln_g': ln_g, 'ln_b': ln_b}
    _L0_attn_in = _L0_attn_setup()

    def _L0_ffn_setup():
        import jax, jax.numpy as jnp
        import numpy as np
        NUM_EXPERTS = 8
        EXPERT_CAPACITY = 2.0
        key = jax.random.key(seed)
        k1, k2, k3, k4 = jax.random.split(key, 4)
        B, T, C, H, E = (4, 512, 128, 512, NUM_EXPERTS)
        x = jax.random.normal(k1, (B, T, C), jnp.float32)
        gate_w = jax.random.normal(k2, (C, E), jnp.float32) * 0.02
        w1 = jax.random.normal(k3, (E, C, H), jnp.float32) * 0.02
        w2 = jax.random.normal(k4, (E, H, C), jnp.float32) * 0.02
        return {'x': x, 'gate_w': gate_w, 'w1': w1, 'w2': w2}
    _L0_ffn_in = _L0_ffn_setup()

    def _L1_attn_setup():
        import jax, jax.numpy as jnp
        import numpy as np
        E = 128
        NH = 4
        DH = E // NH
        GATE_SOFT_CAP = 15.0
        NORM_EPS = 1e-06
        BACKEND_EPS = 1e-06

        def soft_cap(x, cap):
            return cap * jnp.tanh(x / cap)

        def mlstm_parallel(q, k, v, ig, fg):
            q = q.transpose(0, 2, 1, 3)
            k = k.transpose(0, 2, 1, 3)
            v = v.transpose(0, 2, 1, 3)
            ig = ig.squeeze(-1).transpose(0, 2, 1)
            fg = fg.squeeze(-1).transpose(0, 2, 1)
            S = q.shape[2]
            log_fg = jax.nn.log_sigmoid(fg)
            lf_cum = jnp.cumsum(log_fg, axis=-1)
            fg_mat = lf_cum[..., :, None] - lf_cum[..., None, :]
            causal = jnp.tril(jnp.ones((S, S), dtype=bool))
            neg_inf = jnp.finfo(q.dtype).min
            log_D = jnp.where(causal, fg_mat + ig[..., None, :], neg_inf)
            m = jnp.max(log_D, axis=-1, keepdims=True)
            D = jnp.exp(log_D - m)
            scores = jnp.einsum('bhid,bhjd->bhij', q, k) / jnp.sqrt(jnp.float32(DH))
            C = scores * D
            n = jnp.maximum(jnp.abs(C.sum(axis=-1, keepdims=True)), jnp.exp(-m))
            h = jnp.einsum('bhij,bhjd->bhid', C, v) / (n + BACKEND_EPS)
            return h.transpose(0, 2, 1, 3)

        def multi_head_norm(h, w, eps):
            mu = h.mean(axis=-1, keepdims=True)
            var = ((h - mu) ** 2).mean(axis=-1, keepdims=True)
            return (h - mu) * jax.lax.rsqrt(var + eps) * w
        key = jax.random.key(seed)
        ks = jax.random.split(key, 12)
        B, S = (2, 256)
        sd = 1.0 / np.sqrt(E)
        x = jax.random.normal(ks[0], (B, S, E), jnp.float32)
        Wq = jax.random.normal(ks[1], (E, E), jnp.float32) * sd
        Wk = jax.random.normal(ks[2], (E, E), jnp.float32) * sd
        Wv = jax.random.normal(ks[3], (E, E), jnp.float32) * sd
        Wo = jax.random.normal(ks[4], (E, E), jnp.float32) * sd
        Wig = jax.random.normal(ks[5], (E, NH), jnp.float32) * 0.01
        big = jax.random.normal(ks[6], (NH,), jnp.float32) * 0.1 - 10.0
        Wfg = jax.random.normal(ks[7], (E, NH), jnp.float32) * 0.01
        bfg = jnp.linspace(3.0, 6.0, NH, dtype=jnp.float32)
        norm_w = jnp.ones((NH, DH), jnp.float32)
        Wdown = jax.random.normal(ks[8], (E, E), jnp.float32) * sd
        return {'x': x, 'Wq': Wq, 'Wk': Wk, 'Wv': Wv, 'Wo': Wo, 'Wig': Wig, 'big': big, 'Wfg': Wfg, 'bfg': bfg, 'norm_w': norm_w, 'Wdown': Wdown}
    _L1_attn_in = _L1_attn_setup()

    def _L1_ffn_setup():
        import jax, jax.numpy as jnp
        import numpy as np
        B, S, D, M, E, K = (2, 256, 128, 176, 8, 2)
        key = jax.random.key(seed)
        k0, k1, k2, k3, k4 = jax.random.split(key, 5)
        scale = 0.02
        return {'x': jax.random.normal(k0, (B, S, D), dtype=jnp.float32), 'w_gate': jax.random.normal(k1, (D, E), dtype=jnp.float32) * scale, 'w_g': jax.random.normal(k2, (E, D, M), dtype=jnp.float32) * scale, 'w_u': jax.random.normal(k3, (E, D, M), dtype=jnp.float32) * scale, 'w_d': jax.random.normal(k4, (E, M, D), dtype=jnp.float32) * scale}
    _L1_ffn_in = _L1_ffn_setup()
    _d = {'L0_attn_x': _L0_attn_in['x'], 'L0_attn_time_decay': _L0_attn_in['time_decay'], 'L0_attn_time_mix_k': _L0_attn_in['time_mix_k'], 'L0_attn_time_mix_v': _L0_attn_in['time_mix_v'], 'L0_attn_time_mix_r': _L0_attn_in['time_mix_r'], 'L0_attn_Wk': _L0_attn_in['Wk'], 'L0_attn_Wv': _L0_attn_in['Wv'], 'L0_attn_Wr': _L0_attn_in['Wr'], 'L0_attn_Wo': _L0_attn_in['Wo'], 'L0_attn_ln_g': _L0_attn_in['ln_g'], 'L0_attn_ln_b': _L0_attn_in['ln_b'], 'L0_ffn_gate_w': _L0_ffn_in['gate_w'], 'L0_ffn_w1': _L0_ffn_in['w1'], 'L0_ffn_w2': _L0_ffn_in['w2'], 'L1_attn_Wq': _L1_attn_in['Wq'], 'L1_attn_Wk': _L1_attn_in['Wk'], 'L1_attn_Wv': _L1_attn_in['Wv'], 'L1_attn_Wo': _L1_attn_in['Wo'], 'L1_attn_Wig': _L1_attn_in['Wig'], 'L1_attn_big': _L1_attn_in['big'], 'L1_attn_Wfg': _L1_attn_in['Wfg'], 'L1_attn_bfg': _L1_attn_in['bfg'], 'L1_attn_norm_w': _L1_attn_in['norm_w'], 'L1_attn_Wdown': _L1_attn_in['Wdown'], 'L1_ffn_w_gate': _L1_ffn_in['w_gate'], 'L1_ffn_w_g': _L1_ffn_in['w_g'], 'L1_ffn_w_u': _L1_ffn_in['w_u'], 'L1_ffn_w_d': _L1_ffn_in['w_d']}
    _x0 = _d['L0_attn_x']
    _d['L0_attn_x'] = jax.random.normal(jax.random.fold_in(jax.random.key(seed), 1), (32, 256, 128), dtype=_x0.dtype)
    del _x0
    return _d

def reference(L0_attn_x, L0_attn_time_decay, L0_attn_time_mix_k, L0_attn_time_mix_v, L0_attn_time_mix_r, L0_attn_Wk, L0_attn_Wv, L0_attn_Wr, L0_attn_Wo, L0_attn_ln_g, L0_attn_ln_b, L0_ffn_gate_w, L0_ffn_w1, L0_ffn_w2, L1_attn_Wq, L1_attn_Wk, L1_attn_Wv, L1_attn_Wo, L1_attn_Wig, L1_attn_big, L1_attn_Wfg, L1_attn_bfg, L1_attn_norm_w, L1_attn_Wdown, L1_ffn_w_gate, L1_ffn_w_g, L1_ffn_w_u, L1_ffn_w_d):

    def _L0_attn_ref(x, time_decay, time_mix_k, time_mix_v, time_mix_r, Wk, Wv, Wr, Wo, ln_g, ln_b):
        import jax, jax.numpy as jnp
        from jax import lax
        import numpy as np
        B, T, C = (8, 256, 128)
        ATT_SCALE = 1.0
        LN_EPS = 1e-05

        def _layernorm(x, g, b):
            mu = jnp.mean(x, axis=-1, keepdims=True)
            var = jnp.mean(jnp.square(x - mu), axis=-1, keepdims=True)
            return (x - mu) * lax.rsqrt(var + LN_EPS) * g + b

        def _wkv_scan(k, v, td):
            kT = jnp.swapaxes(k, 0, 1)
            vT = jnp.swapaxes(v, 0, 1)

            def step(carry, kv):
                num, den = carry
                kt, vt = kv
                den = den * td + kt
                num = num * td + kt * vt
                return ((num, den), num / (den + 1e-08))
            z = jnp.zeros((k.shape[0], k.shape[2]), dtype=k.dtype)
            _, wkvT = lax.scan(step, (z, z), (kT, vT))
            return jnp.swapaxes(wkvT, 0, 1)

        def _reference_tuple_inner(x, time_decay, time_mix_k, time_mix_v, time_mix_r, Wk, Wv, Wr, Wo, ln_g, ln_b):
            x = _layernorm(x, ln_g, ln_b)
            last_x = jnp.pad(x[:, :-1], ((0, 0), (1, 0), (0, 0)))
            k = (x * time_mix_k + last_x * (1.0 - time_mix_k)) @ Wk.T
            v = (x * time_mix_v + last_x * (1.0 - time_mix_v)) @ Wv.T
            r = (x * time_mix_r + last_x * (1.0 - time_mix_r)) @ Wr.T
            k = k * ATT_SCALE
            td = jnp.exp(time_decay)
            wkv = _wkv_scan(jnp.exp(k), v, td)
            out = jax.nn.sigmoid(r) * wkv @ Wo.T
            new_state = x[:, -1:]
            return (out, new_state)
        return _reference_tuple_inner(x, time_decay, time_mix_k, time_mix_v, time_mix_r, Wk, Wv, Wr, Wo, ln_g, ln_b)[0]

    def _L0_ffn_ref(x, gate_w, w1, w2):
        import jax, jax.numpy as jnp
        import numpy as np
        NUM_EXPERTS = 8
        EXPERT_CAPACITY = 2.0
        B, T, C = x.shape
        E = gate_w.shape[1]
        cap = int(EXPERT_CAPACITY * T / E)
        scores = jnp.einsum('BTC,CE->BTE', x, gate_w)
        probs = jax.nn.softmax(scores, axis=-1)
        probs_et = jnp.transpose(probs, (0, 2, 1))
        top_p, top_idx = jax.lax.top_k(probs_et, cap)
        xin = jnp.take_along_axis(x[:, None, :, :], top_idx[..., None], axis=2)
        h = jax.nn.gelu(jnp.einsum('BElC,ECH->BElH', xin, w1), approximate=False)
        y = jnp.einsum('BElH,EHC->BElC', h, w2)
        y = y * top_p[..., None]
        b_idx = jnp.arange(B)[:, None, None]
        out = jnp.zeros((B, T, C), x.dtype).at[b_idx, top_idx].add(y)
        return out

    def _L1_attn_ref(x, Wq, Wk, Wv, Wo, Wig, big, Wfg, bfg, norm_w, Wdown):
        import jax, jax.numpy as jnp
        import numpy as np
        E = 128
        NH = 4
        DH = E // NH
        GATE_SOFT_CAP = 15.0
        NORM_EPS = 1e-06
        BACKEND_EPS = 1e-06

        def soft_cap(x, cap):
            return cap * jnp.tanh(x / cap)

        def mlstm_parallel(q, k, v, ig, fg):
            q = q.transpose(0, 2, 1, 3)
            k = k.transpose(0, 2, 1, 3)
            v = v.transpose(0, 2, 1, 3)
            ig = ig.squeeze(-1).transpose(0, 2, 1)
            fg = fg.squeeze(-1).transpose(0, 2, 1)
            S = q.shape[2]
            log_fg = jax.nn.log_sigmoid(fg)
            lf_cum = jnp.cumsum(log_fg, axis=-1)
            fg_mat = lf_cum[..., :, None] - lf_cum[..., None, :]
            causal = jnp.tril(jnp.ones((S, S), dtype=bool))
            neg_inf = jnp.finfo(q.dtype).min
            log_D = jnp.where(causal, fg_mat + ig[..., None, :], neg_inf)
            m = jnp.max(log_D, axis=-1, keepdims=True)
            D = jnp.exp(log_D - m)
            scores = jnp.einsum('bhid,bhjd->bhij', q, k) / jnp.sqrt(jnp.float32(DH))
            C = scores * D
            n = jnp.maximum(jnp.abs(C.sum(axis=-1, keepdims=True)), jnp.exp(-m))
            h = jnp.einsum('bhij,bhjd->bhid', C, v) / (n + BACKEND_EPS)
            return h.transpose(0, 2, 1, 3)

        def multi_head_norm(h, w, eps):
            mu = h.mean(axis=-1, keepdims=True)
            var = ((h - mu) ** 2).mean(axis=-1, keepdims=True)
            return (h - mu) * jax.lax.rsqrt(var + eps) * w
        B, S, _ = x.shape
        q = (x @ Wq).reshape(B, S, NH, DH)
        k = (x @ Wk).reshape(B, S, NH, DH)
        v = (x @ Wv).reshape(B, S, NH, DH)
        o = x @ Wo
        ig = soft_cap(x @ Wig + big, GATE_SOFT_CAP)[..., None]
        fg = soft_cap(x @ Wfg + bfg, GATE_SOFT_CAP)[..., None]
        h = mlstm_parallel(q, k, v, ig, fg)
        hn = multi_head_norm(h, norm_w, NORM_EPS).reshape(B, S, -1)
        h_out = jax.nn.sigmoid(o) * hn
        return h_out @ Wdown

    def _L1_ffn_ref(x, w_gate, w_g, w_u, w_d):
        import jax, jax.numpy as jnp
        import numpy as np
        B, S, D, M, E, K = (2, 256, 128, 176, 8, 2)
        scores = x @ w_gate
        topk_scores, topk_idx = jax.lax.top_k(scores, K)
        topk_probs = jax.nn.softmax(topk_scores, axis=-1)
        gating = jnp.sum(jax.nn.one_hot(topk_idx, E, dtype=topk_probs.dtype) * topk_probs[..., None], axis=-2)
        hidden = jax.nn.silu(jnp.einsum('bsd,edm->ebsm', x, w_g)) * jnp.einsum('bsd,edm->ebsm', x, w_u)
        expert_out = jnp.einsum('ebsm,emd->ebsd', hidden, w_d)
        y = jnp.einsum('bse,ebsd->bsd', gating, expert_out)
        return y
    x = L0_attn_x
    x = x + 0.5 * _L0_ffn_ref(_layernorm(x, axis=-1), L0_ffn_gate_w, L0_ffn_w1, L0_ffn_w2)
    x = x + _L0_attn_ref(_layernorm(x, axis=-1), L0_attn_time_decay, L0_attn_time_mix_k, L0_attn_time_mix_v, L0_attn_time_mix_r, L0_attn_Wk, L0_attn_Wv, L0_attn_Wr, L0_attn_Wo, L0_attn_ln_g, L0_attn_ln_b)
    x = x + 0.5 * _L0_ffn_ref(_layernorm(x, axis=-1), L0_ffn_gate_w, L0_ffn_w1, L0_ffn_w2)
    x = x + 0.5 * _L1_ffn_ref(_layernorm(x, axis=-1), L1_ffn_w_gate, L1_ffn_w_g, L1_ffn_w_u, L1_ffn_w_d)
    x = x + _L1_attn_ref(_layernorm(x, axis=-1), L1_attn_Wq, L1_attn_Wk, L1_attn_Wv, L1_attn_Wo, L1_attn_Wig, L1_attn_big, L1_attn_Wfg, L1_attn_bfg, L1_attn_norm_w, L1_attn_Wdown)
    x = x + 0.5 * _L1_ffn_ref(_layernorm(x, axis=-1), L1_ffn_w_gate, L1_ffn_w_g, L1_ffn_w_u, L1_ffn_w_d)
    return x

_drawn_inputs = setup_inputs


def setup_inputs(seed=0):
    import zlib

    import numpy as np

    out = dict(_drawn_inputs(seed))
    spreads = {'L0_attn_ln_g': (1.0, 0.2), 'L0_attn_ln_b': (0.0, 0.1), 'L1_attn_norm_w': (1.0, 0.6)}
    factors = {'L0_ffn_gate_w': 5.262,
     'L0_ffn_w1': 4.609,
     'L0_ffn_w2': 4.548,
     'L1_attn_Wig': 22.488,
     'L1_attn_big': 52.784,
     'L1_attn_Wfg': 64.0,
     'L1_ffn_w_gate': 8.0,
     'L1_ffn_w_g': 8.0,
     'L1_ffn_w_u': 8.0,
     'L1_ffn_w_d': 8.0,
     'L1_attn_Wq': 7.964,
     'L1_attn_Wk': 6.733,
     'L1_attn_Wv': 5.008,
     'L1_attn_Wo': 8.0,
     'L1_attn_bfg': 8.0,
     'L1_attn_Wdown': 5.935}
    for name, (base, spread) in spreads.items():
        noise = np.random.default_rng([zlib.crc32(name.encode()), seed]).standard_normal(out[name].shape)
        drawn = base * np.exp(spread * noise) if base else spread * noise
        out[name] = jnp.asarray(drawn.astype(out[name].dtype))
    for name, factor in factors.items():
        out[name] = (out[name] * factor).astype(out[name].dtype)
    return out
```

```python
import math
from contextlib import ExitStack

import concourse.bass as bass
from concourse import mybir

F32 = mybir.dt.float32
F32R = mybir.dt.float32r
U32 = mybir.dt.uint32
ACT = mybir.ActivationFunctionType
ALU = mybir.AluOpType
AX = mybir.AxisListType

P = 128
B, T, C = 32, 256, 128
TP = T // P
NT = B * TP
E = 8
H0 = 512
HC = H0 // P
CAP = 2 * T // E
SLOTS = E * CAP
EP = E // 2
M1 = 176
HID = E * M1
NCH = HID // P
SL = 2 * M1
NH, DH = 4, 32
EPS_LN = 1e-5
EPS_HEAD = 1e-6
CAPG = 15.0
BIG = 1.0e30
XC = 4

LAYERS = ("choice", "rwkv", "choice", "top2", "mlstm", "top2")


def need(eng, sem, value):
    if isinstance(value, int) and value <= 0:
        return
    eng.wait_ge(sem, value)


def apart(eng, sem, value, passed):
    if not (isinstance(value, int) and value <= 0):
        eng.wait_ge(sem, value).then_inc(passed, 1)


def inside(b, n=B):
    return not isinstance(b, int) or 0 <= b < n


def pipeline(eng, step, first, last, lo, hi, o=0):
    for s in range(first, lo):
        step(o + s, s % 2)
    with eng.Fori((o + lo) // 2, (o + hi + 1) // 2) as i:
        for u in range(2):
            step(2 * i + u, u)
    for s in range(hi + 1, last + 1):
        step(o + s, s % 2)


class Layer:

    def stand(self, layer, run):
        self.layer, self.run, self.o = layer, run, run * B
        self.x0 = layer * B - self.o
        self.norm.layer, self.norm.o = layer, self.o

    def moments_next(self, dve, b, u):
        if self.has(b):
            self.sh.moments.moments_of(dve, self.layer + 1, b - self.o, u)

    def scale_next(self, pool, b, u):
        if self.has(b):
            self.sh.moments.scale(pool, self.layer + 1, b - self.o, u)

    def has(self, b):
        return not isinstance(b, int) or inside(b - self.o)


class Chain:

    def __init__(self, sem, per, base=0):
        self.sem, self.per, self.base = sem, per, base

    def begin(self, b):
        self.b, self.k = b, 0

    def link(self, eng, ins, passed=None):
        self.k += 1
        ins.then_inc(self.sem, 1)
        if passed is not None:
            apart(eng, self.sem, self.base + self.b * self.per + self.k, passed)
        else:
            eng.wait_ge(self.sem, self.base + self.b * self.per + self.k)

    def end(self):
        assert self.k == self.per, (self.k, self.per)


class Memory:

    def __init__(self, nc, base):
        self.nc, self.at, self.top = nc, base, 0

    def take(self, name, shape, dtype=F32):
        n = 4
        for d in shape[1:]:
            n *= d
        t = self.nc.alloc_sbuf_tensor_at(name, shape, dtype, offset=self.at)
        self.at += (n + 31) // 32 * 32
        self.top = max(self.top, self.at)
        assert self.at <= self.nc.sbuf_usable_end, (name, self.at)
        return t


class Shared:

    def __init__(self, nc, ctx, args):
        self.nc, self.ctx, self.args = nc, ctx, args
        self.mem = Memory(nc, (nc.sbuf_base + 63) // 64 * 64)
        m = self.mem
        self.X = m.take("X", [P, NT, C])
        self.ident = m.take("ident", [P, P])
        self.mhalf = m.take("minus_half", [P, 16])
        self.mone = m.take("minus_one", [P, TP])
        self.euler = m.take("e", [P, TP])
        self.iota_tok = m.take("iota_tok", [P, T])
        self.iota_part = m.take("iota_part", [P, TP])
        self.iota_i = m.take("iota_tok_int", [P, T], mybir.dt.int32)
        self.iota_pi = m.take("iota_part_int", [P, TP], mybir.dt.int32)
        self.banks = [ctx.enter_context(nc.psum_tensor(f"bank{i}", [P, 512], F32)) for i in range(8)]
        self.x_loaded = [self.sem(f"x_loaded{c}") for c in range(XC)]
        self.consts = self.sem("consts_ready")
        self.passed = self.sem("passed")
        self.x_done = self.sem("x_done")
        self.stored = self.sem("stored")
        self.moments = Moments(self)

    def sem(self, name):
        return self.ctx.enter_context(self.nc.semaphore(name))

    N_CONSTS = 9

    def start(self, eng, x0):
        if x0:
            eng.wait_ge(self.x_done, x0)
        else:
            for sem in self.x_loaded:
                eng.wait_ge(sem, 16)

    def moments_first(self, dve):
        n = B // XC
        for c in range(XC):
            dve.wait_ge(self.x_loaded[c], 16)
            pipeline(dve, lambda b, u: self.moments.moments_of(dve, 0, b, u), c * n, c * n + n - 1, c * n + 2 * (c == 0), c * n + n - 1)

    def scale_first(self, pool):
        pipeline(pool, lambda b, u: self.moments.scale(pool, 0, b, u), 0, B - 1, 2, B - 3)

    def constants(self, pool):
        nc = self.nc
        pool.memset(self.ident[:, :], 0.0).then_inc(self.consts, 1)
        pool.memset(self.mhalf[:, :], -0.5).then_inc(self.consts, 1)
        pool.memset(self.mone[:, :], -1.0).then_inc(self.consts, 1)
        pool.memset(self.euler[:, :], math.e).then_inc(self.consts, 1)
        pool.iota(self.iota_i[:, :], [[1, T]], base=0, channel_multiplier=0).then_inc(self.consts, 1)
        pool.iota(self.iota_pi[:, :], [[P, TP]], base=0, channel_multiplier=1).then_inc(self.consts, 1)
        pool.wait_ge(self.consts, 6)
        pool.affine_select(out=self.ident[:, :], in_=self.ident[:, :], compare_op=ALU.not_equal, fill=1.0,
                           base=0, pattern=[[-1, P]], channel_multiplier=1).then_inc(self.consts, 1)
        pool.tensor_copy(self.iota_tok[:, :], self.iota_i[:, :]).then_inc(self.consts, 1)
        pool.tensor_copy(self.iota_part[:, :], self.iota_pi[:, :]).then_inc(self.consts, 1)


class Moments:

    def __init__(self, sh):
        mem, self.sh = sh.mem, sh
        self.st = mem.take("bnstats", [P, 2, TP, 6])
        self.mv = mem.take("moments", [P, 2, TP, 2])
        self.small = mem.take("rstd_steps", [P, 2, 4, TP])
        self.nm = mem.take("negmean", [P, B, TP])
        self.rs = mem.take("rstd", [P, B, TP])
        self.stats, self.moments, self.scaled = sh.sem("stats_done"), sh.sem("moments_done"), sh.sem("scaled")
        steps = sh.sem("rstd_steps")
        self.chains, base = [], 0
        for kind in LAYERS:
            self.chains.append(Chain(steps, self.PER[kind == "rwkv"], base))
            base += B * self.PER[kind == "rwkv"]

    PER = (1, 6)

    def moments_of(self, dve, layer, b, u):
        if layer == len(LAYERS) or not inside(b):
            return
        n = layer * B + b
        if layer:
            apart(dve, self.sh.x_done, n - B + 1, self.sh.passed)
        apart(dve, self.scaled, n - 1, self.sh.passed)
        for t in range(TP):
            i = dve.bn_stats(self.st[:, u, t, :], self.sh.X[:, bass.ds(TP * b + t, 1), :])
        i.then_inc(self.stats, 1)
        apart(dve, self.stats, n + 1, self.sh.passed)
        for t in range(TP):
            i = dve.bn_aggr(self.mv[:, u, t, :], self.st[:, u, t, :])
        i.then_inc(self.moments, 1)

    def scale(self, pool, layer, b, u):
        if layer == len(LAYERS) or not inside(b):
            return
        n, sm, ch = layer * B + b, self.small, self.chains[layer]
        flat = lambda t: t[:, bass.ds(b, 1), :].rearrange("p a t -> p (a t)")
        half = self.sh.mhalf[:, 0:TP]
        ch.begin(b)
        apart(pool, self.moments, n + 1, self.sh.passed)
        var = self.mv[:, u, :, 1]
        pool.tensor_tensor(flat(self.nm), self.mv[:, u, :, 0], self.sh.mone[:, 0:TP], ALU.mult)
        ch.link(pool, pool.tensor_scalar(sm[:, u, 0, :], var, 1.0, EPS_LN, ALU.mult, ALU.add))
        if ch.per > 1:
            ch.link(pool, pool.tensor_tensor(sm[:, u, 1, :], sm[:, u, 0, :], half, ALU.pow))
            ch.link(pool, pool.tensor_tensor(sm[:, u, 2, :], sm[:, u, 1, :], sm[:, u, 1, :], ALU.mult))
            ch.link(pool, pool.tensor_tensor(sm[:, u, 2, :], sm[:, u, 2, :], var, ALU.mult), self.sh.passed)
            ch.link(pool, pool.tensor_scalar(sm[:, u, 2, :], sm[:, u, 2, :], 1.0, EPS_LN, ALU.mult, ALU.add))
            ch.link(pool, pool.tensor_tensor(sm[:, u, 3, :], sm[:, u, 2, :], half, ALU.pow))
            i = pool.tensor_tensor(flat(self.rs), sm[:, u, 1, :], sm[:, u, 3, :], ALU.mult)
        else:
            i = pool.tensor_tensor(flat(self.rs), sm[:, u, 0, :], half, ALU.pow)
        ch.end()
        i.then_inc(self.scaled, 1)


class Normed:

    def __init__(self, sh, tag, mem):
        self.sh, self.layer, self.o = sh, 0, 0
        self.xn = mem.take(f"{tag}_xn", [P, 2, TP, C])
        self.centred, self.done = sh.sem(f"{tag}_xn_centred"), sh.sem(f"{tag}_xn_done")

    def both(self, b):
        m, at = self.sh.moments, bass.ds(b - self.o, 1)
        return (t[:, at, :].rearrange("p a t -> p (a t)") for t in (m.nm, m.rs))

    def gpsimd(self, pool, b, u, xn_free):
        apart(pool, self.sh.moments.scaled, self.layer * B + b - self.o + 1, self.sh.passed)
        xn_free()
        self.spread(pool, b, u, self.centred, self.done)

    def spread(self, pool, b, u, centred, done):
        nm, rs = (t.unsqueeze(2).to_broadcast([P, TP, C]) for t in self.both(b))
        xn = self.xn[:, u, :, :]
        pool.tensor_tensor(xn, self.sh.X[:, bass.ds(TP * (b - self.o), TP), :], nm, ALU.add).then_inc(centred, 1)
        apart(pool, centred, b + 1, self.sh.passed)
        pool.tensor_tensor(xn, xn, rs, ALU.mult).then_inc(done, 1)

    def vector(self, dve, b, u, xn_free):
        apart(dve, self.sh.moments.scaled, self.layer * B + b - self.o + 1, self.sh.passed)
        xn_free()
        nm, rs = self.both(b)
        for t in range(TP):
            i = dve.tensor_scalar(self.xn[:, u, t, :], self.sh.X[:, bass.ds(TP * (b - self.o) + t, 1), :].rearrange("p a c -> p (a c)"),
                                  nm[:, t:t + 1], rs[:, t:t + 1], ALU.add, ALU.mult)
        i.then_inc(self.done, 1)


class Top2(Layer):

    def __init__(self, sh, tag, w, mem):
        self.sh, self.w = sh, w
        self.norm = Normed(sh, tag, mem)
        f = lambda n, s, d=F32: mem.take(f"{tag}_{n}", s, d)
        self.xhi = f("xhi", [P, 2, T], F32R)
        self.xlo = f("xlo", [P, 2, T], F32R)
        self.silu = f("silu", [P, 2, SL])
        self.sc = f("scores", [P, 2, TP, E])
        self.top = f("top8", [P, 2, TP, 8])
        self.idx = f("top8_index", [P, 2, TP, 8], U32)
        self.idxf = f("top2_index", [P, 2, TP, 2])
        self.g = f("gate_small", [P, 2, 5, TP])
        self.one = f("gate_onehot", [P, 2, 2, TP, E])
        self.gate = f("gate", [P, 2, TP, E])
        self.big = mem.at
        self.hid = f("hid", [P, 2, TP, HID])
        self.hhi = f("hhi", [P, NCH + 1, T], F32R)
        self.hlo = f("hlo", [P, NCH + 1, T], F32R)
        self.yT = f("yT", [P, T])
        bk = sh.banks
        self.pg, self.pu, self.pt = bk[0:2], bk[2:4], bk[4:6]
        self.py, self.pm = bk[6], bk[7]
        s = lambda n: sh.sem(f"{tag}_{n}")
        self.xT_ready, self.xhi_done, self.xlo_done = s("xT_ready"), s("xhi_done"), s("xlo_done")
        self.scores_ready, self.gap_done, self.gexp_done = s("scores_ready"), s("gap_done"), s("gexp_done")
        self.chain = Chain(s("gate_steps"), 9)
        self.gate_done = s("gate_done")
        self.gu_done, self.silu_done, self.hid_done = s("gu_done"), s("silu_done"), s("hid_done")
        self.tr_done, self.hhi_done, self.hlo_done = s("tr_done"), s("hhi_done"), s("hlo_done")
        self.y_done, self.yev_done, self.ytr_done = s("y_done"), s("yev_done"), s("ytr_done")

    NG = (NCH + 1) // 2

    def steps(self, eng, step, pre):
        self.sh.start(eng, self.layer * B)
        pre()
        pipeline(eng, step, 0, B + 1, 2, B - 3, self.o)

    def tensor(self, pe):
        sh, w, ident = self.sh, self.w, self.sh.ident

        def transposes(b, u):
            pe.wait_ge(self.norm.done, b + 1)
            need(pe, self.xlo_done, b)
            for t in range(TP):
                i = pe.transpose(self.pm[:, t * P:(t + 1) * P], self.norm.xn[:, u, t, :], ident[:, :])
            i.then_inc(self.xT_ready, 1)

        def scores(b, u):
            pe.wait_ge(self.xlo_done, b + 1)
            need(pe, self.gap_done, b)
            for t in range(TP):
                o = self.pm[:, T + t * E:T + (t + 1) * E]
                hi, lo = self.xhi[:, u, t * P:(t + 1) * P], self.xlo[:, u, t * P:(t + 1) * P]
                pe.matmul(o, hi, w.gate_hi[:, :], start=True, stop=False)
                pe.matmul(o, hi, w.gate_lo[:, :], start=False, stop=False)
                i = pe.matmul(o, lo, w.gate_hi[:, :], start=False, stop=True)
            i.then_inc(self.scores_ready, 1)

        def gate_up(b, u, k):
            t, q = divmod(k, E // 2)
            hi, lo = self.xhi[:, u, t * P:(t + 1) * P], self.xlo[:, u, t * P:(t + 1) * P]
            g, up = self.pg[k % 2][:, 0:SL], self.pu[k % 2][:, 0:SL]
            c = slice(q * SL, (q + 1) * SL)
            if k == 0:
                pe.wait_ge(self.xlo_done, b + 1)
            need(pe, self.hid_done, 8 * b + k - 1)
            pe.matmul(g, hi, w.g_hi[:, c], start=True, stop=False)
            pe.matmul(g, hi, w.g_lo[:, c], start=False, stop=False)
            pe.matmul(up, hi, w.u_hi[:, c], start=True, stop=False)
            pe.matmul(up, hi, w.u_lo[:, c], start=False, stop=False)
            pe.matmul(g, lo, w.g_hi[:, c], start=False, stop=True)
            pe.matmul(up, lo, w.u_hi[:, c], start=False, stop=True).then_inc(self.gu_done, 1)

        def turn(b, u, j):
            if j == 0:
                pe.wait_ge(self.hid_done, 8 * b + 8)
            need(pe, self.hlo_done, self.NG * b + j - 1)
            for c in range(2 * j, min(2 * j + 2, NCH)):
                for t in range(TP):
                    o = (c % 2) * T + t * P
                    i = pe.transpose(self.pt[j % 2][:, o:o + P], self.hid[:, u, t, c * P:(c + 1) * P], ident[:, :])
            i.then_inc(self.tr_done, 1)

        def down(b):
            pe.wait_ge(self.hlo_done, self.NG * (b + 1))
            need(pe, self.yev_done, b)
            o = self.py[:, 0:T]
            for c in range(NCH):
                pe.matmul(o, w.d_hi[:, c, :], self.hhi[:, c, :], start=(c == 0), stop=False)
                pe.matmul(o, w.d_hi[:, c, :], self.hlo[:, c, :], start=False, stop=False)
                i = pe.matmul(o, w.d_lo[:, c, :], self.hhi[:, c, :], start=False, stop=(c == NCH - 1))
            i.then_inc(self.y_done, 1)

        def turn_back(b):
            pe.wait_ge(self.yev_done, b + 1)
            need(pe, sh.x_done, self.x0 + b)
            for t in range(TP):
                i = pe.transpose(self.py[:, T + t * P:T + (t + 1) * P], self.yT[:, t * P:(t + 1) * P], ident[:, :])
            i.then_inc(self.ytr_done, 1)

        def step(s, u):
            for k in range(8):
                if self.has(s):
                    gate_up(s, u, k)
                if k == 0 and self.has(s - 2):
                    turn_back(s - 2)
                if 1 <= k <= self.NG and self.has(s - 1):
                    turn(s - 1, 1 - u, k - 1)
                if k == 2 and self.has(s + 1):
                    transposes(s + 1, 1 - u)
                if k == 5 and self.has(s + 1):
                    scores(s + 1, 1 - u)
            if self.has(s - 1):
                down(s - 1)

        def pre():
            pe.wait_ge(sh.consts, sh.N_CONSTS)
            w.ready(pe)
            transposes(self.o, 0)
            scores(self.o, 0)

        self.steps(pe, step, pre)

    def scalar(self, act):
        def xhi(b, u):
            act.wait_ge(self.xT_ready, b + 1)
            need(act, self.gu_done, 8 * (b - 1))
            act.activation(self.xhi[:, u, :], self.pm[:, 0:T], ACT.Copy).then_inc(self.xhi_done, 1)

        def silu(b, u, k):
            act.wait_ge(self.gu_done, 8 * b + k + 1)
            need(act, self.hid_done, 8 * b + k - 1)
            act.activation(self.silu[:, k % 2, :], self.pg[k % 2][:, 0:SL], ACT.Silu).then_inc(self.silu_done, 1)

        def hhi(b, j):
            act.wait_ge(self.tr_done, self.NG * b + j + 1)
            if j == 0:
                need(act, self.y_done, b)
            n = T * (min(2 * j + 2, NCH) - 2 * j)
            o = self.hhi[:, 2 * j:2 * j + n // T, :].rearrange("p c t -> p (c t)")
            act.activation(o, self.pt[j % 2][:, 0:n], ACT.Copy).then_inc(self.hhi_done, 1)

        def yev(b):
            act.wait_ge(self.y_done, b + 1)
            need(act, self.ytr_done, b)
            act.activation(self.yT[:, :], self.py[:, 0:T], ACT.Copy).then_inc(self.yev_done, 1)

        def step(s, u):
            if self.has(s - 2):
                yev(s - 2)
            for k in range(8):
                if self.has(s):
                    silu(s, u, k)
                if 1 <= k <= self.NG and self.has(s - 1):
                    hhi(s - 1, k - 1)
                if k == 2 and self.has(s + 1):
                    xhi(s + 1, 1 - u)

        def pre():
            self.w.split.scalar_once(act)
            xhi(self.o, 0)

        self.steps(act, step, pre)

    def vector(self, dve):
        sh, X = self.sh, self.sh.X
        ch = self.chain

        def xlo(b, u):
            dve.wait_ge(self.xhi_done, b + 1)
            dve.tensor_tensor(self.xlo[:, u, :], self.pm[:, 0:T], self.xhi[:, u, :].bitcast(F32),
                              ALU.subtract).then_inc(self.xlo_done, 1)

        def choose(b, u):
            ch.begin(b)
            dve.wait_ge(self.scores_ready, b + 1)
            sc, top, idx = self.sc[:, u, :, :], self.top, self.idx
            ch.link(dve, dve.tensor_copy(sc.rearrange("p t e -> p (t e)"), self.pm[:, T:T + TP * E]), sh.passed)
            for t in range(TP):
                i = dve.max(top[:, u, t, :], self.sc[:, u, t, :])
            ch.link(dve, i)
            dve.tensor_tensor(self.g[:, u, 0, :], top[:, u, :, 1], top[:, u, :, 0], ALU.subtract).then_inc(self.gap_done, 1)
            for t in range(TP):
                i = dve.max_index(idx[:, u, t, :], top[:, u, t, :], self.sc[:, u, t, :])
            ch.link(dve, i)
            ch.link(dve, dve.tensor_copy(self.idxf[:, u, :, :], idx[:, u, :, 0:2]))

        def weigh(b, u):
            g = self.g
            dve.wait_ge(self.gexp_done, b + 1)
            ch.link(dve, dve.tensor_scalar(g[:, u, 2, :], g[:, u, 1, :], 1.0, None, ALU.add))
            ch.link(dve, dve.reciprocal(g[:, u, 2, :], g[:, u, 2, :]))
            ch.link(dve, dve.tensor_scalar(g[:, u, 3, :], g[:, u, 2, :], 0.5, None, ALU.mult))
            ch.link(dve, dve.tensor_tensor(g[:, u, 4, :], g[:, u, 1, :], g[:, u, 3, :], ALU.mult))
            for n in range(2):
                for t in range(TP):
                    i = dve.tensor_scalar(self.one[:, u, n, t, :], sh.iota_tok[:, 0:E], self.idxf[:, u, t, n:n + 1],
                                          g[:, u, 3 + n, t:t + 1], ALU.is_equal, ALU.mult)
            ch.link(dve, i)
            dve.tensor_tensor(self.gate[:, u, :, :], self.one[:, u, 0, :, :], self.one[:, u, 1, :, :],
                              ALU.add).then_inc(self.gate_done, 1)
            ch.end()

        def hidden(b, u, k):
            t, q = divmod(k, E // 2)
            dve.wait_ge(self.silu_done, 8 * b + k + 1)
            if k == 0:
                dve.wait_ge(self.gate_done, b + 1)
                need(dve, self.tr_done, self.NG * (b - 1))
            for e in range(2):
                i = dve.scalar_tensor_tensor(
                    out=self.hid[:, u, t, (2 * q + e) * M1:(2 * q + e + 1) * M1],
                    in0=self.silu[:, k % 2, e * M1:(e + 1) * M1], scalar=self.gate[:, u, t, 2 * q + e:2 * q + e + 1],
                    in1=self.pu[k % 2][:, e * M1:(e + 1) * M1], op0=ALU.mult, op1=ALU.mult)
            i.then_inc(self.hid_done, 1)

        def hlo(b, j):
            dve.wait_ge(self.hhi_done, self.NG * b + j + 1)
            n = T * (min(2 * j + 2, NCH) - 2 * j)
            c = slice(2 * j, 2 * j + n // T)
            dve.tensor_tensor(self.hlo[:, c, :].rearrange("p c t -> p (c t)"), self.pt[j % 2][:, 0:n],
                              self.hhi[:, c, :].rearrange("p c t -> p (c t)").bitcast(F32),
                              ALU.subtract).then_inc(self.hlo_done, 1)

        def update(b):
            dve.wait_ge(self.ytr_done, b + 1)
            x = X[:, bass.ds(TP * (b - self.o), TP), :]
            dve.tensor_tensor(x, x, self.py[:, T:2 * T].rearrange("p (t c) -> p t c", t=TP),
                              ALU.add).then_inc(sh.x_done, 1)

        def step(s, u):
            for k in range(8):
                if self.has(s):
                    hidden(s, u, k)
                if 1 <= k <= self.NG and self.has(s - 1):
                    hlo(s - 1, k - 1)
                if k == 1 and self.has(s - 2):
                    update(s - 2)
                if k == 3 and self.has(s + 1):
                    xlo(s + 1, 1 - u)
                if k == 4:
                    self.moments_next(dve, s - 2, u)
                if k == 6 and self.has(s + 1):
                    choose(s + 1, 1 - u)
            if self.has(s + 1):
                weigh(s + 1, 1 - u)

        def pre():
            self.w.split.vector_once(dve)
            xlo(self.o, 0)
            choose(self.o, 0)
            weigh(self.o, 0)

        self.steps(dve, step, pre)

    def gpsimd(self, pool):
        sh = self.sh

        def norm(b, u):
            self.norm.gpsimd(pool, b, u, lambda: apart(pool, self.xT_ready, b - 1, sh.passed))

        def gate_exp(b, u):
            apart(pool, self.gap_done, b + 1, sh.passed)
            pool.tensor_tensor(self.g[:, u, 1, :], sh.euler[:, :], self.g[:, u, 0, :], ALU.pow).then_inc(self.gexp_done, 1)

        def step(s, u):
            if self.has(s + 2):
                norm(s + 2, u)
            self.scale_next(pool, s - 2, u)
            if self.has(s + 1):
                gate_exp(s + 1, 1 - u)

        def pre():
            norm(self.o, 0)
            norm(self.o + 1, 1)
            gate_exp(self.o, 0)

        self.steps(pool, step, pre)


    def sync(self, sp):
        self.w.split.sync_once(sp)


class Top2Weights:
    def __init__(self, sh, mem):
        self.g_hi, self.g_lo = (mem.take(f"t2_g_{x}", [P, HID], F32R) for x in ("hi", "lo"))
        self.u_hi, self.u_lo = (mem.take(f"t2_u_{x}", [P, HID], F32R) for x in ("hi", "lo"))
        self.d_hi, self.d_lo = (mem.take(f"t2_d_{x}", [P, NCH, C], F32R) for x in ("hi", "lo"))
        self.gate_hi, self.gate_lo = (mem.take(f"t2_gate_{x}", [P, E], F32R) for x in ("hi", "lo"))
        self.parts = [(self.g_hi[:, :], self.g_lo[:, :], "t2_wg"), (self.u_hi[:, :], self.u_lo[:, :], "t2_wu"),
                      (self.d_hi[:, :, :].rearrange("p a b -> p (a b)"),
                       self.d_lo[:, :, :].rearrange("p a b -> p (a b)"), "t2_wd"),
                      (self.gate_hi[:, :], self.gate_lo[:, :], "t2_gate")]

    def ready(self, pe):
        self.split.ready(pe)


class Choice(Layer):

    GB = 4
    NGRP = B // GB
    GS = GB * CAP
    BH = B // 2

    def __init__(self, sh, tag, w, mem):
        self.sh, self.w = sh, w
        self.norm = Normed(sh, tag, mem)
        f = lambda n, s, d=F32: mem.take(f"{tag}_{n}", s, d)
        self.xT = f("xT", [P, 2, T])
        self.slot_token = f("slot_token", [P, B, EP])
        self.slot_weight = f("slot_weight", [P, B, EP])
        self.xhi = f("xhi", [P, 2, TP, C], F32R)
        self.xlo = f("xlo", [P, 2, TP, C], F32R)
        self.token_row = f("token_row", [P, 2, SLOTS])
        self.pick = f("pick", [P, TP, SLOTS], F32R)
        self.spread = f("spread", [P, 2, EP, T], F32R)
        self.yw = f("yw", [P, 2, EP * C])
        self.yhi = f("yhi", [P, 2, EP * C], F32R)
        self.ylo = f("ylo", [P, 2, EP * C], F32R)
        self.hhi = f("hhi", [P, 2, HC, self.GS], F32R)
        self.hlo = f("hlo", [P, 2, HC, self.GS], F32R)
        self.h = f("h", [P, 2, 2 * self.GS])
        self.big = mem.at
        self.xin_hi = f("xin_hi", [P, 2, self.GB, SLOTS], F32R)
        self.xin_lo = f("xin_lo", [P, 2, self.GB, SLOTS], F32R)
        at = mem.at
        self.yT = f("yT", [P, 2, self.GB, SLOTS])
        end = mem.at
        mem.at = at
        g = lambda n, s, d=F32: mem.take(f"{tag}_c_{n}", s, d)
        self.max = g("max", [P, NT])
        self.sum = g("sum", [P, NT])
        self.prob = g("prob", [P, TP, B, E])
        self.ranked = g("ranked", [P, 2, 2, T])
        self.best = g("best", [P, 2, CAP])
        self.best_at = g("best_at", [P, 2, CAP], U32)
        self.best_atf = g("best_atf", [P, 2, CAP])
        self.twice = g("twice", [P, 2, 2, 2, CAP])
        mem.at = max(end, mem.at)
        bk = sh.banks
        self.ph, self.py, self.pghi, self.pglo = bk[0:2], (bk[2], bk[7]), bk[3], bk[4]
        self.pback, self.psc, self.pxt = bk[5], bk[6], bk[7]
        self.pfirst = bk[0:2]
        s = lambda n: sh.sem(f"{tag}_{n}")
        self.xT_ready, self.xT_done, self.scored = s("xT_ready"), s("xT_done"), s("scored")
        self.soft, self.exp_done, self.prob_done = s("softmax_steps"), s("exp_done"), s("prob_done")
        self.probT_ready, self.rank_steps, self.twice_done = s("probT_ready"), s("rank_steps"), s("twice_done")
        self.slots_ready, self.slots_done = s("slots_ready"), s("slots_done")
        self.tokens_stored = s("tokens_stored")
        self.row_in = [s("token_row_in0"), s("token_row_in1")]
        self.pick_done, self.pick_used = s("pick_done"), s("pick_used")
        self.xa_done, self.xa_centred, self.xhi_done, self.xlo_done = s("xa_done"), s("xa_centred"), s("xhi_done"), s("xlo_done")
        self.gathered, self.xin_done = s("gathered"), s("xin_done")
        self.w1_done, self.gelu_done, self.hhi_done, self.hlo_done = s("w1_done"), s("gelu_done"), s("hhi_done"), s("hlo_done")
        self.w2_done, self.yev_done, self.ytr_done = s("w2_done"), s("yev_done"), s("ytr_done")
        self.yw_done, self.yhi_done, self.ylo_done, self.spread_done = s("yw_done"), s("yhi_done"), s("ylo_done"), s("spread_done")
        self.scattered = s("scattered")
        self.token_dram = sh.nc.dram_tensor(f"{tag}_tokens", [B, SLOTS], F32).ap()

    def groups(self, eng, step):
        pipeline(eng, step, 0, self.NGRP + 1, 2, self.NGRP - 3, self.o // self.GB)

    def has_group(self, g):
        return not isinstance(g, int) or inside(g - self.o // self.GB, self.NGRP)

    def back(self, g, e):
        return self.GB * (g - 1) + (e - 1) // 2

    def late(self, g, e):
        return self.GB * (g - 1) + (e - 3) // 2

    def tensor(self, pe):
        sh, w, ident, GS = self.sh, self.w, self.sh.ident, self.GS

        def turn_first(b, u):
            pe.wait_ge(self.norm.done, b + 1)
            need(pe, self.xT_done, b - 1)
            for t in range(TP):
                i = pe.transpose(self.pfirst[u][:, t * P:(t + 1) * P], self.norm.xn[:, u, t, :], ident[:, :])
            i.then_inc(self.xT_ready, 1)

        def score(b, u):
            if self.has(b + 1):
                turn_first(b + 1, 1 - u)
            pe.wait_ge(self.xT_done, b + 1)
            for t in range(TP):
                o = self.psc[:, bass.ds(t * B * E + (b - self.o) * E, E)]
                i = pe.matmul(o, self.xT[:, u, t * P:(t + 1) * P], w.gate[:, :], start=True, stop=True)
            i.then_inc(self.scored, 1)

        def turn_choice():
            pe.wait_ge(self.prob_done, self.run + 1)
            for h in range(2):
                for t in range(TP):
                    src = self.prob[:, t, h * self.BH:(h + 1) * self.BH, :].rearrange("p b e -> p (b e)")
                    pe.transpose(self.pback[:, h * T + t * P:h * T + (t + 1) * P], src, ident[:, :]).then_inc(self.probT_ready, 1)
            for h in range(2):
                pe.wait_ge(self.twice_done, 2 * self.run + h + 1)
                for n in range(2):
                    src = self.twice[:, h, n, :, :].rearrange("p a j -> p (a j)")
                    i = pe.transpose(self.pxt[:, h * T + n * P:h * T + (n + 1) * P], src, ident[:, :])
                i.then_inc(self.slots_ready, 1)

        def gather(q, uq, gp, t):
            pe.wait_ge(self.pick_done, TP * q + t + 1)
            if t == 0:
                pe.wait_ge(self.xlo_done, q + 1)
                need(pe, self.xin_done, q)
            pe.matmul(self.pghi[:, :], self.xhi[:, uq, t, :], self.pick[:, t, :], start=(t == 0), stop=(t == TP - 1))
            i = pe.matmul(self.pglo[:, :], self.xlo[:, uq, t, :], self.pick[:, t, :], start=(t == 0), stop=(t == TP - 1))
            i.then_inc(self.pick_used, 1)

        def up(g, gp, e):
            n = E * g + e
            if e == 0:
                pe.wait_ge(self.xin_done, self.GB * (g + 1))
            hi = self.xin_hi[:, gp, :, e * CAP:(e + 1) * CAP]
            lo = self.xin_lo[:, gp, :, e * CAP:(e + 1) * CAP]
            for c in range(HC):
                if c % 2 == 0:
                    need(pe, self.gelu_done, 2 * n + c // 2 - 1)
                o = self.ph[c // 2][:, (c % 2) * GS:(c % 2 + 1) * GS]
                k = slice(c * P, (c + 1) * P)
                pe.matmul(o, w.w1_hi[:, e, k], hi, start=True, stop=False)
                pe.matmul(o, w.w1_hi[:, e, k], lo, start=False, stop=False)
                i = pe.matmul(o, w.w1_lo[:, e, k], hi, start=False, stop=True)
                if c % 2:
                    i.then_inc(self.w1_done, 1)

        def down(g, e):
            n = E * g + e
            ue = e % 2
            pe.wait_ge(self.hlo_done, 2 * n + 2)
            need(pe, self.yev_done, n - 1)
            o = self.py[ue][:, 0:GS]
            for c in range(HC):
                pe.matmul(o, w.w2_hi[:, e, c, :], self.hhi[:, ue, c, :], start=(c == 0), stop=False)
                pe.matmul(o, w.w2_hi[:, e, c, :], self.hlo[:, ue, c, :], start=False, stop=False)
                i = pe.matmul(o, w.w2_lo[:, e, c, :], self.hhi[:, ue, c, :], start=False, stop=(c == HC - 1))
            i.then_inc(self.w2_done, 1)

        def turn(b, gp, bb):
            if bb == 0:
                pe.wait_ge(self.yev_done, 2 * (b + self.GB))
            need(pe, self.yw_done, b)
            for n in range(EP):
                i = pe.transpose(self.pback[:, n * P:(n + 1) * P], self.yT[:, gp, bb, n * P:(n + 1) * P], ident[:, :])
            i.then_inc(self.ytr_done, 1)

        def scatter(b, ub):
            pe.wait_ge(self.ylo_done, b + 1)
            pe.wait_ge(self.spread_done, b + 1)
            need(pe, sh.x_done, self.x0 + b)
            for t in range(TP):
                o = self.psc[:, t * C:(t + 1) * C]
                for n in range(EP):
                    sp = self.spread[:, ub, n, t * P:(t + 1) * P]
                    pe.matmul(o, sp, self.yhi[:, ub, n * C:(n + 1) * C], start=(n == 0), stop=False)
                    i = pe.matmul(o, sp, self.ylo[:, ub, n * C:(n + 1) * C], start=False, stop=(n == EP - 1))
            i.then_inc(self.scattered, 1)

        def step(g, gp):
            for e in range(E):
                if self.has_group(g):
                    up(g, gp, e)
                if e == 0 and self.has_group(g - 1):
                    down(g - 1, E - 1)
                if e and self.has_group(g):
                    down(g, e - 1)
                if self.has_group(g + 1):
                    gather(self.GB * (g + 1) + e // 2, (e // 2) % 2, 1 - gp, e % 2)
                if e % 2:
                    if self.has(self.back(g, e)):
                        turn(self.back(g, e), 1 - gp, (e - 1) // 2)
                    if self.has(self.late(g, e)):
                        scatter(self.late(g, e), ((e - 3) // 2) % 2)

        sh.start(pe, self.layer * B)
        pe.wait_ge(sh.consts, sh.N_CONSTS)
        pe.wait_ge(w.gate_in, 16)
        turn_first(self.o, 0)
        pipeline(pe, score, 0, B - 1, 2, B - 3, self.o)
        turn_choice()
        w.ready(pe)
        for q in range(self.GB):
            for t in range(TP):
                gather(self.o + q, q % 2, 0, t)
        self.groups(pe, step)

    def scalar(self, act):
        GS = self.GS

        def xT(b, u):
            act.wait_ge(self.xT_ready, b + 1)
            need(act, self.scored, b - 1)
            act.activation(self.xT[:, u, :], self.pfirst[u][:, 0:T], ACT.Copy).then_inc(self.xT_done, 1)

        def gathered(q, gp, bb):
            act.wait_ge(self.pick_used, TP * (q + 1))
            if bb == 0:
                need(act, self.w1_done, 4 * q - 16)
            act.activation(self.xin_hi[:, gp, bb, :], self.pghi[:, :], ACT.Copy)
            act.activation(self.xin_lo[:, gp, bb, :], self.pglo[:, :], ACT.Copy).then_inc(self.xin_done, 1)

        def gelu(g, e):
            n = E * g + e
            for c in range(2):
                act.wait_ge(self.w1_done, 2 * n + c + 1)
                need(act, self.hlo_done, 2 * n + c - 1)
                act.activation(self.h[:, c, :], self.ph[c][:, :], ACT.Gelu).then_inc(self.gelu_done, 1)

        def hhi(g, e):
            n = E * g + e
            need(act, self.w2_done, n - 1)
            for c in range(2):
                act.wait_ge(self.gelu_done, 2 * n + c + 1)
                o = self.hhi[:, e % 2, 2 * c:2 * c + 2, :].rearrange("p c s -> p (c s)")
                act.activation(o, self.h[:, c, :], ACT.Copy).then_inc(self.hhi_done, 1)

        def yev(g, gp, e):
            n = E * g + e
            act.wait_ge(self.w2_done, n + 1)
            if e == 0:
                need(act, self.ytr_done, self.GB * (g - 1))
            src = self.py[e % 2][:, 0:GS].rearrange("p (b j) -> p b j", b=self.GB)
            act.activation(self.yT[:, gp, :, e * CAP:(e + 1) * CAP], src, ACT.Copy).then_inc(self.yev_done, 1)

        def step(g, gp):
            for e in range(E):
                if self.has_group(g):
                    gelu(g, e)
                if e == 0 and self.has_group(g - 1):
                    yev(g - 1, 1 - gp, E - 1)
                if e and self.has_group(g):
                    yev(g, gp, e - 1)
                if self.has_group(g):
                    hhi(g, e)
                if e % 2 and self.has_group(g + 1):
                    gathered(self.GB * (g + 1) + e // 2, 1 - gp, e // 2)

        self.sh.start(act, self.layer * B)
        pipeline(act, xT, 0, B - 1, 2, B - 3, self.o)
        act.wait_ge(self.soft, 4 * self.run + 2)
        flat = lambda t: t[:, :, :, :].rearrange("p t b e -> p (t b e)")
        act.activation(flat(self.prob), flat(self.prob), ACT.Exp).then_inc(self.exp_done, 1)
        self.w.split.scalar_once(act)
        for q in range(self.GB):
            gathered(self.o + q, 0, q)
        self.groups(act, step)

    def vector(self, dve):
        sh, X = self.sh, self.sh.X

        def softmax():
            by = lambda t: t.rearrange("p (n e) -> p n e", e=E)
            prob = by(self.prob[:, :, :, :].rearrange("p t b e -> p (t b e)"))
            wide = lambda t: t[:, :].unsqueeze(2).to_broadcast([P, NT, E])
            dve.wait_ge(self.scored, self.o + B)
            dve.tensor_reduce(self.max[:, :], by(self.psc[:, :]), AX.X, ALU.max).then_inc(self.soft, 1)
            dve.wait_ge(self.soft, 4 * self.run + 1)
            dve.tensor_tensor(prob, by(self.psc[:, :]), wide(self.max), ALU.subtract).then_inc(self.soft, 1)
            dve.wait_ge(self.exp_done, self.run + 1)
            dve.tensor_reduce(self.sum[:, :], prob, AX.X, ALU.add).then_inc(self.soft, 1)
            dve.wait_ge(self.soft, 4 * self.run + 3)
            dve.reciprocal(self.max[:, :], self.sum[:, :]).then_inc(self.soft, 1)
            dve.wait_ge(self.soft, 4 * self.run + 4)
            dve.tensor_tensor(prob, prob, wide(self.max), ALU.mult).then_inc(self.prob_done, 1)

        def rank(h):
            rounds = CAP // 8
            k = [(2 + 2 * rounds) * (2 * self.run + h)]

            def link(ins):
                k[0] += 1
                ins.then_inc(self.rank_steps, 1)
                dve.wait_ge(self.rank_steps, k[0])

            dve.wait_ge(self.probT_ready, 2 * TP * (self.run + 1))
            link(dve.tensor_copy(self.ranked[:, h, 0, :], self.pback[:, h * T:(h + 1) * T]))
            for r in range(rounds):
                now, later = self.ranked[:, h, r % 2, :], self.ranked[:, h, 1 - r % 2, :]
                eight = slice(8 * r, 8 * r + 8)
                link(dve.max(self.best[:, h, eight], now))
                i = dve.max_index(self.best_at[:, h, eight], self.best[:, h, eight], now)
                if r < rounds - 1:
                    i = dve.match_replace(later, self.best[:, h, eight], now, -1.0)
                link(i)
            link(dve.tensor_copy(self.best_atf[:, h, :], self.best_at[:, h, :]))
            wide = lambda t: t[:, h, :].unsqueeze(1).to_broadcast([P, 2, CAP])
            dve.tensor_copy(self.twice[:, h, 0, :, :], wide(self.best_atf))
            dve.tensor_scalar(self.twice[:, h, 1, :, :], wide(self.best), 0.5, None, ALU.mult).then_inc(self.twice_done, 1)

        def slots(h):
            dve.wait_ge(self.slots_ready, 2 * (self.run + 1))
            for n, dst in enumerate((self.slot_token, self.slot_weight)):
                src = self.pxt[:, h * T + n * P:h * T + (n + 1) * P].rearrange("p (b n a) -> p b n a", n=EP, a=2)
                for a in range(2):
                    i = dve.tensor_copy(dst[a * CAP:(a + 1) * CAP, h * self.BH:(h + 1) * self.BH, :],
                                        src[a * CAP:(a + 1) * CAP, :, :, a])
            i.then_inc(self.slots_done, 1)

        def xlo(q, uq):
            dve.wait_ge(self.xhi_done, q + 1)
            dve.tensor_tensor(self.xlo[:, uq, :, :], self.norm.xn[:, uq, :, :], self.xhi[:, uq, :, :].bitcast(F32),
                              ALU.subtract).then_inc(self.xlo_done, 1)

        def pick(q, uq, t):
            if t == 0:
                dve.wait_ge(self.row_in[uq], 8 * (q - uq) + 16)
            need(dve, self.pick_used, TP * q + t - 1)
            dve.tensor_scalar(self.pick[:, t, :], self.token_row[:, uq, :], sh.iota_part[:, t:t + 1], None,
                              ALU.is_equal).then_inc(self.pick_done, 1)

        def hlo(g, e):
            n = E * g + e
            for c in range(2):
                dve.wait_ge(self.hhi_done, 2 * n + c + 1)
                k = slice(2 * c, 2 * c + 2)
                flat = lambda t: t[:, e % 2, k, :].rearrange("p c s -> p (c s)")
                dve.tensor_tensor(flat(self.hlo), self.h[:, c, :], flat(self.hhi).bitcast(F32),
                                  ALU.subtract).then_inc(self.hlo_done, 1)

        def weigh(b, ub):
            dve.wait_ge(self.ytr_done, b + 1)
            need(dve, self.ylo_done, b - 1)
            wide = self.slot_weight[:, bass.ds(b - self.o, 1), :].rearrange("p a n -> p (a n)").unsqueeze(2).to_broadcast([P, EP, C])
            by = lambda t: t.rearrange("p (n c) -> p n c", c=C)
            dve.tensor_tensor(by(self.yw[:, ub, :]), by(self.pback[:, :]), wide, ALU.mult).then_inc(self.yw_done, 1)

        def ylo(b, ub):
            dve.wait_ge(self.yhi_done, b + 1)
            dve.tensor_tensor(self.ylo[:, ub, :], self.yw[:, ub, :], self.yhi[:, ub, :].bitcast(F32),
                              ALU.subtract).then_inc(self.ylo_done, 1)

        def spread(b, ub):
            need(dve, self.scattered, b - 1)
            for n in range(EP):
                at = self.slot_token[:, bass.ds(b - self.o, 1), n]
                i = dve.tensor_scalar(self.spread[:, ub, n, :], sh.iota_tok[:, :], at, None, ALU.is_equal)
            i.then_inc(self.spread_done, 1)

        def update(b):
            dve.wait_ge(self.scattered, b + 1)
            x = X[:, bass.ds(TP * (b - self.o), TP), :]
            dve.tensor_tensor(x, x, self.psc[:, 0:TP * C].rearrange("p (t c) -> p t c", t=TP),
                              ALU.add).then_inc(sh.x_done, 1)

        def step(g, gp):
            for e in range(E):
                q = self.GB * (g + 1) + e // 2
                if self.has_group(g + 1):
                    if e % 2 == 0:
                        xlo(q, (e // 2) % 2)
                    pick(q, (e // 2) % 2, e % 2)
                if e % 2 == 0:
                    b = self.late(g, e + 1)
                    if self.has(b):
                        ub = ((e - 2) // 2) % 2
                        ylo(b, ub)
                        spread(b, ub)
                    self.moments_next(dve, self.GB * (g - 1) + (e - 4) // 2, ((e - 4) // 2) % 2)
                if self.has_group(g):
                    hlo(g, e)
                if e % 2:
                    b = self.back(g, e)
                    if self.has(b):
                        weigh(b, ((e - 1) // 2) % 2)
                    if self.has(self.late(g, e)):
                        update(self.late(g, e))

        sh.start(dve, self.layer * B)
        dve.wait_ge(sh.consts, sh.N_CONSTS)
        pipeline(dve, lambda b, u: self.norm.vector(dve, b, u, lambda: apart(dve, self.xT_ready, b - 1, sh.passed)), 0, B - 1, 2, B - 3, self.o)
        softmax()
        self.w.split.vector_once(dve)
        for h in range(2):
            rank(h)
        for h in range(2):
            slots(h)
        for q in range(self.GB):
            xlo(self.o + q, q % 2)
            for t in range(TP):
                pick(self.o + q, q % 2, t)
        self.groups(dve, step)

    def gpsimd(self, pool):
        sh = self.sh

        def again(q, uq):
            apart(pool, self.xlo_done, q - 1, sh.passed)
            self.norm.spread(pool, q, uq, self.xa_centred, self.xa_done)
            apart(pool, self.pick_used, TP * (q - 1), sh.passed)
            apart(pool, self.xa_done, q + 1, sh.passed)
            pool.tensor_scalar(self.xhi[:, uq, :, :], self.norm.xn[:, uq, :, :], 1.0, 0.0, ALU.mult, ALU.add).then_inc(self.xhi_done, 1)

        def yhi(b, ub):
            apart(pool, self.scattered, b - 1, sh.passed)
            apart(pool, self.yw_done, b + 1, sh.passed)
            pool.tensor_scalar(self.yhi[:, ub, :], self.yw[:, ub, :], 1.0, 0.0, ALU.mult, ALU.add).then_inc(self.yhi_done, 1)

        def step(g, gp):
            for e in range(1, E, 2):
                q = self.GB * (g + 1) + e // 2 + 1
                if self.has(q) and self.has_group(g + 1):
                    again(q, (e // 2 + 1) % 2)
                b = self.back(g, e)
                if self.has(b):
                    yhi(b, ((e - 1) // 2) % 2)
                self.scale_next(pool, self.GB * (g - 1) + (e - 5) // 2, ((e - 5) // 2) % 2)

        sh.start(pool, self.layer * B)
        pool.wait_ge(self.xT_ready, self.o + B)
        for q in range(self.GB + 1):
            again(self.o + q, q % 2)
        self.groups(pool, step)

    def sync(self, sp):
        for h in range(2):
            sp.wait_ge(self.twice_done, 2 * self.run + h + 1)
            dst = self.token_dram[h * self.BH:(h + 1) * self.BH, :].rearrange("b (e j) -> (b e) j", e=E)
            sp.dma_start(dst, self.best_atf[:, h, :]).then_inc(self.tokens_stored, 16)
        sp.wait_ge(self.tokens_stored, 32 * (self.run + 1))

        def row(q, uq):
            need(sp, self.pick_done, TP * (q - 1))
            sp.dma_start(self.token_row[:, uq, :], self.token_dram[bass.ds(q - self.o, 1), :].to_broadcast([P, SLOTS])).then_inc(self.row_in[uq], 16)

        pipeline(sp, row, 0, B - 1, 2, B - 3, self.o)


class ChoiceWeights:
    def __init__(self, sh, mem):
        self.sh = sh
        self.w1_hi, self.w1_lo = (mem.take(f"ec_w1_{x}", [P, E, H0], F32R) for x in ("hi", "lo"))
        self.w2_hi, self.w2_lo = (mem.take(f"ec_w2_{x}", [P, E, HC, C], F32R) for x in ("hi", "lo"))
        self.gate = mem.take("ec_gate", [P, E])
        self.gate_in = sh.sem("ec_gate_in")
        self.split = None
        one = lambda t: t[:, :, :].rearrange("p e h -> p (e h)")
        two = lambda t: t[:, :, :, :].rearrange("p e k c -> p (e k c)")
        self.parts = [(one(self.w1_hi), one(self.w1_lo), "ec_w1"), (two(self.w2_hi), two(self.w2_lo), "ec_w2")]

    def sync(self, sp):
        sp.dma_start(self.gate[:, :], self.sh.args["ec_gate"]).then_inc(self.gate_in, 16)
        self.split.sync(sp)

    def ready(self, pe):
        self.split.ready(pe)


class Rwkv(Layer):

    COLS = ("decay", "mix_k", "mix_v", "mix_r", "ln_g", "ln_b")

    def __init__(self, sh, tag, mem):
        self.sh = sh
        self.norm = Normed(sh, tag, mem)
        f = lambda n, s, d=F32: mem.take(f"{tag}_{n}", s, d)
        self.cols = f("cols", [P, len(self.COLS)])
        self.rest = f("one_minus_mix", [P, 3])
        self.td = f("decay_exp", [P, 1])
        self.w = f("w", [P, 4, C])
        self.now = f("w_now", [P, 3, C])
        self.before = f("w_before", [P, 3, C])
        self.x1 = f("x1", [P, 2, T + 1])
        self.ek, self.er, self.er1, self.ekv, self.num, self.den, self.under, self.over, self.z = (
            f(n, [P, 2, T]) for n in ("ek", "er", "er1", "ekv", "num", "den", "under", "over", "z"))
        bk = sh.banks
        self.px, self.pkv, self.pr, self.po = bk[0], bk[1:3], bk[3:5], bk[5:7]
        s = lambda n: sh.sem(f"{tag}_{n}")
        self.w_in, self.setup = s("w_in"), s("setup_steps")
        self.xT_ready, self.x1_done, self.kv_done, self.r_done = s("xT_ready"), s("x1_done"), s("kv_done"), s("r_done")
        self.ek_done, self.er_done, self.er1_done = s("ek_done"), s("er_done"), s("er1_done")
        self.ekv_done, self.scans_done, self.under_done, self.over_done = s("ekv_done"), s("scans_done"), s("under_done"), s("over_done")
        self.z_done, self.out_done = s("z_done"), s("out_done")

    SETUP = 1 + 2 + 6

    def steps(self, eng, step):
        pipeline(eng, step, 0, B, 2, B - 3)

    def sync(self, sp):
        self.sh.start(sp, self.x0)
        sp.dma_start(self.cols[:, :], self.sh.args["rk_cols"]).then_inc(self.w_in, 16)
        sp.dma_start(self.w[:, :, :].rearrange("p a b -> p (a b)"), self.sh.args["rk_w"]).then_inc(self.w_in, 16)

    def tensor(self, pe):
        sh, ident = self.sh, self.sh.ident

        def turn(b, u):
            pe.wait_ge(self.norm.done, b + 1)
            need(pe, self.x1_done, b)
            for t in range(TP):
                i = pe.transpose(self.px[:, t * P:(t + 1) * P], self.norm.xn[:, u, t, :], ident[:, :])
            i.then_inc(self.xT_ready, 1)

        def project(b, u):
            pe.wait_ge(self.x1_done, b + 1)
            need(pe, self.ekv_done, b - 1)
            need(pe, self.er_done, b - 1)
            for n, (o, done) in enumerate(((self.pkv[u][:, 0:T], None), (self.pkv[u][:, T:2 * T], self.kv_done),
                                           (self.pr[u][:, 0:T], self.r_done))):
                pe.matmul(o, self.now[:, n, :], self.x1[:, u, 1:T + 1], start=True, stop=False)
                i = pe.matmul(o, self.before[:, n, :], self.x1[:, u, 0:T], start=False, stop=True)
                if done is not None:
                    i.then_inc(done, 1)

        def out(b, u):
            pe.wait_ge(self.z_done, b + 1)
            need(pe, sh.x_done, self.x0 + b - 1)
            for t in range(TP):
                i = pe.matmul(self.po[u][:, t * C:(t + 1) * C], self.z[:, u, t * P:(t + 1) * P], self.w[:, 3, :],
                              start=True, stop=True)
            i.then_inc(self.out_done, 1)

        def step(s, u):
            if inside(s + 1):
                turn(s + 1, 1 - u)
            if inside(s):
                project(s, u)
            if inside(s - 1):
                out(s - 1, 1 - u)

        sh.start(pe, self.x0)
        pe.wait_ge(sh.consts, sh.N_CONSTS)
        pe.wait_ge(self.setup, self.SETUP)
        turn(0, 0)
        self.steps(pe, step)

    def scalar(self, act):
        def x1(b, u):
            act.wait_ge(self.xT_ready, b + 1)
            need(act, self.r_done, b - 1)
            act.activation(self.x1[:, u, 1:T + 1], self.px[:, 0:T], ACT.Identity, scale=self.cols[:, 4:5],
                           bias=self.cols[:, 5:6]).then_inc(self.x1_done, 1)

        def exps(b, u):
            act.wait_ge(self.kv_done, b + 1)
            need(act, self.scans_done, b - 1)
            act.activation(self.ek[:, u, :], self.pkv[u][:, 0:T], ACT.Exp).then_inc(self.ek_done, 1)
            act.wait_ge(self.r_done, b + 1)
            need(act, self.er1_done, b - 1)
            act.activation(self.er[:, u, :], self.pr[u][:, 0:T], ACT.Exp, scale=-1.0).then_inc(self.er_done, 1)

        def step(s, u):
            if inside(s + 1):
                x1(s + 1, 1 - u)
            if inside(s):
                exps(s, u)

        self.sh.start(act, self.x0)
        act.wait_ge(self.w_in, 32)
        act.activation(self.td[:, :], self.cols[:, 0:1], ACT.Exp).then_inc(self.setup, 1)
        act.wait_ge(self.setup, self.SETUP)
        x1(0, 0)
        self.steps(act, step)

    def vector(self, dve):
        sh, X = self.sh, self.sh.X

        def mix(b, u):
            td = self.td[:, 0:1].to_broadcast([P, T])
            dve.wait_ge(self.ek_done, b + 1)
            dve.tensor_tensor(self.ekv[:, u, :], self.pkv[u][:, T:2 * T], self.ek[:, u, :], ALU.mult).then_inc(self.ekv_done, 1)
            dve.tensor_tensor_scan(self.den[:, u, :], td, self.ek[:, u, :], 0.0, ALU.mult, ALU.add)
            dve.wait_ge(self.ekv_done, b + 1)
            dve.tensor_tensor_scan(self.num[:, u, :], td, self.ekv[:, u, :], 0.0, ALU.mult, ALU.add).then_inc(self.scans_done, 1)
            dve.wait_ge(self.scans_done, b + 1)
            dve.wait_ge(self.er1_done, b + 1)
            dve.scalar_tensor_tensor(out=self.under[:, u, :], in0=self.den[:, u, :], scalar=1e-8, in1=self.er1[:, u, :],
                                     op0=ALU.add, op1=ALU.mult).then_inc(self.under_done, 1)
            dve.wait_ge(self.under_done, b + 1)
            dve.reciprocal(self.over[:, u, :], self.under[:, u, :]).then_inc(self.over_done, 1)
            dve.wait_ge(self.over_done, b + 1)
            need(dve, self.out_done, b - 1)
            dve.tensor_tensor(self.z[:, u, :], self.num[:, u, :], self.over[:, u, :], ALU.mult).then_inc(self.z_done, 1)

        def update(b, u):
            dve.wait_ge(self.out_done, b + 1)
            x = X[:, bass.ds(TP * b, TP), :]
            dve.tensor_tensor(x, x, self.po[u][:, 0:TP * C].rearrange("p (t c) -> p t c", t=TP), ALU.add).then_inc(sh.x_done, 1)

        def step(s, u):
            self.moments_next(dve, s - 2, u)
            if inside(s):
                mix(s, u)
            if inside(s - 1):
                update(s - 1, 1 - u)

        sh.start(dve, self.x0)
        dve.wait_ge(self.w_in, 32)
        for u in range(2):
            i = dve.memset(self.x1[:, u, 0:1], 0.0)
        i.then_inc(self.setup, 1)
        dve.tensor_scalar(self.rest[:, :], self.cols[:, 1:4], -1.0, 1.0, ALU.mult, ALU.add).then_inc(self.setup, 1)
        dve.wait_ge(self.setup, 3)
        for n in range(3):
            dve.tensor_scalar(self.now[:, n, :], self.w[:, n, :], self.cols[:, 1 + n:2 + n], None, ALU.mult).then_inc(self.setup, 1)
            dve.tensor_scalar(self.before[:, n, :], self.w[:, n, :], self.rest[:, n:n + 1], None, ALU.mult).then_inc(self.setup, 1)
        self.steps(dve, step)
        self.moments_next(dve, B - 1, 1)

    def gpsimd(self, pool):
        def er1(b, u):
            apart(pool, self.under_done, b - 1, self.sh.passed)
            apart(pool, self.er_done, b + 1, self.sh.passed)
            pool.tensor_scalar(self.er1[:, u, :], self.er[:, u, :], 1.0, 1.0, ALU.mult, ALU.add).then_inc(self.er1_done, 1)

        def norm(b, u):
            self.norm.gpsimd(pool, b, u, lambda: apart(pool, self.xT_ready, b - 1, self.sh.passed))

        def step(s, u):
            if inside(s + 2):
                norm(s + 2, u)
            if inside(s):
                er1(s, u)
            self.scale_next(pool, s - 2, u)

        self.sh.start(pool, self.x0)
        norm(0, 0)
        norm(1, 1)
        self.steps(pool, step)
        self.scale_next(pool, B - 1, 1)


class Mlstm(Layer):

    TRI = T + P
    SERIES = 8

    def __init__(self, sh, tag, mem):
        self.sh = sh
        self.norm = Normed(sh, tag, mem)
        f = lambda n, s, d=F32: mem.take(f"{tag}_{n}", s, d)
        self.wq, self.wk, self.wd0, self.wd = f("wq", [P, C]), f("wk", [P, C]), f("wdown_in", [P, C]), f("wdown", [P, C])
        self.wvo = f("wvo", [P, 2 * C])
        self.wgate = f("wgate", [P, 2 * NH])
        self.bias = f("gate_bias", [P, 2 * NH])
        self.nw = f("norm_w", [P, 1])
        self.mask = f("mask", [P, T])
        self.ones = f("ones", [P, 1])
        self.xT = f("xT", [P, 2, T])
        self.aT = f("aT", [P, TP, B * NH])
        self.emT = f("emT", [P, TP, B * NH])
        at = mem.at
        g = lambda n, s, d=F32: mem.take(f"{tag}_g_{n}", s, d)
        self.raw = g("raw", [P, NT, 2 * NH])
        self.cap = g("capped", [P, NT, 2 * NH])
        self.g_ig, self.g_fg, self.g_abs, self.g_e, self.g_s, self.g_s2, self.g_acc, self.g_acc2, self.g_lf, self.g_neg = (
            g(n, [P, TP, B * NH]) for n in ("ig", "fg", "abs", "e", "s", "s2", "acc", "acc2", "lf", "neg"))
        self.r_cum, self.r_a, self.r_run, self.r_negrun, self.r_m, self.r_em = (
            g("row_" + n, [P, T]) for n in ("cum", "a", "run", "negrun", "m", "em"))
        end = mem.at
        mem.at = at
        self.run_row = f("run_row", [P, 2, NH, T])
        self.qs = f("q", [P, 2, T])
        self.ks = f("k", [P, 2, NH, T])
        self.vx = f("v", [P, 2, TP, NH, DH + 1])
        self.th = f("o_tanh", [P, 2, TP, C])
        self.logd = f("log_decay", [P, 2, NH, self.TRI])
        self.ct = f("weights", [P, 2, NH, self.TRI])
        self.av = f("av", [P, 2, TP * NH, DH + 1])
        self.n8 = f("n8", [P, 2, 6, TP * NH])
        self.hv, self.d, self.sq, self.hn, self.hg = (f(n, [P, 2, TP, C]) for n in ("hv", "d", "sq", "hn", "hg"))
        self.hT = f("hT", [P, 2, T])
        mem.at = max(end, mem.at)
        bk = sh.banks
        self.ps, self.pq, self.pvo, self.pav, self.pm = bk[0:4], bk[4], bk[5], bk[6], bk[7]
        s = lambda n: sh.sem(f"{tag}_{n}")
        self.w_in, self.setup = s("w_in"), s("setup_steps")
        self.xT_ready, self.xT_done, self.scored = s("xT_ready"), s("xT_done"), s("scored")
        self.gates, self.tanh_done, self.gexp_done = s("gate_steps"), s("tanh_done"), s("gexp_done")
        self.rows_ready, self.rows, self.em_done = s("rows_ready"), s("row_steps"), s("em_done")
        self.run_stored, self.cols_ready, self.cols_done = s("run_stored"), s("cols_ready"), s("cols_done")
        self.row_in = [s("run_row_in0"), s("run_row_in1")]
        self.xa_centred, self.xa_done, self.yT_ready, self.yT_done = s("xa_centred"), s("xa_done"), s("x2T_ready"), s("x2T_done")
        self.qk_ready, self.vo_ready, self.qk_done, self.vo_done = s("qk_ready"), s("vo_ready"), s("qk_done"), s("vo_done")
        self.s_done, self.logd_done, self.d_done, self.ct_done = s("s_done"), s("logd_done"), s("d_done"), s("ct_done")
        self.av_done, self.avc_done = s("av_done"), s("avc_done")
        self.head = Chain(s("head_steps"), 5)
        self.hsum, self.mean_done, self.mask_set = s("head_sum_done"), s("head_mean_done"), s("mask_set")
        self.cen_done, self.sq_done, self.var_done = s("cen_done"), s("sq_done"), s("var_done")
        self.rstd = Chain(s("head_rstd_steps"), 2)
        self.hn_done, self.hg_done, self.hT_ready, self.hT_done, self.out_done = (
            s("hn_done"), s("hg_done"), s("hT_ready"), s("hT_done"), s("out_done"))
        self.run_dram = sh.nc.dram_tensor(f"{tag}_run", [B, NH * T], F32).ap()

    def steps(self, eng, step):
        pipeline(eng, step, 0, B + 1, 4, B - 3)

    LOADS = ("ml_wq", "ml_wk", "ml_wvo", "ml_wdown", "ml_wgate", "ml_norm_w")

    def sync(self, sp):
        a = self.sh.args
        self.sh.start(sp, self.x0)
        for dst, n in zip((self.wq, self.wk, self.wvo, self.wd0, self.wgate, self.nw), self.LOADS):
            sp.dma_start(dst[:, :], a[n]).then_inc(self.w_in, 16)
        sp.dma_start(self.bias[:, :], a["ml_bias"].to_broadcast([P, 2 * NH])).then_inc(self.w_in, 16)
        sp.wait_ge(self.rows, 4)
        dst = self.run_dram.rearrange("b (h t) -> (b h) t", h=NH)
        sp.dma_start(dst, self.r_negrun[:, :]).then_inc(self.run_stored, 16)
        sp.wait_ge(self.run_stored, 16)
        sp.wait_ge(self.cols_done, 1)

        def row(b, u):
            need(sp, self.logd_done, b - 1)
            dst = self.run_row[:, u, :, :].rearrange("p h t -> p (h t)")
            sp.dma_start(dst, self.run_dram[bass.ds(b, 1), :].to_broadcast([P, NH * T])).then_inc(self.row_in[u], 16)

        pipeline(sp, row, 0, B - 1, 2, B - 3)

    def tensor(self, pe):
        sh, ident = self.sh, self.sh.ident

        def turn_first(b, u):
            pe.wait_ge(self.norm.done, b + 1)
            need(pe, self.xT_done, b - 1)
            for t in range(TP):
                i = pe.transpose(self.ps[u][:, t * P:(t + 1) * P], self.norm.xn[:, u, t, :], ident[:, :])
            i.then_inc(self.xT_ready, 1)

        def score(b, u):
            if inside(b + 1):
                turn_first(b + 1, 1 - u)
            pe.wait_ge(self.xT_done, b + 1)
            for t in range(TP):
                o = self.pq[:, bass.ds(t * B * 2 * NH + b * 2 * NH, 2 * NH)]
                i = pe.matmul(o, self.xT[:, u, t * P:(t + 1) * P], self.wgate[:, :], start=True, stop=True)
            i.then_inc(self.scored, 1)

        def turn_gates():
            pe.wait_ge(self.gates, self.GATE_STEPS)
            for n, src in enumerate((self.g_lf, self.g_ig)):
                for t in range(TP):
                    i = pe.transpose(self.pvo[:, (TP * n + t) * P:(TP * n + t + 1) * P], src[:, t, :], ident[:, :])
            i.then_inc(self.rows_ready, 1)
            pe.wait_ge(self.rows, 3)
            pe.wait_ge(self.em_done, 1)
            for n, src in enumerate((self.r_a, self.r_em)):
                for t in range(TP):
                    i = pe.transpose(self.pav[:, (TP * n + t) * P:(TP * n + t + 1) * P], src[:, t * P:(t + 1) * P], ident[:, :])
            i.then_inc(self.cols_ready, 1)

        def turn(b, u):
            pe.wait_ge(self.xa_done, b + 1)
            need(pe, sh.x_done, self.x0 + b - 3)
            for t in range(TP):
                i = pe.transpose(self.pm[:, t * P:(t + 1) * P], self.norm.xn[:, u, t, :], ident[:, :])
            i.then_inc(self.yT_ready, 1)

        def project_qk(b, u):
            pe.wait_ge(self.yT_done, b + 1)
            need(pe, self.qk_done, b)
            pe.matmul(self.pq[:, 0:T], self.wq[:, :], self.xT[:, u, :], start=True, stop=True)
            pe.matmul(self.pq[:, T:2 * T], self.wk[:, :], self.xT[:, u, :], start=True, stop=True).then_inc(self.qk_ready, 1)

        def project_vo(b, u, t):
            need(pe, self.vo_done, b)
            i = pe.matmul(self.pvo[:, t * 2 * C:(t + 1) * 2 * C], self.xT[:, u, t * P:(t + 1) * P], self.wvo[:, :],
                          start=True, stop=True)
            if t == TP - 1:
                i.then_inc(self.vo_ready, 1)

        def scores(b, u):
            pe.wait_ge(self.qk_done, b + 1)
            for h in range(NH):
                need(pe, self.ct_done, NH * (b - 1) + h + 1)
                pe.matmul(self.ps[h][:, 0:T], self.ks[:, u, h, 0:P], self.qs[:, u, :], start=True, stop=True)
                pe.matmul(self.ps[h][:, T:T + P], self.ks[:, u, h, P:T], self.qs[:, u, P:T], start=True,
                          stop=True).then_inc(self.s_done, 1)

        def attend(b, u, h):
            if h == 0:
                need(pe, self.avc_done, b)
                pe.wait_ge(self.vo_done, b + 1)
            pe.wait_ge(self.ct_done, NH * b + h + 1)
            o = [self.pav[:, (t * NH + h) * (DH + 1):(t * NH + h + 1) * (DH + 1)] for t in range(TP)]
            c = self.ct[:, u, h, :]
            pe.matmul(o[0], c[:, 0:P], self.vx[:, u, 0, h, :], start=True, stop=True)
            pe.matmul(o[1], c[:, P:T], self.vx[:, u, 0, h, :], start=True, stop=False)
            i = pe.matmul(o[1], c[:, T:T + P], self.vx[:, u, 1, h, :], start=False, stop=True)
            if h == NH - 1:
                i.then_inc(self.av_done, 1)

        def turn_back(b, u, newest):
            pe.wait_ge(self.hg_done, b + 1)
            need(pe, self.yT_done, newest)
            need(pe, sh.x_done, self.x0 + b)
            for t in range(TP):
                i = pe.transpose(self.pm[:, t * P:(t + 1) * P], self.hg[:, u, t, :], ident[:, :])
            i.then_inc(self.hT_ready, 1)

        def out(b, u):
            pe.wait_ge(self.hT_done, b + 1)
            for t in range(TP):
                i = pe.matmul(self.pm[:, t * C:(t + 1) * C], self.hT[:, u, t * P:(t + 1) * P], self.wd[:, :],
                              start=True, stop=True)
            i.then_inc(self.out_done, 1)

        def step(s, u):
            if inside(s + 1):
                turn(s + 1, 1 - u)
            if inside(s):
                scores(s, u)
            if inside(s - 2):
                turn_back(s - 2, u, s + 2 if inside(s + 1) else B)
            if inside(s + 1):
                project_qk(s + 1, 1 - u)
            if inside(s - 2):
                out(s - 2, u)
            for h in range(NH):
                if inside(s):
                    attend(s, u, h)
                if h < TP and inside(s + 1):
                    project_vo(s + 1, 1 - u, h)

        sh.start(pe, self.x0)
        pe.wait_ge(sh.consts, sh.N_CONSTS)
        pe.wait_ge(self.setup, 2)
        turn_first(0, 0)
        pipeline(pe, score, 0, B - 1, 2, B - 3)
        turn_gates()
        pe.wait_ge(self.cols_done, 1)
        turn(0, 0)
        project_qk(0, 0)
        for t in range(TP):
            project_vo(0, 0, t)
        self.steps(pe, step)

    def scalar(self, act):
        def xT(b, u):
            act.wait_ge(self.xT_ready, b + 1)
            need(act, self.scored, b - 1)
            act.activation(self.xT[:, u, :], self.ps[u][:, 0:T], ACT.Copy).then_inc(self.xT_done, 1)

        def x2T(b, u):
            act.wait_ge(self.yT_ready, b + 1)
            need(act, self.vo_ready, b - 1)
            act.activation(self.xT[:, u, :], self.pm[:, 0:T], ACT.Copy).then_inc(self.yT_done, 1)

        def qk(b, u):
            act.wait_ge(self.qk_ready, b + 1)
            need(act, self.s_done, NH * (b - 1))
            act.activation(self.qs[:, u, :], self.pq[:, 0:T], ACT.Copy, scale=float(DH) ** -0.5)
            for h in range(NH):
                k = slice(DH * h, DH * h + DH)
                i = act.activation(self.ks[k, u, h, :], self.pq[k, T:2 * T], ACT.Copy)
            i.then_inc(self.qk_done, 1)

        def vo(b, u):
            act.wait_ge(self.vo_ready, b + 1)
            need(act, self.av_done, b - 1)
            need(act, self.hg_done, b - 1)
            src = self.pvo[:, :].rearrange("p (t n) -> p t n", t=TP)
            act.activation(self.vx[:, u, :, :, 0:DH], src[:, :, 0:C].rearrange("p t (h d) -> p t h d", h=NH), ACT.Copy)
            act.activation(self.th[:, u, :, :], src[:, :, C:2 * C], ACT.Tanh, scale=0.5).then_inc(self.vo_done, 1)

        def decay(b, u):
            act.wait_ge(self.logd_done, b + 1)
            d = self.logd[:, u, :, :].rearrange("p h n -> p (h n)")
            act.activation(d, d, ACT.Exp).then_inc(self.d_done, 1)

        def avc(b, u):
            act.wait_ge(self.av_done, b + 1)
            need(act, self.head.sem, 5 * (b - 1))
            n = TP * NH * (DH + 1)
            act.activation(self.av[:, u, :, :].rearrange("p a d -> p (a d)"), self.pav[:, 0:n], ACT.Copy).then_inc(self.avc_done, 1)

        def square(b, u):
            act.wait_ge(self.cen_done, b + 1)
            need(act, self.var_done, b - 1)
            act.activation(self.sq[:, u, :, :], self.d[:, u, :, :], ACT.Square).then_inc(self.sq_done, 1)

        def hT(b, u):
            act.wait_ge(self.hT_ready, b + 1)
            need(act, self.out_done, b - 1)
            act.activation(self.hT[:, u, :], self.pm[:, 0:T], ACT.Copy).then_inc(self.hT_done, 1)

        def step(s, u):
            if inside(s + 1):
                x2T(s + 1, 1 - u)
            if inside(s):
                decay(s, u)
            if inside(s - 2):
                hT(s - 2, u)
            if inside(s - 1):
                square(s - 1, 1 - u)
            if inside(s + 1):
                qk(s + 1, 1 - u)
                vo(s + 1, 1 - u)
            if inside(s):
                avc(s, u)

        self.sh.start(act, self.x0)
        pipeline(act, xT, 0, B - 1, 2, B - 3)
        act.wait_ge(self.gates, 1)
        act.activation(self.cap[:, :, :], self.raw[:, :, :], ACT.Tanh, scale=1.0 / CAPG).then_inc(self.tanh_done, 1)
        act.wait_ge(self.gates, 4)
        act.activation(self.g_e[:, :, :], self.g_abs[:, :, :], ACT.Exp, scale=-1.0).then_inc(self.gexp_done, 1)
        act.wait_ge(self.rows, 5)
        act.activation(self.r_em[:, :], self.r_m[:, :], ACT.Exp, scale=-1.0).then_inc(self.em_done, 1)
        act.wait_ge(self.cols_done, 1)
        x2T(0, 0)
        qk(0, 0)
        vo(0, 0)
        self.steps(act, step)

    GATE_STEPS = 1 + 3 + 4 + SERIES + 1 + 1

    def vector(self, dve):
        sh, X = self.sh, self.sh.X

        def gate_math():
            k = [0]

            def link(ins):
                k[0] += 1
                ins.then_inc(self.gates, 1)
                dve.wait_ge(self.gates, k[0])

            dve.wait_ge(self.scored, B)
            wide = self.bias[:, :].unsqueeze(1).to_broadcast([P, NT, 2 * NH])
            link(dve.tensor_tensor(self.raw[:, :, :], self.pq[:, :].rearrange("p (n g) -> p n g", g=2 * NH), wide, ALU.add))
            dve.wait_ge(self.tanh_done, 1)
            by = lambda t: t[:, :, :].rearrange("p t (b h) -> p (t b) h", h=NH)
            link(dve.tensor_scalar(by(self.g_ig), self.cap[:, :, 0:NH], CAPG, None, ALU.mult))
            link(dve.tensor_scalar(by(self.g_fg), self.cap[:, :, NH:2 * NH], CAPG, None, ALU.mult))
            flat = lambda t: t[:, :, :].rearrange("p t n -> p (t n)")
            fg, e, s, s2, acc, acc2 = (flat(t) for t in (self.g_fg, self.g_e, self.g_s, self.g_s2, self.g_acc, self.g_acc2))
            link(dve.scalar_tensor_tensor(out=flat(self.g_abs), in0=fg, scalar=-1.0, in1=fg, op0=ALU.mult, op1=ALU.max))
            dve.wait_ge(self.gexp_done, 1)
            dve.tensor_scalar(flat(self.g_neg), fg, 0.0, None, ALU.min)
            link(dve.tensor_scalar(acc, e, 2.0, None, ALU.add))
            link(dve.reciprocal(acc2, acc))
            link(dve.tensor_tensor(s, e, acc2, ALU.mult))
            link(dve.tensor_tensor(s2, s, s, ALU.mult))
            n = self.SERIES
            a, b = acc, acc2
            link(dve.tensor_scalar(a, s2, 1.0 / (2 * n + 1), None, ALU.mult))
            for j in range(n - 1, 0, -1):
                link(dve.scalar_tensor_tensor(out=b, in0=a, scalar=1.0 / (2 * j + 1), in1=s2, op0=ALU.add, op1=ALU.mult))
                a, b = b, a
            link(dve.scalar_tensor_tensor(out=b, in0=a, scalar=1.0, in1=s, op0=ALU.add, op1=ALU.mult))
            link(dve.scalar_tensor_tensor(out=flat(self.g_lf), in0=b, scalar=-2.0, in1=flat(self.g_neg), op0=ALU.mult, op1=ALU.add))
            assert k[0] == self.GATE_STEPS, k

        def row_math():
            k = [0]

            def link(ins):
                k[0] += 1
                ins.then_inc(self.rows, 1)
                dve.wait_ge(self.rows, k[0])

            dve.wait_ge(self.rows_ready, 1)
            ones = self.ones[:, 0:1].to_broadcast([P, T])
            link(dve.tensor_tensor_scan(self.r_cum[:, :], ones, self.pvo[:, 0:T], 0.0, ALU.mult, ALU.add))
            link(dve.tensor_tensor(self.r_a[:, :], self.pvo[:, T:2 * T], self.r_cum[:, :], ALU.subtract))
            link(dve.tensor_tensor_scan(self.r_run[:, :], self.r_a[:, :], self.r_a[:, :], -3.0e38, ALU.max, ALU.max))
            link(dve.tensor_scalar(self.r_negrun[:, :], self.r_run[:, :], -1.0, None, ALU.mult))
            link(dve.tensor_tensor(self.r_m[:, :], self.r_cum[:, :], self.r_run[:, :], ALU.add))
            dve.wait_ge(self.cols_ready, 1)
            flat = lambda t: t[:, :, :].rearrange("p t n -> p (t n)")
            dve.tensor_copy(flat(self.aT), self.pav[:, 0:T])
            dve.tensor_copy(flat(self.emT), self.pav[:, T:2 * T])
            dve.wait_ge(self.run_stored, 16)
            dve.memset(self.ks[:, :, :, :], 0.0)
            dve.memset(self.vx[:, :, :, :, DH:DH + 1], 1.0).then_inc(self.cols_done, 1)

        def log_decay(b, u):
            dve.wait_ge(self.row_in[u], 8 * (b - u) + 16)
            need(dve, self.ct_done, NH * (b - 1))
            for h in range(NH):
                a = [self.aT[:, t, bass.ds(NH * b + h, 1)] for t in range(TP)]
                dve.scalar_tensor_tensor(out=self.logd[:, u, h, 0:T], in0=self.run_row[:, u, h, :], scalar=a[0],
                                         in1=self.mask[:, :], op0=ALU.add, op1=ALU.min)
                i = dve.scalar_tensor_tensor(out=self.logd[:, u, h, T:T + P], in0=self.run_row[:, u, h, P:T], scalar=a[1],
                                             in1=self.mask[:, 0:P], op0=ALU.add, op1=ALU.min)
            i.then_inc(self.logd_done, 1)

        def weights(b, u):
            dve.wait_ge(self.d_done, b + 1)
            need(dve, self.av_done, b - 1)
            for h in range(NH):
                dve.wait_ge(self.s_done, NH * b + h + 1)
                dve.tensor_tensor(self.ct[:, u, h, :], self.ps[h][:, 0:self.TRI], self.logd[:, u, h, :],
                                  ALU.mult).then_inc(self.ct_done, 1)

        def heads(b, u):
            ch, n8 = self.head, self.n8
            ch.begin(b)
            dve.wait_ge(self.avc_done, b + 1)
            total = self.av[:, u, :, DH]
            wide = lambda t: t.unsqueeze(2).to_broadcast([P, TP * NH, DH])
            by = lambda t: t[:, u, :, :].rearrange("p t (h d) -> p (t h) d", d=DH)
            ch.link(dve, dve.scalar_tensor_tensor(out=n8[:, u, 0, :], in0=total, scalar=-1.0, in1=total, op0=ALU.mult, op1=ALU.max))
            em = self.emT[:, :, bass.ds(NH * b, NH)]
            two = lambda t: t.rearrange("p (t h) -> p t h", t=TP)
            ch.link(dve, dve.tensor_tensor(two(n8[:, u, 1, :]), two(n8[:, u, 0, :]), em, ALU.max))
            ch.link(dve, dve.tensor_scalar(n8[:, u, 0, :], n8[:, u, 1, :], EPS_HEAD, None, ALU.add))
            ch.link(dve, dve.reciprocal(n8[:, u, 1, :], n8[:, u, 0, :]))
            need(dve, self.cen_done, b - 1)
            ch.link(dve, dve.tensor_tensor(by(self.hv), self.av[:, u, :, 0:DH], wide(n8[:, u, 1, :]), ALU.mult))
            ch.end()
            dve.tensor_reduce(n8[:, u, 2, :], by(self.hv), AX.X, ALU.add).then_inc(self.hsum, 1)

        def variance(b, u):
            dve.wait_ge(self.sq_done, b + 1)
            dve.tensor_reduce(self.n8[:, u, 3, :], self.sq[:, u, :, :].rearrange("p t (h d) -> p (t h) d", d=DH),
                              AX.X, ALU.add).then_inc(self.var_done, 1)

        def gate_out(b, u):
            dve.wait_ge(self.hn_done, b + 1)
            need(dve, self.hT_ready, b - 1)
            flat = lambda t: t[:, u, :, :].rearrange("p t c -> p (t c)")
            dve.scalar_tensor_tensor(out=flat(self.hg), in0=flat(self.th), scalar=1.0, in1=flat(self.hn), op0=ALU.add,
                                     op1=ALU.mult).then_inc(self.hg_done, 1)

        def update(b):
            dve.wait_ge(self.out_done, b + 1)
            x = X[:, bass.ds(TP * b, TP), :]
            dve.tensor_tensor(x, x, self.pm[:, 0:TP * C].rearrange("p (t c) -> p t c", t=TP), ALU.add).then_inc(sh.x_done, 1)

        def step(s, u):
            if inside(s - 1):
                heads(s - 1, 1 - u)
            if inside(s):
                weights(s, u)
            if inside(s - 1):
                variance(s - 1, 1 - u)
            if inside(s + 1):
                log_decay(s + 1, 1 - u)
            self.moments_next(dve, s - 3, 1 - u)
            if inside(s - 1):
                gate_out(s - 1, 1 - u)
            if inside(s - 2):
                update(s - 2)

        sh.start(dve, self.x0)
        dve.wait_ge(sh.consts, sh.N_CONSTS)
        dve.wait_ge(self.w_in, 16 * (len(self.LOADS) + 1))
        dve.memset(self.ones[:, :], 1.0)
        dve.tensor_scalar(self.wd[:, :], self.wd0[:, :], self.nw[:, 0:1], 0.5, ALU.mult, ALU.mult).then_inc(self.setup, 1)
        pipeline(dve, lambda b, u: self.norm.vector(dve, b, u, lambda: apart(dve, self.xT_ready, b - 1, sh.passed)), 0, B - 1, 2, B - 3)
        gate_math()
        row_math()
        log_decay(0, 0)
        self.steps(dve, step)
        self.moments_next(dve, B - 1, 1)

    def gpsimd(self, pool):
        sh = self.sh

        def again(b, u):
            apart(pool, self.yT_ready, b - 1, sh.passed)
            self.norm.spread(pool, b, u, self.xa_centred, self.xa_done)

        by = lambda t, u: t[:, u, :, :].rearrange("p t (h d) -> p (t h) d", d=DH)
        wide = lambda t: t.unsqueeze(2).to_broadcast([P, TP * NH, DH])

        def centre(b, u):
            n8 = self.n8
            apart(pool, self.hsum, b + 1, sh.passed)
            apart(pool, self.hn_done, b - 1, sh.passed)
            pool.tensor_scalar(n8[:, u, 4, :], n8[:, u, 2, :], -1.0 / DH, 0.0, ALU.mult, ALU.add).then_inc(self.mean_done, 1)
            pool.wait_ge(self.mean_done, b + 1)
            pool.tensor_tensor(by(self.d, u), by(self.hv, u), wide(n8[:, u, 4, :]), ALU.add).then_inc(self.cen_done, 1)

        def scale(b, u):
            n8, ch = self.n8, self.rstd
            ch.begin(b)
            apart(pool, self.var_done, b + 1, sh.passed)
            ch.link(pool, pool.tensor_scalar(n8[:, u, 4, :], n8[:, u, 3, :], 1.0 / DH, EPS_HEAD, ALU.mult, ALU.add))
            ch.link(pool, pool.tensor_tensor(n8[:, u, 5, :], n8[:, u, 4, :], sh.mhalf[:, 0:TP * NH], ALU.pow))
            ch.end()
            need(pool, self.hg_done, b - 1)
            pool.tensor_tensor(by(self.hn, u), by(self.d, u), wide(n8[:, u, 5, :]), ALU.mult).then_inc(self.hn_done, 1)

        def step(s, u):
            if inside(s - 1):
                centre(s - 1, 1 - u)
            if inside(s + 2):
                again(s + 2, u)
            if inside(s - 1):
                scale(s - 1, 1 - u)
            self.scale_next(pool, s - 3, 1 - u)

        sh.start(pool, self.x0)
        pool.memset(self.mask[:, :], 0.0).then_inc(self.mask_set, 1)
        pool.wait_ge(self.mask_set, 1)
        pool.affine_select(out=self.mask[:, 0:P], in_=self.mask[:, 0:P], compare_op=ALU.is_ge, fill=-BIG, base=0,
                           pattern=[[1, P]], channel_multiplier=-1).then_inc(self.setup, 1)
        pool.wait_ge(self.xT_ready, B)
        again(0, 0)
        again(1, 1)
        self.steps(pool, step)
        self.scale_next(pool, B - 1, 1)


class Split:

    def __init__(self, sh, tag, parts, stage_mem, after):
        self.sh, self.parts, self.after = sh, parts, after
        self.loaded, self.hi, self.lo = (sh.sem(f"{tag}_{n}") for n in ("loaded", "hi_done", "lo_done"))
        self.told = set()
        self.stage = [stage_mem.take(f"{tag}_stage{n}", [P, p[0].shape[1]]) for n, p in enumerate(parts)]

    def sync(self, sp):
        need(sp, self.sh.x_done, self.after)
        for (_, _, name), st in zip(self.parts, self.stage):
            sp.dma_start(st[:, :], self.sh.args[name]).then_inc(self.loaded, 16)

    def scalar(self, act):
        act.wait_ge(self.loaded, 16 * len(self.parts))
        for (hi, _, _), st in zip(self.parts, self.stage):
            act.activation(hi, st[:, :], ACT.Copy).then_inc(self.hi, 1)

    def vector(self, dve):
        for n, ((hi, lo, _), st) in enumerate(zip(self.parts, self.stage)):
            dve.wait_ge(self.hi, n + 1)
            dve.tensor_tensor(lo, st[:, :], hi.bitcast(F32), ALU.subtract).then_inc(self.lo, 1)

    def once(self, eng, part):
        if part not in self.told:
            self.told.add(part)
            part(eng)

    def sync_once(self, sp):
        self.once(sp, self.sync)

    def scalar_once(self, act):
        self.once(act, self.scalar)

    def vector_once(self, dve):
        self.once(dve, self.vector)

    def ready(self, eng):
        eng.wait_ge(self.lo, len(self.parts))


def build(nc, args, out):
    with ExitStack() as ctx:
        sh = Shared(nc, ctx, args)
        mem = sh.mem
        base = mem.at
        layers = []
        first = {}
        choice_w = ChoiceWeights(sh, mem) if "choice" in LAYERS else None
        above = mem.at
        for n, kind in enumerate(LAYERS):
            if kind in first:
                layers.append((first[kind], n, 1))
                continue
            if kind == "choice":
                mem.at = above
                layer = Choice(sh, "choice", choice_w, mem)
                mem.at = layer.big
                choice_w.split = Split(sh, "ec", choice_w.parts, mem, 0)
            elif kind == "top2":
                mem.at = base
                w = Top2Weights(sh, mem)
                above_top2 = mem.at
                layer = Top2(sh, "top2", w, mem)
                mem.at = layer.big
                w.split = Split(sh, "t2", w.parts, mem, n * B)
            elif kind == "rwkv":
                mem.at = above
                layer = Rwkv(sh, "rwkv", mem)
            elif kind == "mlstm":
                mem.at = above_top2 if "top2" in LAYERS else base
                layer = Mlstm(sh, "mlstm", mem)
            first[kind] = layer
            layers.append((layer, n, 0))
        block = ctx.enter_context(nc.Block())

        @block.sync
        def _(sp):
            part = [slice(c * NT // XC, (c + 1) * NT // XC) for c in range(XC)]
            for c in range(XC):
                sp.dma_start(sh.X[:, part[c], :], args["x"][:, part[c], :]).then_inc(sh.x_loaded[c], 16)
            if choice_w is not None:
                choice_w.sync(sp)
            for layer, n, run in layers:
                layer.stand(n, run)
                layer.sync(sp)
            for c in range(XC):
                sp.wait_ge(sh.x_done, (len(LAYERS) - 1) * B + (c + 1) * B // XC)
                sp.dma_start(out[:, part[c], :], sh.X[:, part[c], :]).then_inc(sh.stored, 16)
            sp.wait_ge(sh.stored, 16 * XC)

        @block.tensor
        def _(pe):
            for layer, n, run in layers:
                layer.stand(n, run)
                layer.tensor(pe)

        @block.scalar
        def _(act):
            for layer, n, run in layers:
                layer.stand(n, run)
                layer.scalar(act)

        @block.vector
        def _(dve):
            sh.moments_first(dve)
            for layer, n, run in layers:
                layer.stand(n, run)
                layer.vector(dve)

        @block.gpsimd
        def _(pool):
            sh.constants(pool)
            sh.scale_first(pool)
            for layer, n, run in layers:
                layer.stand(n, run)
                layer.gpsimd(pool)


def laid_out(i):
    import numpy as np
    a = {k: np.asarray(v) for k, v in i.items()}
    t = lambda v: np.ascontiguousarray(v)
    return {
        "x": t(a["L0_attn_x"].reshape(NT, P, C).transpose(1, 0, 2)),
        "rk_cols": t(np.stack([a[n].reshape(C) for n in (
            "L0_attn_time_decay", "L0_attn_time_mix_k", "L0_attn_time_mix_v", "L0_attn_time_mix_r",
            "L0_attn_ln_g", "L0_attn_ln_b")], 1)),
        "rk_w": t(np.concatenate([a[n].T for n in ("L0_attn_Wk", "L0_attn_Wv", "L0_attn_Wr", "L0_attn_Wo")], 1)),
        "ml_wq": t(a["L1_attn_Wq"]),
        "ml_wk": t(a["L1_attn_Wk"]),
        "ml_wvo": t(np.concatenate([a["L1_attn_Wv"], a["L1_attn_Wo"]], 1)),
        "ml_wdown": t(a["L1_attn_Wdown"]),
        "ml_wgate": t(np.concatenate([a["L1_attn_Wig"], a["L1_attn_Wfg"]], 1)),
        "ml_norm_w": t(a["L1_attn_norm_w"].reshape(C, 1)),
        "ml_bias": t(np.concatenate([a["L1_attn_big"], a["L1_attn_bfg"]]).reshape(1, 2 * NH)),
        "ec_gate": t(a["L0_ffn_gate_w"]),
        "ec_w1": t(a["L0_ffn_w1"].transpose(1, 0, 2).reshape(C, E * H0)),
        "ec_w2": t(a["L0_ffn_w2"].reshape(E, HC, P, C).transpose(2, 0, 1, 3).reshape(P, E * H0)),
        "t2_wg": t(a["L1_ffn_w_g"].transpose(1, 0, 2).reshape(C, HID)),
        "t2_wu": t(a["L1_ffn_w_u"].transpose(1, 0, 2).reshape(C, HID)),
        "t2_wd": t(a["L1_ffn_w_d"].reshape(NCH, P, C).transpose(1, 0, 2).reshape(P, HID)),
        "t2_gate": t(a["L1_ffn_w_gate"]),
    }


def kernel(**inputs):
    import numpy as np
    import concourse.bacc as bacc
    from concourse.bass_utils import run_bass_kernel_spmd

    nc = bacc.Bacc("TRN2", target_bir_lowering=False, num_devices=1)
    arrays = laid_out(inputs)
    args = {n: nc.dram_tensor(f"in_{n}", a.shape, F32, kind="ExternalInput").ap() for n, a in arrays.items()}
    out = nc.dram_tensor("out_x", (P, NT, C), F32, kind="ExternalOutput").ap()
    build(nc, args, out)
    r = run_bass_kernel_spmd(nc, [{f"in_{n}": a for n, a in arrays.items()}], core_ids=[0])
    y = np.asarray(r.results[0]["out_x"])
    return np.ascontiguousarray(y.transpose(1, 0, 2)).reshape(B, T, C)
```

```python
import math
from contextlib import ExitStack

import concourse.bass as bass
from concourse import mybir

F32 = mybir.dt.float32
F32R = mybir.dt.float32r
U32 = mybir.dt.uint32
ACT = mybir.ActivationFunctionType
ALU = mybir.AluOpType
AX = mybir.AxisListType

P = 128
B, T, C = 32, 256, 128
TP = T // P
NT = B * TP
E = 8
H0 = 512
HC = H0 // P
CAP = 2 * T // E
SLOTS = E * CAP
EP = E // 2
M1 = 176
HID = E * M1
NCH = HID // P
NH, DH = 4, 32
EPS_LN = 1e-5
EPS_HEAD = 1e-6
CAPG = 15.0
BIG = 1.0e30
FB = 4
XC = B // FB

LAYERS = ("choice", "rwkv", "choice", "top2", "mlstm", "top2")


def need(eng, sem, value):
    if isinstance(value, int) and value <= 0:
        return
    eng.wait_ge(sem, value)


def apart(eng, sem, value, passed):
    if not (isinstance(value, int) and value <= 0):
        eng.wait_ge(sem, value).then_inc(passed, 1)


def inside(b, n=B):
    return not isinstance(b, int) or 0 <= b < n


def pipeline(eng, step, first, last, lo, hi, o=0):
    for s in range(first, lo):
        step(o + s, s % 2)
    with eng.Fori((o + lo) // 2, (o + hi + 1) // 2) as i:
        for u in range(2):
            step(2 * i + u, u)
    for s in range(hi + 1, last + 1):
        step(o + s, s % 2)


class Layer:

    def stand(self, layer, run):
        self.layer, self.run, self.o = layer, run, run * B
        self.x0 = layer * B - self.o
        self.norm.layer, self.norm.o = layer, self.o
        self.ahead = layer > 0 and LAYERS[layer - 1] == "rwkv"

    def moments_next(self, dve, b, u):
        if self.has(b):
            self.sh.moments.moments_of(dve, self.layer + 1, b - self.o, u)

    def scale_next(self, pool, b, u):
        if self.has(b):
            self.sh.moments.scale(pool, self.layer + 1, b - self.o, u)

    def has(self, b):
        return not isinstance(b, int) or inside(b - self.o)


class Chain:

    def __init__(self, sem, per, base=0):
        self.sem, self.per, self.base = sem, per, base

    def begin(self, b):
        self.b, self.k = b, 0

    def link(self, eng, ins, passed=None):
        self.k += 1
        ins.then_inc(self.sem, 1)
        if passed is not None:
            apart(eng, self.sem, self.base + self.b * self.per + self.k, passed)
        else:
            eng.wait_ge(self.sem, self.base + self.b * self.per + self.k)

    def end(self):
        assert self.k == self.per, (self.k, self.per)


class Memory:

    def __init__(self, nc, base):
        self.nc, self.at, self.top = nc, base, 0

    def take(self, name, shape, dtype=F32):
        n = 4
        for d in shape[1:]:
            n *= d
        t = self.nc.alloc_sbuf_tensor_at(name, shape, dtype, offset=self.at)
        self.at += (n + 31) // 32 * 32
        self.top = max(self.top, self.at)
        assert self.at <= self.nc.sbuf_usable_end, (name, self.at)
        return t


class Shared:

    def __init__(self, nc, ctx, args):
        self.nc, self.ctx, self.args = nc, ctx, args
        self.mem = Memory(nc, (nc.sbuf_base + 63) // 64 * 64)
        m = self.mem
        self.X = m.take("X", [P, NT, C])
        self.ident = m.take("ident", [P, P])
        self.mhalf = m.take("minus_half", [P, 16])
        self.mone = m.take("minus_one", [P, FB * TP])
        self.euler = m.take("e", [P, TP])
        self.iota_tok = m.take("iota_tok", [P, T])
        self.iota_part = m.take("iota_part", [P, TP])
        self.iota_i = m.take("iota_tok_int", [P, T], mybir.dt.int32)
        self.iota_pi = m.take("iota_part_int", [P, TP], mybir.dt.int32)
        self.banks = [ctx.enter_context(nc.psum_tensor(f"bank{i}", [P, 512], F32)) for i in range(8)]
        self.x_loaded = [self.sem(f"x_loaded{c}") for c in range(XC)]
        self.consts = self.sem("consts_ready")
        self.passed = self.sem("passed")
        self.x_done = self.sem("x_done")
        self.stored = self.sem("stored")
        self.moments = Moments(self)

    def sem(self, name):
        return self.ctx.enter_context(self.nc.semaphore(name))

    N_CONSTS = 9

    def start(self, eng, x0):
        need(eng, self.x_done, x0)

    def constants(self, pool):
        nc = self.nc
        pool.memset(self.ident[:, :], 0.0).then_inc(self.consts, 1)
        pool.memset(self.mhalf[:, :], -0.5).then_inc(self.consts, 1)
        pool.memset(self.mone[:, :], -1.0).then_inc(self.consts, 1)
        pool.memset(self.euler[:, :], math.e).then_inc(self.consts, 1)
        pool.iota(self.iota_i[:, :], [[1, T]], base=0, channel_multiplier=0).then_inc(self.consts, 1)
        pool.iota(self.iota_pi[:, :], [[P, TP]], base=0, channel_multiplier=1).then_inc(self.consts, 1)
        pool.wait_ge(self.consts, 6)
        pool.affine_select(out=self.ident[:, :], in_=self.ident[:, :], compare_op=ALU.not_equal, fill=1.0,
                           base=0, pattern=[[-1, P]], channel_multiplier=1).then_inc(self.consts, 1)
        pool.tensor_copy(self.iota_tok[:, :], self.iota_i[:, :]).then_inc(self.consts, 1)
        pool.tensor_copy(self.iota_part[:, :], self.iota_pi[:, :]).then_inc(self.consts, 1)


class Moments:

    def __init__(self, sh):
        mem, self.sh = sh.mem, sh
        self.st = mem.take("bnstats", [P, 2, FB * TP, 6])
        self.mv = mem.take("moments", [P, 2, FB * TP, 2])
        self.small = mem.take("rstd_steps", [P, 2, 4, FB * TP])
        self.nm = mem.take("negmean", [P, B, TP])
        self.rs = mem.take("rstd", [P, B, TP])
        self.stats, self.moments, self.scaled = sh.sem("stats_done"), sh.sem("moments_done"), sh.sem("scaled")
        steps = sh.sem("rstd_steps")
        self.chains, base = [], 0
        for n, kind in enumerate(LAYERS):
            self.chains.append(Chain(steps, self.PER[kind == "rwkv"], base))
            base += (B if n else XC) * self.PER[kind == "rwkv"]

    PER = (1, 6)

    def moments_of(self, dve, layer, b, u):
        if layer == len(LAYERS) or not inside(b):
            return
        n = layer * B + b
        apart(dve, self.sh.x_done, n - B + 1, self.sh.passed)
        self.take(dve, n, 1, b, slice(0, TP), u)

    def scale(self, pool, layer, b, u):
        if layer < len(LAYERS) and inside(b):
            self.rstd(pool, layer, b, 1, b, slice(0, TP), u)

    def moments_first(self, dve, between=None):
        for c in range(XC):
            dve.wait_ge(self.sh.x_loaded[c], 16)
            self.take(dve, FB * c, FB, FB * c, slice(0, FB * TP), c % 2)
            if between is not None and c:
                between(c - 1)
        if between is not None:
            between(XC - 1)

    def scale_first(self, pool):
        for c in range(XC):
            self.rstd(pool, 0, c, FB, FB * c, slice(0, FB * TP), c % 2)

    def take(self, dve, n, count, b, tiles, u):
        apart(dve, self.scaled, n - count, self.sh.passed)
        for t in range(tiles.stop):
            i = dve.bn_stats(self.st[:, u, t, :], self.sh.X[:, bass.ds(TP * b + t, 1), :])
        i.then_inc(self.stats, count)
        apart(dve, self.stats, n + count, self.sh.passed)
        for t in range(tiles.stop):
            i = dve.bn_aggr(self.mv[:, u, t, :], self.st[:, u, t, :])
        i.then_inc(self.moments, count)

    def rstd(self, pool, layer, k, count, b, tiles, u):
        n, ch = layer * B + b, self.chains[layer]
        sm = self.small[:, u, :, tiles]
        flat = lambda t: t[:, bass.ds(b, count), :].rearrange("p a t -> p (a t)")
        half, one = self.sh.mhalf[:, tiles], self.sh.mone[:, tiles]
        ch.begin(k)
        apart(pool, self.moments, n + count, self.sh.passed)
        mean, var = self.mv[:, u, tiles, 0], self.mv[:, u, tiles, 1]
        pool.tensor_tensor(flat(self.nm), mean, one, ALU.mult)
        ch.link(pool, pool.tensor_scalar(sm[:, 0, :], var, 1.0, EPS_LN, ALU.mult, ALU.add))
        if ch.per > 1:
            ch.link(pool, pool.tensor_tensor(sm[:, 1, :], sm[:, 0, :], half, ALU.pow))
            ch.link(pool, pool.tensor_tensor(sm[:, 2, :], sm[:, 1, :], sm[:, 1, :], ALU.mult))
            ch.link(pool, pool.tensor_tensor(sm[:, 2, :], sm[:, 2, :], var, ALU.mult), self.sh.passed)
            ch.link(pool, pool.tensor_scalar(sm[:, 2, :], sm[:, 2, :], 1.0, EPS_LN, ALU.mult, ALU.add))
            ch.link(pool, pool.tensor_tensor(sm[:, 3, :], sm[:, 2, :], half, ALU.pow))
            i = pool.tensor_tensor(flat(self.rs), sm[:, 1, :], sm[:, 3, :], ALU.mult)
        else:
            i = pool.tensor_tensor(flat(self.rs), sm[:, 0, :], half, ALU.pow)
        ch.end()
        i.then_inc(self.scaled, count)


class Normed:

    def __init__(self, sh, tag, mem):
        self.sh, self.layer, self.o = sh, 0, 0
        self.xn = mem.take(f"{tag}_xn", [P, 2, TP, C])
        self.centred, self.done = sh.sem(f"{tag}_xn_centred"), sh.sem(f"{tag}_xn_done")

    def both(self, b):
        m, at = self.sh.moments, bass.ds(b - self.o, 1)
        return (t[:, at, :].rearrange("p a t -> p (a t)") for t in (m.nm, m.rs))

    def gpsimd(self, pool, b, u, xn_free, other=0):
        apart(pool, self.sh.moments.scaled, self.layer * B + b - self.o + 1, self.sh.passed)
        xn_free()
        self.spread(pool, b, u, self.centred, self.done, other)

    def spread(self, pool, b, u, centred, done, other=0):
        nm, rs = (t.unsqueeze(2).to_broadcast([P, TP, C]) for t in self.both(b))
        xn = self.xn[:, u, :, :]
        pool.tensor_tensor(xn, self.sh.X[:, bass.ds(TP * (b - self.o), TP), :], nm, ALU.add).then_inc(centred, 1)
        apart(pool, centred, b - other + 1, self.sh.passed)
        pool.tensor_tensor(xn, xn, rs, ALU.mult).then_inc(done, 1)

    def vector(self, dve, b, u, xn_free):
        apart(dve, self.sh.moments.scaled, self.layer * B + b - self.o + 1, self.sh.passed)
        xn_free()
        nm, rs = self.both(b)
        for t in range(TP):
            i = dve.tensor_scalar(self.xn[:, u, t, :], self.sh.X[:, bass.ds(TP * (b - self.o) + t, 1), :].rearrange("p a c -> p (a c)"),
                                  nm[:, t:t + 1], rs[:, t:t + 1], ALU.add, ALU.mult)
        i.then_inc(self.done, 1)


class Top2(Layer):

    NG = (NCH + 1) // 2

    def __init__(self, sh, tag, w, mem):
        self.sh, self.w = sh, w
        self.norm = Normed(sh, tag, mem)
        f = lambda n, s, d=F32: mem.take(f"{tag}_{n}", s, d)
        self.xhi = f("xhi", [P, 2, T], F32R)
        self.xlo = f("xlo", [P, 2, T], F32R)
        self.silu = f("silu", [P, 2, 2 * T])
        self.sc = f("scores", [P, 2, TP, E])
        self.top = f("top8", [P, 2, TP, 8])
        self.idx = f("top8_index", [P, 2, TP, 8], U32)
        self.idxf = f("top2_index", [P, 2, TP, 2])
        self.g = f("gate_small", [P, 2, 5, TP])
        self.one = f("gate_onehot", [P, 2, 2, TP, E])
        self.gate = f("gate", [P, 2, TP, E])
        self.gate2 = f("gate_hi_lo", [P, 2, TP, 2, E], F32R)
        self.gT = f("gate_turned", [2 * E, 2, T], F32R)
        self.big = mem.at
        self.gated = f("silu_gated", [P, 2, 2 * T])
        self.h = f("h", [P, self.NG, 2 * T])
        self.hhi = f("hhi", [P, 2, NCH + 1, T], F32R)
        self.hlo = f("hlo", [P, 2, NCH + 1, T], F32R)
        self.yT = f("yT", [P, T])
        bk = sh.banks
        self.pg, self.pu, self.pG = bk[0:2], bk[2:4], bk[4:6]
        self.py, self.pm = bk[6], bk[7]
        s = lambda n: sh.sem(f"{tag}_{n}")
        self.xT_ready, self.xhi_done, self.xlo_done = s("xT_ready"), s("xhi_done"), s("xlo_done")
        self.scores_ready, self.gap_done, self.gexp_done = s("scores_ready"), s("gap_done"), s("gexp_done")
        self.chain = Chain(s("gate_steps"), 11)
        self.gate_done, self.gT_ready, self.gT_done = s("gate_done"), s("gate_turned"), s("gate_turned_copied")
        self.g_ready, self.gu_done, self.silu_done = s("g_ready"), s("gu_done"), s("silu_done")
        self.gated_done, self.h_done = s("silu_gated_done"), s("h_done")
        self.hhi_done, self.hlo_done = s("hhi_done"), s("hlo_done")
        self.y_done, self.yev_done, self.ytr_done = s("y_done"), s("yev_done"), s("ytr_done")

    def steps(self, eng, step, pre):
        self.sh.start(eng, self.layer * B)
        pre()
        pipeline(eng, step, 0, B + 1, 2, B - 3, self.o)

    def columns(self, k):
        return T * (min(2 * k + 2, NCH) - 2 * k)

    def tensor(self, pe):
        sh, w, ident = self.sh, self.w, self.sh.ident

        def transposes(b, u):
            pe.wait_ge(self.norm.done, b + 1)
            need(pe, self.gT_done, b)
            for t in range(TP):
                i = pe.transpose(self.pm[:, t * P:(t + 1) * P], self.norm.xn[:, u, t, :], ident[:, :])
            i.then_inc(self.xT_ready, 1)

        def scores(b, u):
            pe.wait_ge(self.xlo_done, b + 1)
            for t in range(TP):
                o = self.pm[:, T + t * E:T + (t + 1) * E]
                hi, lo = self.xhi[:, u, t * P:(t + 1) * P], self.xlo[:, u, t * P:(t + 1) * P]
                pe.matmul(o, hi, w.gate_hi[:, :], start=True, stop=False)
                pe.matmul(o, hi, w.gate_lo[:, :], start=False, stop=False)
                i = pe.matmul(o, lo, w.gate_hi[:, :], start=False, stop=True)
            i.then_inc(self.scores_ready, 1)

        def gate_turn(b, u):
            pe.wait_ge(self.gate_done, b + 1)
            for t in range(TP):
                src = self.gate2[:, u, t, :, :].rearrange("p a e -> p (a e)").bitcast(F32)
                i = pe.transpose(self.pm[0:2 * E, t * P:(t + 1) * P], src, ident[:, :])
            i.then_inc(self.gT_ready, 1)

        def pair(b, u, k):
            hi, lo = self.xhi[:, u, :], self.xlo[:, u, :]
            if k == 0:
                pe.wait_ge(self.xlo_done, b + 1)
            for bank, w_hi, w_lo, done, free in ((self.pg, w.g_hi, w.g_lo, self.g_ready, self.silu_done),
                                                 (self.pu, w.u_hi, w.u_lo, None, self.h_done)):
                need(pe, free, self.NG * b + k - 1)
                for c in range(2 * k, min(2 * k + 2, NCH)):
                    o = bank[k % 2][:, (c % 2) * T:(c % 2 + 1) * T]
                    m = slice(c * P, (c + 1) * P)
                    pe.matmul(o, w_hi[:, m], hi, start=True, stop=False)
                    pe.matmul(o, w_hi[:, m], lo, start=False, stop=False)
                    i = pe.matmul(o, w_lo[:, m], hi, start=False, stop=True)
                if done is not None:
                    i.then_inc(done, 1)
            if k == 0:
                pe.wait_ge(self.gT_done, b + 1)
            for c in range(2 * k, min(2 * k + 2, NCH)):
                i = pe.matmul(self.pG[k % 2][:, (c % 2) * T:(c % 2 + 1) * T], w.sel[:, c * P:(c + 1) * P], self.gT[:, u, :],
                              start=True, stop=True)
            i.then_inc(self.gu_done, 1)

        def down(b, u):
            pe.wait_ge(self.hlo_done, self.NG * (b + 1))
            need(pe, sh.x_done, self.x0 + b)
            o = self.py[:, 0:T]
            for c in range(NCH):
                pe.matmul(o, w.d_hi[:, c, :], self.hhi[:, u, c, :], start=(c == 0), stop=False)
                pe.matmul(o, w.d_hi[:, c, :], self.hlo[:, u, c, :], start=False, stop=False)
                i = pe.matmul(o, w.d_lo[:, c, :], self.hhi[:, u, c, :], start=False, stop=(c == NCH - 1))
            i.then_inc(self.y_done, 1)

        def turn_back(b):
            pe.wait_ge(self.yev_done, b + 1)
            for t in range(TP):
                i = pe.transpose(self.py[:, T + t * P:T + (t + 1) * P], self.yT[:, t * P:(t + 1) * P], ident[:, :])
            i.then_inc(self.ytr_done, 1)

        def step(s, u):
            if self.has(s + 1):
                transposes(s + 1, 1 - u)
            for k in range(self.NG):
                if self.has(s):
                    pair(s, u, k)
                if k == 1 and self.has(s + 1):
                    scores(s + 1, 1 - u)
                if k == 2 and self.has(s - 1):
                    down(s - 1, 1 - u)
                if k == 4 and self.has(s - 1):
                    turn_back(s - 1)
                if k == 3 and self.has(s + 1):
                    gate_turn(s + 1, 1 - u)

        def pre():
            pe.wait_ge(sh.consts, sh.N_CONSTS)
            w.ready(pe)
            transposes(self.o, 0)
            scores(self.o, 0)
            gate_turn(self.o, 0)

        self.steps(pe, step, pre)

    def scalar(self, act):
        def xhi(b, u):
            act.wait_ge(self.xT_ready, b + 1)
            need(act, self.gu_done, self.NG * (b - 1))
            act.activation(self.xhi[:, u, :], self.pm[:, 0:T], ACT.Copy).then_inc(self.xhi_done, 1)

        def gate_turned(b, u):
            act.wait_ge(self.gT_ready, b + 1)
            act.activation(self.gT[:, u, :], self.pm[0:2 * E, 0:T], ACT.Copy).then_inc(self.gT_done, 1)

        def silu(b, k):
            n = self.columns(k)
            act.wait_ge(self.g_ready, self.NG * b + k + 1)
            need(act, self.gated_done, self.NG * b + k - 1)
            act.activation(self.silu[:, k % 2, 0:n], self.pg[k % 2][:, 0:n], ACT.Silu).then_inc(self.silu_done, 1)

        def hhi(b, u, k):
            n = self.columns(k)
            act.wait_ge(self.h_done, self.NG * b + k + 1)
            if k == 0:
                need(act, self.y_done, b - 1)
            o = self.hhi[:, u, 2 * k:2 * k + n // T, :].rearrange("p c t -> p (c t)")
            act.activation(o, self.h[:, k, 0:n], ACT.Copy).then_inc(self.hhi_done, 1)

        def yev(b):
            act.wait_ge(self.y_done, b + 1)
            need(act, self.ytr_done, b)
            act.activation(self.yT[:, :], self.py[:, 0:T], ACT.Copy).then_inc(self.yev_done, 1)

        def step(s, u):
            if self.has(s + 1):
                xhi(s + 1, 1 - u)
            for k in range(self.NG):
                if self.has(s):
                    silu(s, k)
                if k == 4 and self.has(s + 1):
                    gate_turned(s + 1, 1 - u)
                if k == 0 and self.has(s - 1):
                    hhi(s - 1, 1 - u, self.NG - 1)
                if k and self.has(s):
                    hhi(s, u, k - 1)
                if k == 3 and self.has(s - 1):
                    yev(s - 1)

        def pre():
            self.w.split.scalar_once(act)
            self.w.split.once(act, self.w.select)
            xhi(self.o, 0)
            gate_turned(self.o, 0)

        self.steps(act, step, pre)

    def vector(self, dve):
        sh, X = self.sh, self.sh.X
        ch = self.chain

        def xlo(b, u):
            dve.wait_ge(self.xhi_done, b + 1)
            dve.tensor_tensor(self.xlo[:, u, :], self.pm[:, 0:T], self.xhi[:, u, :].bitcast(F32),
                              ALU.subtract).then_inc(self.xlo_done, 1)

        def choose(b, u):
            ch.begin(b)
            dve.wait_ge(self.scores_ready, b + 1)
            sc, top, idx = self.sc[:, u, :, :], self.top, self.idx
            ch.link(dve, dve.tensor_copy(sc.rearrange("p t e -> p (t e)"), self.pm[:, T:T + TP * E]), sh.passed)
            for t in range(TP):
                i = dve.max(top[:, u, t, :], self.sc[:, u, t, :])
            ch.link(dve, i)
            dve.tensor_tensor(self.g[:, u, 0, :], top[:, u, :, 1], top[:, u, :, 0], ALU.subtract).then_inc(self.gap_done, 1)
            for t in range(TP):
                i = dve.max_index(idx[:, u, t, :], top[:, u, t, :], self.sc[:, u, t, :])
            ch.link(dve, i)
            ch.link(dve, dve.tensor_copy(self.idxf[:, u, :, :], idx[:, u, :, 0:2]))

        def weigh(b, u):
            g = self.g
            dve.wait_ge(self.gexp_done, b + 1)
            ch.link(dve, dve.tensor_scalar(g[:, u, 2, :], g[:, u, 1, :], 1.0, None, ALU.add))
            ch.link(dve, dve.reciprocal(g[:, u, 2, :], g[:, u, 2, :]))
            ch.link(dve, dve.tensor_scalar(g[:, u, 3, :], g[:, u, 2, :], 0.5, None, ALU.mult))
            ch.link(dve, dve.tensor_tensor(g[:, u, 4, :], g[:, u, 1, :], g[:, u, 3, :], ALU.mult))
            for n in range(2):
                for t in range(TP):
                    i = dve.tensor_scalar(self.one[:, u, n, t, :], sh.iota_tok[:, 0:E], self.idxf[:, u, t, n:n + 1],
                                          g[:, u, 3 + n, t:t + 1], ALU.is_equal, ALU.mult)
            ch.link(dve, i)
            ch.link(dve, dve.tensor_tensor(self.gate[:, u, :, :], self.one[:, u, 0, :, :], self.one[:, u, 1, :, :], ALU.add))
            need(dve, self.gT_ready, b - 1)
            hi, lo = self.gate2[:, u, :, 0, :], self.gate2[:, u, :, 1, :]
            ch.link(dve, dve.tensor_copy(hi, self.gate[:, u, :, :]))
            dve.tensor_tensor(lo, self.gate[:, u, :, :], hi.bitcast(F32), ALU.subtract).then_inc(self.gate_done, 1)
            ch.end()

        def hidden(b, k):
            n = self.columns(k)
            dve.wait_ge(self.silu_done, self.NG * b + k + 1)
            dve.wait_ge(self.gu_done, self.NG * b + k + 1)
            need(dve, self.hlo_done, self.NG * (b - 1) + k + 1)
            dve.tensor_tensor(self.gated[:, k % 2, 0:n], self.silu[:, k % 2, 0:n], self.pG[k % 2][:, 0:n],
                              ALU.mult).then_inc(self.gated_done, 1)
            dve.wait_ge(self.gated_done, self.NG * b + k + 1)
            dve.tensor_tensor(self.h[:, k, 0:n], self.gated[:, k % 2, 0:n], self.pu[k % 2][:, 0:n],
                              ALU.mult).then_inc(self.h_done, 1)

        def update(b):
            dve.wait_ge(self.ytr_done, b + 1)
            x = X[:, bass.ds(TP * (b - self.o), TP), :]
            dve.tensor_tensor(x, x, self.py[:, T:2 * T].rearrange("p (t c) -> p t c", t=TP),
                              ALU.add).then_inc(sh.x_done, 1)

        def step(s, u):
            if self.has(s + 1):
                xlo(s + 1, 1 - u)
            for k in range(self.NG):
                if self.has(s):
                    hidden(s, k)
                if k == 0:
                    self.moments_next(dve, s - 2, u)
                if k == 1 and self.has(s + 1):
                    choose(s + 1, 1 - u)
                if k == 2 and self.has(s + 1):
                    weigh(s + 1, 1 - u)
            if self.has(s - 1):
                update(s - 1)

        def pre():
            self.w.split.rest_once(dve)
            xlo(self.o, 0)
            choose(self.o, 0)
            weigh(self.o, 0)

        self.steps(dve, step, pre)

    def gpsimd(self, pool):
        sh = self.sh

        def norm(b, u):
            self.norm.gpsimd(pool, b, u, lambda: apart(pool, self.xT_ready, b - 1, sh.passed))

        def gate_exp(b, u):
            apart(pool, self.gap_done, b + 1, sh.passed)
            pool.tensor_tensor(self.g[:, u, 1, :], sh.euler[:, :], self.g[:, u, 0, :], ALU.pow).then_inc(self.gexp_done, 1)

        def hlo(b, u, k):
            n = self.columns(k)
            c = slice(2 * k, 2 * k + n // T)
            flat = lambda t: t[:, u, c, :].rearrange("p c t -> p (c t)")
            apart(pool, self.hhi_done, self.NG * b + k + 1, sh.passed)
            pool.tensor_tensor(flat(self.hlo), self.h[:, k, 0:n], flat(self.hhi).bitcast(F32),
                               ALU.subtract).then_inc(self.hlo_done, 1)

        def step(s, u):
            for k in range(self.NG):
                if k == 0 and self.has(s - 1):
                    hlo(s - 1, 1 - u, self.NG - 1)
                if k == 2 and self.has(s + 1):
                    gate_exp(s + 1, 1 - u)
                if k and self.has(s):
                    hlo(s, u, k - 1)
                if k == 3 and self.has(s + 2):
                    norm(s + 2, u)
                if k == 4:
                    self.scale_next(pool, s - 2, u)

        def pre():
            norm(self.o, 0)
            norm(self.o + 1, 1)
            gate_exp(self.o, 0)

        self.steps(pool, step, pre)

    def sync(self, sp):
        self.w.split.sync_once(sp)
        self.w.split.once(sp, self.w.load_sel)


class Top2Weights:
    def __init__(self, sh, mem):
        self.sh = sh
        self.sel0 = mem.take("t2_sel_in", [2 * E, HID])
        self.sel = mem.take("t2_sel", [2 * E, HID], F32R)
        self.sel_in, self.sel_done = sh.sem("t2_sel_in"), sh.sem("t2_sel_done")
        self.g_hi, self.g_lo = (mem.take(f"t2_g_{x}", [P, HID], F32R) for x in ("hi", "lo"))
        self.u_hi, self.u_lo = (mem.take(f"t2_u_{x}", [P, HID], F32R) for x in ("hi", "lo"))
        self.d_hi, self.d_lo = (mem.take(f"t2_d_{x}", [P, NCH, C], F32R) for x in ("hi", "lo"))
        self.gate_hi, self.gate_lo = (mem.take(f"t2_gate_{x}", [P, E], F32R) for x in ("hi", "lo"))
        self.parts = [(self.g_hi[:, :], self.g_lo[:, :], "t2_wg"), (self.u_hi[:, :], self.u_lo[:, :], "t2_wu"),
                      (self.d_hi[:, :, :].rearrange("p a b -> p (a b)"),
                       self.d_lo[:, :, :].rearrange("p a b -> p (a b)"), "t2_wd"),
                      (self.gate_hi[:, :], self.gate_lo[:, :], "t2_gate")]

    def load_sel(self, sp):
        sp.dma_start(self.sel0[:, :], self.sh.args["t2_sel"]).then_inc(self.sel_in, 16)

    def select(self, act):
        act.wait_ge(self.sel_in, 16)
        act.activation(self.sel[:, :], self.sel0[:, :], ACT.Copy).then_inc(self.sel_done, 1)

    def ready(self, pe):
        pe.wait_ge(self.sel_done, 1)
        self.split.ready(pe)


class Choice(Layer):

    GB = 4
    NGRP = B // GB
    GS = GB * CAP
    BH = B // 2

    def __init__(self, sh, tag, w, mem):
        self.sh, self.w = sh, w
        self.norm = Normed(sh, tag, mem)
        f = lambda n, s, d=F32: mem.take(f"{tag}_{n}", s, d)
        self.xT = f("xT", [P, 2, T])
        self.first_end = mem.at
        self.slot_token = f("slot_token", [P, B, EP])
        self.slot_weight = f("slot_weight", [P, B, EP])
        self.xhi = f("xhi", [P, 2, TP, C], F32R)
        self.xlo = f("xlo", [P, 2, TP, C], F32R)
        self.token_row = f("token_row", [P, 2, SLOTS])
        self.pick = f("pick", [P, TP, SLOTS], F32R)
        self.spread = f("spread", [P, 2, EP, T], F32R)
        self.yw = f("yw", [P, 2, EP * C])
        self.yhi = f("yhi", [P, 2, EP * C], F32R)
        self.ylo = f("ylo", [P, 2, EP * C], F32R)
        self.hhi = f("hhi", [P, 2, HC, self.GS], F32R)
        self.hlo = f("hlo", [P, 2, HC, self.GS], F32R)
        self.h = f("h", [P, 2, 2 * self.GS])
        self.big = mem.at
        self.xin_hi = f("xin_hi", [P, 2, self.GB, SLOTS], F32R)
        self.xin_lo = f("xin_lo", [P, 2, self.GB, SLOTS], F32R)
        at = mem.at
        self.yT = f("yT", [P, 2, self.GB, SLOTS])
        end = mem.at
        mem.at = at
        g = lambda n, s, d=F32: mem.take(f"{tag}_c_{n}", s, d)
        self.max = g("max", [P, NT])
        self.sum = g("sum", [P, NT])
        self.prob = g("prob", [P, TP, B, E])
        self.ranked = g("ranked", [P, 2, 2, T])
        self.best = g("best", [P, 2, CAP])
        self.best_at = g("best_at", [P, 2, CAP], U32)
        self.best_atf = g("best_atf", [P, 2, CAP])
        self.twice = g("twice", [P, 2, 2, 2, CAP])
        mem.at = max(end, mem.at)
        bk = sh.banks
        self.ph, self.py, self.pghi, self.pglo = bk[0:2], (bk[2], bk[7]), bk[3], bk[4]
        self.pback, self.psc, self.pxt = bk[5], bk[6], bk[7]
        self.first_banks = ((self.pghi, self.pglo), bk[0:2])
        s = lambda n: sh.sem(f"{tag}_{n}")
        self.xT_ready, self.xT_done, self.scored = s("xT_ready"), s("xT_done"), s("scored")
        self.soft, self.exp_done, self.prob_done = s("softmax_steps"), s("exp_done"), s("prob_done")
        self.probT_ready, self.rank_steps, self.twice_done = s("probT_ready"), s("rank_steps"), s("twice_done")
        self.slots_ready, self.slots_done = s("slots_ready"), s("slots_done")
        self.tokens_stored = s("tokens_stored")
        self.row_in = [s("token_row_in0"), s("token_row_in1")]
        self.pick_done, self.pick_used = s("pick_done"), s("pick_used")
        self.xa_done, self.xa_centred, self.xhi_done, self.xlo_done = s("xa_done"), s("xa_centred"), s("xhi_done"), s("xlo_done")
        self.gathered, self.xin_done = s("gathered"), s("xin_done")
        self.w1_done, self.gelu_done, self.hhi_done, self.hlo_done = s("w1_done"), s("gelu_done"), s("hhi_done"), s("hlo_done")
        self.w2_done, self.yev_done, self.ytr_done = s("w2_done"), s("yev_done"), s("ytr_done")
        self.yw_done, self.yhi_done, self.ylo_done, self.spread_done = s("yw_done"), s("yhi_done"), s("ylo_done"), s("spread_done")
        self.scattered = s("scattered")
        self.token_dram = sh.nc.dram_tensor(f"{tag}_tokens", [B, SLOTS], F32).ap()

    def groups(self, eng, step):
        pipeline(eng, step, 0, self.NGRP + 1, 2, self.NGRP - 3, self.o // self.GB)

    def has_group(self, g):
        return not isinstance(g, int) or inside(g - self.o // self.GB, self.NGRP)

    def back(self, g, e):
        return self.GB * (g - 1) + (e - 1) // 2

    def late(self, g, e):
        return self.GB * (g - 1) + (e - 3) // 2

    def pfirst(self, u):
        return self.sh.banks[7][:, T:2 * T] if self.ahead else self.sh.banks[u][:, 0:T]

    def first_norm(self, pool, b, u):
        self.norm.gpsimd(pool, b, u, lambda: apart(pool, self.xT_ready, b - 1, self.sh.passed), self.o)

    def turn_first(self, pe, b, u):
        pe.wait_ge(self.norm.done, b + 1)
        need(pe, self.xT_done, b if self.ahead else b - 1)
        for t in range(TP):
            i = pe.transpose(self.pfirst(u)[:, t * P:(t + 1) * P], self.norm.xn[:, u, t, :], self.sh.ident[:, :])
        i.then_inc(self.xT_ready, 1)

    def first_xT(self, act, b, u):
        act.wait_ge(self.xT_ready, b + 1)
        need(act, self.scored, b - 1)
        act.activation(self.xT[:, u, :], self.pfirst(u), ACT.Copy).then_inc(self.xT_done, 1)

    def score(self, pe, b, u):
        pe.wait_ge(self.xT_done, b + 1)
        for t in range(TP):
            o = self.psc[:, bass.ds(t * B * E + (b - self.o) * E, E)]
            i = pe.matmul(o, self.xT[:, u, t * P:(t + 1) * P], self.w.gate[:, :], start=True, stop=True)
        i.then_inc(self.scored, 1)

    def tensor(self, pe):
        sh, w, ident, GS = self.sh, self.w, self.sh.ident, self.GS

        def turn_choice():
            pe.wait_ge(self.prob_done, self.run + 1)
            for h in range(2):
                for t in range(TP):
                    src = self.prob[:, t, h * self.BH:(h + 1) * self.BH, :].rearrange("p b e -> p (b e)")
                    pe.transpose(self.pback[:, h * T + t * P:h * T + (t + 1) * P], src, ident[:, :]).then_inc(self.probT_ready, 1)
            for h in range(2):
                pe.wait_ge(self.twice_done, 2 * self.run + h + 1)
                for n in range(2):
                    src = self.twice[:, h, n, :, :].rearrange("p a j -> p (a j)")
                    i = pe.transpose(self.pxt[:, h * T + n * P:h * T + (n + 1) * P], src, ident[:, :])
                i.then_inc(self.slots_ready, 1)

        def gather(q, uq, gp, t, banks=None, free=0):
            hi, lo = banks or (self.pghi, self.pglo)
            pe.wait_ge(self.pick_done, TP * q + t + 1)
            if t == 0:
                pe.wait_ge(self.xlo_done, q + 1)
                need(pe, self.xin_done, q - free)
            pe.matmul(hi[:, :], self.xhi[:, uq, t, :], self.pick[:, t, :], start=(t == 0), stop=(t == TP - 1))
            i = pe.matmul(lo[:, :], self.xlo[:, uq, t, :], self.pick[:, t, :], start=(t == 0), stop=(t == TP - 1))
            i.then_inc(self.pick_used, 1)

        def up(g, gp, e):
            n = E * g + e
            if e == 0:
                pe.wait_ge(self.xin_done, self.GB * (g + 1))
            hi = self.xin_hi[:, gp, :, e * CAP:(e + 1) * CAP]
            lo = self.xin_lo[:, gp, :, e * CAP:(e + 1) * CAP]
            for c in range(HC):
                if c % 2 == 0:
                    need(pe, self.gelu_done, 2 * n + c // 2 - 1)
                o = self.ph[c // 2][:, (c % 2) * GS:(c % 2 + 1) * GS]
                k = slice(c * P, (c + 1) * P)
                pe.matmul(o, w.w1_hi[:, e, k], hi, start=True, stop=False)
                pe.matmul(o, w.w1_hi[:, e, k], lo, start=False, stop=False)
                i = pe.matmul(o, w.w1_lo[:, e, k], hi, start=False, stop=True)
                if c % 2:
                    i.then_inc(self.w1_done, 1)

        def down(g, e):
            n = E * g + e
            ue = e % 2
            pe.wait_ge(self.hlo_done, 2 * n + 2)
            need(pe, self.yev_done, n - 1)
            o = self.py[ue][:, 0:GS]
            for c in range(HC):
                pe.matmul(o, w.w2_hi[:, e, c, :], self.hhi[:, ue, c, :], start=(c == 0), stop=False)
                pe.matmul(o, w.w2_hi[:, e, c, :], self.hlo[:, ue, c, :], start=False, stop=False)
                i = pe.matmul(o, w.w2_lo[:, e, c, :], self.hhi[:, ue, c, :], start=False, stop=(c == HC - 1))
            i.then_inc(self.w2_done, 1)

        def turn(b, gp, bb):
            if bb == 0:
                pe.wait_ge(self.yev_done, 2 * (b + self.GB))
            need(pe, self.yw_done, b)
            for n in range(EP):
                i = pe.transpose(self.pback[:, n * P:(n + 1) * P], self.yT[:, gp, bb, n * P:(n + 1) * P], ident[:, :])
            i.then_inc(self.ytr_done, 1)

        def scatter(b, ub):
            pe.wait_ge(self.ylo_done, b + 1)
            pe.wait_ge(self.spread_done, b + 1)
            need(pe, sh.x_done, self.x0 + b)
            for t in range(TP):
                o = self.psc[:, t * C:(t + 1) * C]
                for n in range(EP):
                    sp = self.spread[:, ub, n, t * P:(t + 1) * P]
                    pe.matmul(o, sp, self.yhi[:, ub, n * C:(n + 1) * C], start=(n == 0), stop=False)
                    i = pe.matmul(o, sp, self.ylo[:, ub, n * C:(n + 1) * C], start=False, stop=(n == EP - 1))
            i.then_inc(self.scattered, 1)

        def step(g, gp):
            for e in range(E):
                if self.has_group(g):
                    up(g, gp, e)
                if e == 0 and self.has_group(g - 1):
                    down(g - 1, E - 1)
                if e and self.has_group(g):
                    down(g, e - 1)
                if self.has_group(g + 1):
                    gather(self.GB * (g + 1) + e // 2, (e // 2) % 2, 1 - gp, e % 2)
                if e % 2:
                    if self.has(self.back(g, e)):
                        turn(self.back(g, e), 1 - gp, (e - 1) // 2)
                    if self.has(self.late(g, e)):
                        scatter(self.late(g, e), ((e - 3) // 2) % 2)

        sh.start(pe, self.layer * B)
        pe.wait_ge(sh.consts, sh.N_CONSTS)
        pe.wait_ge(w.gate_in, 16)
        def first(b, u):
            if self.has(b + 1):
                self.turn_first(pe, b + 1, 1 - u)
            self.score(pe, b, u)

        if not self.ahead:
            self.turn_first(pe, self.o, 0)
            pipeline(pe, first, 0, B - 1, 2, B - 3, self.o)
        turn_choice()
        w.ready(pe)
        for q in range(self.GB):
            for t in range(TP):
                gather(self.o + q, q % 2, 0, t, self.first_banks[q % 2], 1 if q else 0)
        self.groups(pe, step)

    def scalar(self, act):
        GS = self.GS

        def gathered(q, gp, bb, banks=None):
            act.wait_ge(self.pick_used, TP * (q + 1))
            if bb == 0:
                need(act, self.w1_done, 4 * q - 16)
            hi, lo = banks or (self.pghi, self.pglo)
            act.activation(self.xin_hi[:, gp, bb, :], hi[:, :], ACT.Copy)
            act.activation(self.xin_lo[:, gp, bb, :], lo[:, :], ACT.Copy).then_inc(self.xin_done, 1)

        def gelu(g, e):
            n = E * g + e
            for c in range(2):
                act.wait_ge(self.w1_done, 2 * n + c + 1)
                need(act, self.hlo_done, 2 * n + c - 1)
                act.activation(self.h[:, c, :], self.ph[c][:, :], ACT.Gelu).then_inc(self.gelu_done, 1)

        def hhi(g, e):
            n = E * g + e
            need(act, self.w2_done, n - 1)
            for c in range(2):
                act.wait_ge(self.gelu_done, 2 * n + c + 1)
                o = self.hhi[:, e % 2, 2 * c:2 * c + 2, :].rearrange("p c s -> p (c s)")
                act.activation(o, self.h[:, c, :], ACT.Copy).then_inc(self.hhi_done, 1)

        def yev(g, gp, e):
            n = E * g + e
            act.wait_ge(self.w2_done, n + 1)
            if e == 0:
                need(act, self.ytr_done, self.GB * (g - 1))
            src = self.py[e % 2][:, 0:GS].rearrange("p (b j) -> p b j", b=self.GB)
            act.activation(self.yT[:, gp, :, e * CAP:(e + 1) * CAP], src, ACT.Copy).then_inc(self.yev_done, 1)

        def step(g, gp):
            for e in range(E):
                if self.has_group(g):
                    gelu(g, e)
                    hhi(g, e)
                if e == 0 and self.has_group(g - 1):
                    yev(g - 1, 1 - gp, E - 1)
                if e and self.has_group(g):
                    yev(g, gp, e - 1)
                if e % 2 and self.has_group(g + 1):
                    gathered(self.GB * (g + 1) + e // 2, 1 - gp, e // 2)

        self.sh.start(act, self.layer * B)
        if not self.ahead:
            pipeline(act, lambda b, u: self.first_xT(act, b, u), 0, B - 1, 2, B - 3, self.o)
        act.wait_ge(self.soft, 4 * self.run + 2)
        flat = lambda t: t[:, :, :, :].rearrange("p t b e -> p (t b e)")
        act.activation(flat(self.prob), flat(self.prob), ACT.Exp).then_inc(self.exp_done, 1)
        self.w.split.scalar_once(act)
        for q in range(self.GB):
            gathered(self.o + q, 0, q, self.first_banks[q % 2])
        self.groups(act, step)

    def vector(self, dve):
        sh, X = self.sh, self.sh.X

        def softmax():
            by = lambda t: t.rearrange("p (n e) -> p n e", e=E)
            prob = by(self.prob[:, :, :, :].rearrange("p t b e -> p (t b e)"))
            wide = lambda t: t[:, :].unsqueeze(2).to_broadcast([P, NT, E])
            dve.wait_ge(self.scored, self.o + B)
            dve.tensor_reduce(self.max[:, :], by(self.psc[:, :]), AX.X, ALU.max).then_inc(self.soft, 1)
            dve.wait_ge(self.soft, 4 * self.run + 1)
            dve.tensor_tensor(prob, by(self.psc[:, :]), wide(self.max), ALU.subtract).then_inc(self.soft, 1)
            dve.wait_ge(self.exp_done, self.run + 1)
            dve.tensor_reduce(self.sum[:, :], prob, AX.X, ALU.add).then_inc(self.soft, 1)
            dve.wait_ge(self.soft, 4 * self.run + 3)
            dve.reciprocal(self.max[:, :], self.sum[:, :]).then_inc(self.soft, 1)
            dve.wait_ge(self.soft, 4 * self.run + 4)
            dve.tensor_tensor(prob, prob, wide(self.max), ALU.mult).then_inc(self.prob_done, 1)

        def rank():
            rounds = CAP // 8
            k = [2 * (1 + 2 * rounds) * self.run]

            def link(ins):
                k[0] += 1
                ins.then_inc(self.rank_steps, 1)
                need(dve, self.rank_steps, k[0] - 1)

            dve.wait_ge(self.probT_ready, 2 * TP * (self.run + 1))
            for h in range(2):
                link(dve.tensor_copy(self.ranked[:, h, 0, :], self.pback[:, h * T:(h + 1) * T]))
            for r in range(rounds):
                eight = slice(8 * r, 8 * r + 8)
                for h in range(2):
                    link(dve.max(self.best[:, h, eight], self.ranked[:, h, r % 2, :]))
                for h in range(2):
                    now, later = self.ranked[:, h, r % 2, :], self.ranked[:, h, 1 - r % 2, :]
                    i = dve.max_index(self.best_at[:, h, eight], self.best[:, h, eight], now)
                    if r < rounds - 1:
                        i = dve.match_replace(later, self.best[:, h, eight], now, -1.0)
                    link(i)
            dve.wait_ge(self.rank_steps, k[0])
            for h in range(2):
                wide = lambda t: t[:, h, :].unsqueeze(1).to_broadcast([P, 2, CAP])
                dve.tensor_copy(self.best_atf[:, h, :], self.best_at[:, h, :])
                dve.tensor_copy(self.twice[:, h, 0, :, :], wide(self.best_at))
                dve.tensor_scalar(self.twice[:, h, 1, :, :], wide(self.best), 0.5, None, ALU.mult).then_inc(self.twice_done, 1)

        def slots(h):
            dve.wait_ge(self.slots_ready, 2 * (self.run + 1))
            for n, dst in enumerate((self.slot_token, self.slot_weight)):
                src = self.pxt[:, h * T + n * P:h * T + (n + 1) * P].rearrange("p (b n a) -> p b n a", n=EP, a=2)
                for a in range(2):
                    i = dve.tensor_copy(dst[a * CAP:(a + 1) * CAP, h * self.BH:(h + 1) * self.BH, :],
                                        src[a * CAP:(a + 1) * CAP, :, :, a])
            i.then_inc(self.slots_done, 1)

        def xlo(q, uq):
            dve.wait_ge(self.xhi_done, q + 1)
            dve.tensor_tensor(self.xlo[:, uq, :, :], self.norm.xn[:, uq, :, :], self.xhi[:, uq, :, :].bitcast(F32),
                              ALU.subtract).then_inc(self.xlo_done, 1)

        def pick(q, uq, t):
            if t == 0:
                dve.wait_ge(self.row_in[uq], 8 * (q - uq) + 16)
            need(dve, self.pick_used, TP * q + t - 1)
            dve.tensor_scalar(self.pick[:, t, :], self.token_row[:, uq, :], sh.iota_part[:, t:t + 1], None,
                              ALU.is_equal).then_inc(self.pick_done, 1)

        def hlo(g, e):
            n = E * g + e
            for c in range(2):
                dve.wait_ge(self.hhi_done, 2 * n + c + 1)
                k = slice(2 * c, 2 * c + 2)
                flat = lambda t: t[:, e % 2, k, :].rearrange("p c s -> p (c s)")
                dve.tensor_tensor(flat(self.hlo), self.h[:, c, :], flat(self.hhi).bitcast(F32),
                                  ALU.subtract).then_inc(self.hlo_done, 1)

        def weigh(b, ub):
            dve.wait_ge(self.ytr_done, b + 1)
            need(dve, self.ylo_done, b - 1)
            wide = self.slot_weight[:, bass.ds(b - self.o, 1), :].rearrange("p a n -> p (a n)").unsqueeze(2).to_broadcast([P, EP, C])
            by = lambda t: t.rearrange("p (n c) -> p n c", c=C)
            dve.tensor_tensor(by(self.yw[:, ub, :]), by(self.pback[:, :]), wide, ALU.mult).then_inc(self.yw_done, 1)

        def ylo(b, ub):
            dve.wait_ge(self.yhi_done, b + 1)
            dve.tensor_tensor(self.ylo[:, ub, :], self.yw[:, ub, :], self.yhi[:, ub, :].bitcast(F32),
                              ALU.subtract).then_inc(self.ylo_done, 1)

        def spread(b, ub):
            need(dve, self.scattered, b - 1)
            for n in range(EP):
                at = self.slot_token[:, bass.ds(b - self.o, 1), n]
                i = dve.tensor_scalar(self.spread[:, ub, n, :], sh.iota_tok[:, :], at, None, ALU.is_equal)
            i.then_inc(self.spread_done, 1)

        def update(b):
            dve.wait_ge(self.scattered, b + 1)
            x = X[:, bass.ds(TP * (b - self.o), TP), :]
            dve.tensor_tensor(x, x, self.psc[:, 0:TP * C].rearrange("p (t c) -> p t c", t=TP),
                              ALU.add).then_inc(sh.x_done, 1)

        def step(g, gp):
            for e in range(E):
                q = self.GB * (g + 1) + e // 2
                if self.has_group(g + 1):
                    if e % 2 == 0:
                        xlo(q, (e // 2) % 2)
                    pick(q, (e // 2) % 2, e % 2)
                if e % 2 == 0:
                    b = self.late(g, e + 1)
                    if self.has(b):
                        ub = ((e - 2) // 2) % 2
                        ylo(b, ub)
                    self.moments_next(dve, self.GB * (g - 1) + (e - 4) // 2, ((e - 4) // 2) % 2)
                if self.has_group(g):
                    hlo(g, e)
                if e % 2:
                    b = self.back(g, e)
                    if self.has(b):
                        weigh(b, ((e - 1) // 2) % 2)
                        spread(b, ((e - 1) // 2) % 2)
                    if self.has(self.late(g, e)):
                        update(self.late(g, e))

        sh.start(dve, self.layer * B)
        dve.wait_ge(sh.consts, sh.N_CONSTS)
        norm = lambda b, u: self.norm.vector(dve, b, u, lambda: apart(dve, self.xT_ready, b - 1, sh.passed))
        if self.layer and not self.ahead:
            pipeline(dve, norm, 0, B - 1, 2, B - 3, self.o)
        if not self.layer:
            sh.moments.moments_first(dve, lambda c: [norm(b, b % 2) for b in range(FB * c, FB * c + FB)])
        softmax()
        rank()
        for h in range(2):
            slots(h)
        for q in range(self.GB):
            xlo(self.o + q, q % 2)
            for t in range(TP):
                pick(self.o + q, q % 2, t)
        self.groups(dve, step)

    def gpsimd(self, pool):
        sh = self.sh

        def again(q, uq):
            apart(pool, self.xlo_done, q - 1, sh.passed)
            self.norm.spread(pool, q, uq, self.xa_centred, self.xa_done)
            apart(pool, self.pick_used, TP * (q - 1), sh.passed)
            apart(pool, self.xa_done, q + 1, sh.passed)
            pool.tensor_scalar(self.xhi[:, uq, :, :], self.norm.xn[:, uq, :, :], 1.0, 0.0, ALU.mult, ALU.add).then_inc(self.xhi_done, 1)

        def yhi(b, ub):
            apart(pool, self.scattered, b - 1, sh.passed)
            apart(pool, self.yw_done, b + 1, sh.passed)
            pool.tensor_scalar(self.yhi[:, ub, :], self.yw[:, ub, :], 1.0, 0.0, ALU.mult, ALU.add).then_inc(self.yhi_done, 1)

        def step(g, gp):
            for e in range(1, E, 2):
                q = self.GB * (g + 1) + e // 2 + 1
                if self.has(q) and self.has_group(g + 1):
                    again(q, (e // 2 + 1) % 2)
                b = self.back(g, e)
                if self.has(b):
                    yhi(b, ((e - 1) // 2) % 2)
                self.scale_next(pool, self.GB * (g - 1) + (e - 5) // 2, ((e - 5) // 2) % 2)

        sh.start(pool, self.layer * B)
        self.w.split.rest_once(pool)
        pool.wait_ge(self.xT_ready, self.o + B)
        for q in range(self.GB + 1):
            again(self.o + q, q % 2)
        self.groups(pool, step)

    def sync(self, sp):
        for h in range(2):
            sp.wait_ge(self.twice_done, 2 * self.run + h + 1)
            dst = self.token_dram[h * self.BH:(h + 1) * self.BH, :].rearrange("b (e j) -> (b e) j", e=E)
            sp.dma_start(dst, self.best_atf[:, h, :]).then_inc(self.tokens_stored, 16)
        sp.wait_ge(self.tokens_stored, 32 * (self.run + 1))

        def row(q, uq):
            need(sp, self.pick_done, TP * (q - 1))
            sp.dma_start(self.token_row[:, uq, :], self.token_dram[bass.ds(q - self.o, 1), :].to_broadcast([P, SLOTS])).then_inc(self.row_in[uq], 16)

        pipeline(sp, row, 0, B - 1, 2, B - 3, self.o)


class ChoiceWeights:
    def __init__(self, sh, mem):
        self.sh = sh
        self.w1_hi, self.w1_lo = (mem.take(f"ec_w1_{x}", [P, E, H0], F32R) for x in ("hi", "lo"))
        self.w2_hi, self.w2_lo = (mem.take(f"ec_w2_{x}", [P, E, HC, C], F32R) for x in ("hi", "lo"))
        self.gate = mem.take("ec_gate", [P, E])
        self.gate_in = sh.sem("ec_gate_in")
        self.split = None
        one = lambda t: t[:, :, :].rearrange("p e h -> p (e h)")
        two = lambda t: t[:, :, :, :].rearrange("p e k c -> p (e k c)")
        self.parts = [(one(self.w1_hi), one(self.w1_lo), "ec_w1"), (two(self.w2_hi), two(self.w2_lo), "ec_w2")]

    def sync(self, sp):
        sp.dma_start(self.gate[:, :], self.sh.args["ec_gate"]).then_inc(self.gate_in, 16)
        self.split.sync(sp)

    def ready(self, pe):
        self.split.ready(pe)


class Rwkv(Layer):

    COLS = ("decay", "mix_k", "mix_v", "mix_r", "ln_g", "ln_b")

    def __init__(self, sh, tag, mem):
        self.sh = sh
        self.norm = Normed(sh, tag, mem)
        f = lambda n, s, d=F32: mem.take(f"{tag}_{n}", s, d)
        self.cols = f("cols", [P, len(self.COLS)])
        self.rest = f("one_minus_mix", [P, 3])
        self.td = f("decay_exp", [P, 1])
        self.w = f("w", [P, 4, C])
        self.now = f("w_now", [P, 3, C])
        self.before = f("w_before", [P, 3, C])
        self.x1 = f("x1", [P, 2, T + 1])
        self.ek, self.er, self.er1, self.ekv, self.num, self.den, self.under, self.over, self.z = (
            f(n, [P, 2, T]) for n in ("ek", "er", "er1", "ekv", "num", "den", "under", "over", "z"))
        bk = sh.banks
        self.px, self.pkv, self.pr, self.po = bk[7], bk[0:2], bk[2:4], bk[4:6]
        self.next = None
        s = lambda n: sh.sem(f"{tag}_{n}")
        self.w_in, self.setup = s("w_in"), s("setup_steps")
        self.xT_ready, self.x1_done, self.kv_done, self.r_done = s("xT_ready"), s("x1_done"), s("kv_done"), s("r_done")
        self.ek_done, self.er_done, self.er1_done = s("ek_done"), s("er_done"), s("er1_done")
        self.ekv_done, self.scans_done, self.under_done, self.over_done = s("ekv_done"), s("scans_done"), s("under_done"), s("over_done")
        self.z_done, self.out_done = s("z_done"), s("out_done")

    SETUP = 1 + 2 + 6

    def steps(self, eng, step):
        pipeline(eng, step, 0, B + 4, 6, B - 3)

    def ahead_for_next(self, eng, part, b, u):
        if self.next is not None and inside(b):
            part(eng, self.next.o + b, u)

    def sync(self, sp):
        self.sh.start(sp, self.x0)
        sp.dma_start(self.cols[:, :], self.sh.args["rk_cols"]).then_inc(self.w_in, 16)
        sp.dma_start(self.w[:, :, :].rearrange("p a b -> p (a b)"), self.sh.args["rk_w"]).then_inc(self.w_in, 16)

    def tensor(self, pe):
        sh, ident = self.sh, self.sh.ident

        def turn(b, u):
            pe.wait_ge(self.norm.done, b + 1)
            need(pe, self.x1_done, b)
            if self.next is not None and inside(b - 6):
                pe.wait_ge(self.next.xT_done, self.next.o + b - 5)
            for t in range(TP):
                i = pe.transpose(self.px[:, t * P:(t + 1) * P], self.norm.xn[:, u, t, :], ident[:, :])
            i.then_inc(self.xT_ready, 1)

        def project(b, u):
            pe.wait_ge(self.x1_done, b + 1)
            need(pe, self.ekv_done, b - 1)
            need(pe, self.er_done, b - 1)
            for n, (o, done) in enumerate(((self.pkv[u][:, 0:T], None), (self.pkv[u][:, T:2 * T], self.kv_done),
                                           (self.pr[u][:, 0:T], self.r_done))):
                pe.matmul(o, self.now[:, n, :], self.x1[:, u, 1:T + 1], start=True, stop=False)
                i = pe.matmul(o, self.before[:, n, :], self.x1[:, u, 0:T], start=False, stop=True)
                if done is not None:
                    i.then_inc(done, 1)

        def out(b, u):
            pe.wait_ge(self.z_done, b + 1)
            need(pe, sh.x_done, self.x0 + b - 1)
            for t in range(TP):
                i = pe.matmul(self.po[u][:, t * C:(t + 1) * C], self.z[:, u, t * P:(t + 1) * P], self.w[:, 3, :],
                              start=True, stop=True)
            i.then_inc(self.out_done, 1)

        def step(s, u):
            if inside(s + 1):
                turn(s + 1, 1 - u)
            if inside(s):
                project(s, u)
            if inside(s - 1):
                out(s - 1, 1 - u)
            if self.next is not None:
                if inside(s + 1) and inside(s - 4):
                    pe.wait_ge(self.x1_done, s + 2)
                self.ahead_for_next(pe, self.next.turn_first, s - 4, u)
                self.ahead_for_next(pe, self.next.score, s - 5, 1 - u)

        sh.start(pe, self.x0)
        pe.wait_ge(sh.consts, sh.N_CONSTS)
        pe.wait_ge(self.setup, self.SETUP)
        turn(0, 0)
        self.steps(pe, step)

    def scalar(self, act):
        def x1(b, u):
            act.wait_ge(self.xT_ready, b + 1)
            need(act, self.r_done, b - 1)
            act.activation(self.x1[:, u, 1:T + 1], self.px[:, 0:T], ACT.Identity, scale=self.cols[:, 4:5],
                           bias=self.cols[:, 5:6]).then_inc(self.x1_done, 1)

        def exps(b, u):
            act.wait_ge(self.kv_done, b + 1)
            need(act, self.scans_done, b - 1)
            act.activation(self.ek[:, u, :], self.pkv[u][:, 0:T], ACT.Exp).then_inc(self.ek_done, 1)
            act.wait_ge(self.r_done, b + 1)
            need(act, self.er1_done, b - 1)
            act.activation(self.er[:, u, :], self.pr[u][:, 0:T], ACT.Exp, scale=-1.0).then_inc(self.er_done, 1)

        def step(s, u):
            if inside(s + 1):
                x1(s + 1, 1 - u)
            if inside(s):
                exps(s, u)
            if self.next is not None:
                self.ahead_for_next(act, self.next.first_xT, s - 4, u)

        self.sh.start(act, self.x0)
        act.wait_ge(self.w_in, 32)
        act.activation(self.td[:, :], self.cols[:, 0:1], ACT.Exp).then_inc(self.setup, 1)
        act.wait_ge(self.setup, self.SETUP)
        x1(0, 0)
        self.steps(act, step)

    def vector(self, dve):
        sh, X = self.sh, self.sh.X

        def mix(b, u):
            td = self.td[:, 0:1].to_broadcast([P, T])
            dve.wait_ge(self.ek_done, b + 1)
            dve.tensor_tensor(self.ekv[:, u, :], self.pkv[u][:, T:2 * T], self.ek[:, u, :], ALU.mult).then_inc(self.ekv_done, 1)
            dve.tensor_tensor_scan(self.den[:, u, :], td, self.ek[:, u, :], 0.0, ALU.mult, ALU.add)
            dve.wait_ge(self.ekv_done, b + 1)
            dve.tensor_tensor_scan(self.num[:, u, :], td, self.ekv[:, u, :], 0.0, ALU.mult, ALU.add).then_inc(self.scans_done, 1)
            dve.wait_ge(self.scans_done, b + 1)
            dve.wait_ge(self.er1_done, b + 1)
            dve.scalar_tensor_tensor(out=self.under[:, u, :], in0=self.den[:, u, :], scalar=1e-8, in1=self.er1[:, u, :],
                                     op0=ALU.add, op1=ALU.mult).then_inc(self.under_done, 1)
            dve.wait_ge(self.under_done, b + 1)
            dve.reciprocal(self.over[:, u, :], self.under[:, u, :]).then_inc(self.over_done, 1)
            dve.wait_ge(self.over_done, b + 1)
            need(dve, self.out_done, b - 1)
            dve.tensor_tensor(self.z[:, u, :], self.num[:, u, :], self.over[:, u, :], ALU.mult).then_inc(self.z_done, 1)

        def update(b, u):
            dve.wait_ge(self.out_done, b + 1)
            x = X[:, bass.ds(TP * b, TP), :]
            dve.tensor_tensor(x, x, self.po[u][:, 0:TP * C].rearrange("p (t c) -> p t c", t=TP), ALU.add).then_inc(sh.x_done, 1)

        def step(s, u):
            self.moments_next(dve, s - 2, u)
            if inside(s):
                mix(s, u)
            if inside(s - 1):
                update(s - 1, 1 - u)

        sh.start(dve, self.x0)
        dve.wait_ge(self.w_in, 32)
        for u in range(2):
            i = dve.memset(self.x1[:, u, 0:1], 0.0)
        i.then_inc(self.setup, 1)
        dve.tensor_scalar(self.rest[:, :], self.cols[:, 1:4], -1.0, 1.0, ALU.mult, ALU.add).then_inc(self.setup, 1)
        dve.wait_ge(self.setup, 3)
        for n in range(3):
            dve.tensor_scalar(self.now[:, n, :], self.w[:, n, :], self.cols[:, 1 + n:2 + n], None, ALU.mult).then_inc(self.setup, 1)
            dve.tensor_scalar(self.before[:, n, :], self.w[:, n, :], self.rest[:, n:n + 1], None, ALU.mult).then_inc(self.setup, 1)
        self.steps(dve, step)

    def gpsimd(self, pool):
        def er1(b, u):
            apart(pool, self.under_done, b - 1, self.sh.passed)
            apart(pool, self.er_done, b + 1, self.sh.passed)
            pool.tensor_scalar(self.er1[:, u, :], self.er[:, u, :], 1.0, 1.0, ALU.mult, ALU.add).then_inc(self.er1_done, 1)

        def norm(b, u):
            self.norm.gpsimd(pool, b, u, lambda: apart(pool, self.xT_ready, b - 1, self.sh.passed))

        def step(s, u):
            if inside(s + 2):
                norm(s + 2, u)
            if inside(s):
                er1(s, u)
            self.scale_next(pool, s - 2, u)
            if self.next is not None:
                self.ahead_for_next(pool, self.next.first_norm, s - 3, 1 - u)

        self.sh.start(pool, self.x0)
        norm(0, 0)
        norm(1, 1)
        self.steps(pool, step)


class Mlstm(Layer):

    TRI = T + P
    SERIES = 8

    def __init__(self, sh, tag, mem):
        self.sh = sh
        self.norm = Normed(sh, tag, mem)
        f = lambda n, s, d=F32: mem.take(f"{tag}_{n}", s, d)
        self.wq, self.wk, self.wd0, self.wd = f("wq", [P, C]), f("wk", [P, C]), f("wdown_in", [P, C]), f("wdown", [P, C])
        self.wvo = f("wvo", [P, 2 * C])
        self.wgate = f("wgate", [P, 2 * NH])
        self.bias = f("gate_bias", [P, 2 * NH])
        self.nw = f("norm_w", [P, 1])
        self.mask = f("mask", [P, P])
        self.ones = f("ones", [P, 1])
        self.xT = f("xT", [P, 2, T])
        self.aT = f("aT", [P, TP, B * NH])
        self.emT = f("emT", [P, TP, B * NH])
        at = mem.at
        g = lambda n, s, d=F32: mem.take(f"{tag}_g_{n}", s, d)
        self.raw = g("raw", [P, NT, 2 * NH])
        self.cap = g("capped", [P, NT, 2 * NH])
        self.g_ig, self.g_fg, self.g_abs, self.g_e, self.g_s, self.g_s2, self.g_acc, self.g_acc2, self.g_lf, self.g_neg = (
            g(n, [P, TP, B * NH]) for n in ("ig", "fg", "abs", "e", "s", "s2", "acc", "acc2", "lf", "neg"))
        self.r_cum, self.r_a, self.r_run, self.r_negrun, self.r_m, self.r_em = (
            g("row_" + n, [P, T]) for n in ("cum", "a", "run", "negrun", "m", "em"))
        end = mem.at
        mem.at = at
        self.run_row = f("run_row", [P, 2, NH, T])
        self.qs = f("q", [P, 2, T])
        self.ks = f("k", [P, 2, NH, T])
        self.vx = f("v", [P, 2, TP, NH, DH + 1])
        self.th = f("o_tanh", [P, 2, TP, C])
        self.logd = f("log_decay", [P, 2, NH, self.TRI])
        self.ct = f("weights", [P, 2, NH, self.TRI])
        self.av = f("av", [P, 2, TP * NH, DH + 1])
        self.n8 = f("n8", [P, 2, 6, TP * NH])
        self.hv, self.d, self.sq, self.hn, self.hg = (f(n, [P, 2, TP, C]) for n in ("hv", "d", "sq", "hn", "hg"))
        self.hT = f("hT", [P, 2, T])
        mem.at = max(end, mem.at)
        bk = sh.banks
        self.ps, self.pq, self.pvo, self.pav, self.pm = bk[0:4], bk[4], bk[5], bk[6], bk[7]
        s = lambda n: sh.sem(f"{tag}_{n}")
        self.w_in, self.setup = s("w_in"), s("setup_steps")
        self.xT_ready, self.xT_done, self.scored = s("xT_ready"), s("xT_done"), s("scored")
        self.gates, self.tanh_done, self.gexp_done = s("gate_steps"), s("tanh_done"), s("gexp_done")
        self.rows_ready, self.rows, self.em_done = s("rows_ready"), s("row_steps"), s("em_done")
        self.run_stored, self.cols_ready, self.cols_done = s("run_stored"), s("cols_ready"), s("cols_done")
        self.row_in = [s("run_row_in0"), s("run_row_in1")]
        self.xa_centred, self.xa_done, self.yT_ready, self.yT_done = s("xa_centred"), s("xa_done"), s("x2T_ready"), s("x2T_done")
        self.qk_ready, self.vo_ready, self.qk_done, self.vo_done = s("qk_ready"), s("vo_ready"), s("qk_done"), s("vo_done")
        self.s_done, self.logd_done, self.d_done, self.ct_done = s("s_done"), s("logd_done"), s("d_done"), s("ct_done")
        self.av_done, self.avc_done = s("av_done"), s("avc_done")
        self.head = Chain(s("head_steps"), 5)
        self.hsum, self.mean_done, self.mask_set = s("head_sum_done"), s("head_mean_done"), s("mask_set")
        self.cen_done, self.sq_done, self.var_done = s("cen_done"), s("sq_done"), s("var_done")
        self.rstd = Chain(s("head_rstd_steps"), 2)
        self.hn_done, self.hg_done, self.hT_ready, self.hT_done, self.out_done = (
            s("hn_done"), s("hg_done"), s("hT_ready"), s("hT_done"), s("out_done"))
        self.run_dram = sh.nc.dram_tensor(f"{tag}_run", [B, NH * T], F32).ap()

    def steps(self, eng, step):
        pipeline(eng, step, 0, B + 1, 4, B - 3)

    LOADS = ("ml_wq", "ml_wk", "ml_wvo", "ml_wdown", "ml_wgate", "ml_norm_w")

    def sync(self, sp):
        a = self.sh.args
        self.sh.start(sp, self.x0)
        for dst, n in zip((self.wq, self.wk, self.wvo, self.wd0, self.wgate, self.nw), self.LOADS):
            sp.dma_start(dst[:, :], a[n]).then_inc(self.w_in, 16)
        sp.dma_start(self.bias[:, :], a["ml_bias"].to_broadcast([P, 2 * NH])).then_inc(self.w_in, 16)
        sp.wait_ge(self.rows, 4)
        dst = self.run_dram.rearrange("b (h t) -> (b h) t", h=NH)
        sp.dma_start(dst, self.r_negrun[:, :]).then_inc(self.run_stored, 16)
        sp.wait_ge(self.run_stored, 16)
        sp.wait_ge(self.cols_done, 1)

        def row(b, u):
            need(sp, self.d_done, b - 1)
            dst = self.run_row[:, u, :, :].rearrange("p h t -> p (h t)")
            sp.dma_start(dst, self.run_dram[bass.ds(b, 1), :].to_broadcast([P, NH * T])).then_inc(self.row_in[u], 16)

        pipeline(sp, row, 0, B - 1, 2, B - 3)

    def tensor(self, pe):
        sh, ident = self.sh, self.sh.ident

        def turn_first(b, u):
            pe.wait_ge(self.norm.done, b + 1)
            need(pe, self.xT_done, b - 1)
            for t in range(TP):
                i = pe.transpose(self.ps[u][:, t * P:(t + 1) * P], self.norm.xn[:, u, t, :], ident[:, :])
            i.then_inc(self.xT_ready, 1)

        def score(b, u):
            if inside(b + 1):
                turn_first(b + 1, 1 - u)
            pe.wait_ge(self.xT_done, b + 1)
            for t in range(TP):
                o = self.pq[:, bass.ds(t * B * 2 * NH + b * 2 * NH, 2 * NH)]
                i = pe.matmul(o, self.xT[:, u, t * P:(t + 1) * P], self.wgate[:, :], start=True, stop=True)
            i.then_inc(self.scored, 1)

        def turn_gates():
            pe.wait_ge(self.gates, self.GATE_STEPS)
            for n, src in enumerate((self.g_lf, self.g_ig)):
                for t in range(TP):
                    i = pe.transpose(self.pvo[:, (TP * n + t) * P:(TP * n + t + 1) * P], src[:, t, :], ident[:, :])
            i.then_inc(self.rows_ready, 1)
            pe.wait_ge(self.rows, 3)
            pe.wait_ge(self.em_done, 1)
            for n, src in enumerate((self.r_a, self.r_em)):
                for t in range(TP):
                    i = pe.transpose(self.pav[:, (TP * n + t) * P:(TP * n + t + 1) * P], src[:, t * P:(t + 1) * P], ident[:, :])
            i.then_inc(self.cols_ready, 1)

        def turn(b, u):
            pe.wait_ge(self.xa_done, b + 1)
            need(pe, sh.x_done, self.x0 + b - 3)
            for t in range(TP):
                i = pe.transpose(self.pm[:, t * P:(t + 1) * P], self.norm.xn[:, u, t, :], ident[:, :])
            i.then_inc(self.yT_ready, 1)

        def project_qk(b, u):
            pe.wait_ge(self.yT_done, b + 1)
            need(pe, self.qk_done, b)
            pe.matmul(self.pq[:, 0:T], self.wq[:, :], self.xT[:, u, :], start=True, stop=True)
            pe.matmul(self.pq[:, T:2 * T], self.wk[:, :], self.xT[:, u, :], start=True, stop=True).then_inc(self.qk_ready, 1)

        def project_vo(b, u, t):
            need(pe, self.vo_done, b)
            i = pe.matmul(self.pvo[:, t * 2 * C:(t + 1) * 2 * C], self.xT[:, u, t * P:(t + 1) * P], self.wvo[:, :],
                          start=True, stop=True)
            if t == TP - 1:
                i.then_inc(self.vo_ready, 1)

        def scores(b, u):
            pe.wait_ge(self.qk_done, b + 1)
            for h in range(NH):
                need(pe, self.ct_done, NH * (b - 1) + h + 1)
                pe.matmul(self.ps[h][:, 0:T], self.ks[:, u, h, 0:P], self.qs[:, u, :], start=True, stop=True)
                pe.matmul(self.ps[h][:, T:T + P], self.ks[:, u, h, P:T], self.qs[:, u, P:T], start=True,
                          stop=True).then_inc(self.s_done, 1)

        def attend(b, u, h):
            if h == 0:
                need(pe, self.avc_done, b)
                pe.wait_ge(self.vo_done, b + 1)
            pe.wait_ge(self.ct_done, NH * b + h + 1)
            o = [self.pav[:, (t * NH + h) * (DH + 1):(t * NH + h + 1) * (DH + 1)] for t in range(TP)]
            c = self.ct[:, u, h, :]
            pe.matmul(o[0], c[:, 0:P], self.vx[:, u, 0, h, :], start=True, stop=True)
            pe.matmul(o[1], c[:, P:T], self.vx[:, u, 0, h, :], start=True, stop=False)
            i = pe.matmul(o[1], c[:, T:T + P], self.vx[:, u, 1, h, :], start=False, stop=True)
            if h == NH - 1:
                i.then_inc(self.av_done, 1)

        def turn_back(b, u, newest):
            pe.wait_ge(self.hg_done, b + 1)
            need(pe, self.yT_done, newest)
            need(pe, sh.x_done, self.x0 + b)
            for t in range(TP):
                i = pe.transpose(self.pm[:, t * P:(t + 1) * P], self.hg[:, u, t, :], ident[:, :])
            i.then_inc(self.hT_ready, 1)

        def out(b, u):
            pe.wait_ge(self.hT_done, b + 1)
            for t in range(TP):
                i = pe.matmul(self.pm[:, t * C:(t + 1) * C], self.hT[:, u, t * P:(t + 1) * P], self.wd[:, :],
                              start=True, stop=True)
            i.then_inc(self.out_done, 1)

        def step(s, u):
            if inside(s + 1):
                turn(s + 1, 1 - u)
            if inside(s):
                scores(s, u)
            if inside(s - 2):
                turn_back(s - 2, u, s + 2 if inside(s + 1) else B)
            if inside(s + 1):
                project_qk(s + 1, 1 - u)
            if inside(s - 2):
                out(s - 2, u)
            for h in range(NH):
                if inside(s):
                    attend(s, u, h)
                if h < TP and inside(s + 1):
                    project_vo(s + 1, 1 - u, h)

        sh.start(pe, self.x0)
        pe.wait_ge(sh.consts, sh.N_CONSTS)
        pe.wait_ge(self.setup, 2)
        turn_first(0, 0)
        pipeline(pe, score, 0, B - 1, 2, B - 3)
        turn_gates()
        pe.wait_ge(self.cols_done, 1)
        turn(0, 0)
        project_qk(0, 0)
        for t in range(TP):
            project_vo(0, 0, t)
        self.steps(pe, step)

    def scalar(self, act):
        def xT(b, u):
            act.wait_ge(self.xT_ready, b + 1)
            need(act, self.scored, b - 1)
            act.activation(self.xT[:, u, :], self.ps[u][:, 0:T], ACT.Copy).then_inc(self.xT_done, 1)

        def x2T(b, u):
            act.wait_ge(self.yT_ready, b + 1)
            need(act, self.vo_ready, b - 1)
            act.activation(self.xT[:, u, :], self.pm[:, 0:T], ACT.Copy).then_inc(self.yT_done, 1)

        def qk(b, u):
            act.wait_ge(self.qk_ready, b + 1)
            need(act, self.s_done, NH * (b - 1))
            act.activation(self.qs[:, u, :], self.pq[:, 0:T], ACT.Copy, scale=float(DH) ** -0.5)
            for h in range(NH):
                k = slice(DH * h, DH * h + DH)
                i = act.activation(self.ks[k, u, h, :], self.pq[k, T:2 * T], ACT.Copy)
            i.then_inc(self.qk_done, 1)

        def vo(b, u):
            act.wait_ge(self.vo_ready, b + 1)
            need(act, self.av_done, b - 1)
            need(act, self.hg_done, b - 1)
            src = self.pvo[:, :].rearrange("p (t n) -> p t n", t=TP)
            act.activation(self.vx[:, u, :, :, 0:DH], src[:, :, 0:C].rearrange("p t (h d) -> p t h d", h=NH), ACT.Copy)
            act.activation(self.th[:, u, :, :], src[:, :, C:2 * C], ACT.Tanh, scale=0.5).then_inc(self.vo_done, 1)

        def decay_later(b, u):
            act.wait_ge(self.row_in[u], 8 * (b - u) + 16)
            need(act, self.ct_done, NH * (b - 1))
            for h in range(NH):
                act.activation(self.logd[:, u, h, P:T], self.run_row[:, u, h, P:T], ACT.Exp,
                               bias=self.aT[:, 0, bass.ds(NH * b + h, 1)])

        def decay(b, u):
            act.wait_ge(self.logd_done, b + 1)
            d = self.logd[:, u, :, :].rearrange("p h (c n) -> p h c n", n=P)[:, :, 0:3:2, :]
            act.activation(d, d, ACT.Exp).then_inc(self.d_done, 1)

        def avc(b, u):
            act.wait_ge(self.av_done, b + 1)
            need(act, self.head.sem, 5 * (b - 1))
            n = TP * NH * (DH + 1)
            act.activation(self.av[:, u, :, :].rearrange("p a d -> p (a d)"), self.pav[:, 0:n], ACT.Copy).then_inc(self.avc_done, 1)

        def square(b, u):
            act.wait_ge(self.cen_done, b + 1)
            need(act, self.var_done, b - 1)
            act.activation(self.sq[:, u, :, :], self.d[:, u, :, :], ACT.Square).then_inc(self.sq_done, 1)

        def hT(b, u):
            act.wait_ge(self.hT_ready, b + 1)
            need(act, self.out_done, b - 1)
            act.activation(self.hT[:, u, :], self.pm[:, 0:T], ACT.Copy).then_inc(self.hT_done, 1)

        def step(s, u):
            if inside(s + 1):
                x2T(s + 1, 1 - u)
            if inside(s):
                decay(s, u)
            if inside(s - 2):
                hT(s - 2, u)
            if inside(s - 1):
                square(s - 1, 1 - u)
            if inside(s + 1):
                decay_later(s + 1, 1 - u)
            if inside(s + 1):
                qk(s + 1, 1 - u)
            if inside(s + 1):
                vo(s + 1, 1 - u)
            if inside(s):
                avc(s, u)

        self.sh.start(act, self.x0)
        pipeline(act, xT, 0, B - 1, 2, B - 3)
        act.wait_ge(self.gates, 1)
        act.activation(self.cap[:, :, :], self.raw[:, :, :], ACT.Tanh, scale=1.0 / CAPG).then_inc(self.tanh_done, 1)
        act.wait_ge(self.gates, 4)
        act.activation(self.g_e[:, :, :], self.g_abs[:, :, :], ACT.Exp, scale=-1.0).then_inc(self.gexp_done, 1)
        act.wait_ge(self.rows, 5)
        act.activation(self.r_em[:, :], self.r_m[:, :], ACT.Exp, scale=-1.0).then_inc(self.em_done, 1)
        act.wait_ge(self.cols_done, 1)
        x2T(0, 0)
        qk(0, 0)
        vo(0, 0)
        decay_later(0, 0)
        self.steps(act, step)

    GATE_STEPS = 1 + 3 + 4 + SERIES + 1 + 1

    def vector(self, dve):
        sh, X = self.sh, self.sh.X

        def gate_math():
            k = [0]

            def link(ins):
                k[0] += 1
                ins.then_inc(self.gates, 1)
                dve.wait_ge(self.gates, k[0])

            dve.wait_ge(self.scored, B)
            wide = self.bias[:, :].unsqueeze(1).to_broadcast([P, NT, 2 * NH])
            link(dve.tensor_tensor(self.raw[:, :, :], self.pq[:, :].rearrange("p (n g) -> p n g", g=2 * NH), wide, ALU.add))
            dve.wait_ge(self.tanh_done, 1)
            by = lambda t: t[:, :, :].rearrange("p t (b h) -> p (t b) h", h=NH)
            link(dve.tensor_scalar(by(self.g_ig), self.cap[:, :, 0:NH], CAPG, None, ALU.mult))
            link(dve.tensor_scalar(by(self.g_fg), self.cap[:, :, NH:2 * NH], CAPG, None, ALU.mult))
            flat = lambda t: t[:, :, :].rearrange("p t n -> p (t n)")
            fg, e, s, s2, acc, acc2 = (flat(t) for t in (self.g_fg, self.g_e, self.g_s, self.g_s2, self.g_acc, self.g_acc2))
            link(dve.scalar_tensor_tensor(out=flat(self.g_abs), in0=fg, scalar=-1.0, in1=fg, op0=ALU.mult, op1=ALU.max))
            dve.wait_ge(self.gexp_done, 1)
            dve.tensor_scalar(flat(self.g_neg), fg, 0.0, None, ALU.min)
            link(dve.tensor_scalar(acc, e, 2.0, None, ALU.add))
            link(dve.reciprocal(acc2, acc))
            link(dve.tensor_tensor(s, e, acc2, ALU.mult))
            link(dve.tensor_tensor(s2, s, s, ALU.mult))
            n = self.SERIES
            a, b = acc, acc2
            link(dve.tensor_scalar(a, s2, 1.0 / (2 * n + 1), None, ALU.mult))
            for j in range(n - 1, 0, -1):
                link(dve.scalar_tensor_tensor(out=b, in0=a, scalar=1.0 / (2 * j + 1), in1=s2, op0=ALU.add, op1=ALU.mult))
                a, b = b, a
            link(dve.scalar_tensor_tensor(out=b, in0=a, scalar=1.0, in1=s, op0=ALU.add, op1=ALU.mult))
            link(dve.scalar_tensor_tensor(out=flat(self.g_lf), in0=b, scalar=-2.0, in1=flat(self.g_neg), op0=ALU.mult, op1=ALU.add))
            assert k[0] == self.GATE_STEPS, k

        def row_math():
            k = [0]

            def link(ins):
                k[0] += 1
                ins.then_inc(self.rows, 1)
                dve.wait_ge(self.rows, k[0])

            dve.wait_ge(self.rows_ready, 1)
            ones = self.ones[:, 0:1].to_broadcast([P, T])
            link(dve.tensor_tensor_scan(self.r_cum[:, :], ones, self.pvo[:, 0:T], 0.0, ALU.mult, ALU.add))
            link(dve.tensor_tensor(self.r_a[:, :], self.pvo[:, T:2 * T], self.r_cum[:, :], ALU.subtract))
            link(dve.tensor_tensor_scan(self.r_run[:, :], self.r_a[:, :], self.r_a[:, :], -3.0e38, ALU.max, ALU.max))
            link(dve.tensor_scalar(self.r_negrun[:, :], self.r_run[:, :], -1.0, None, ALU.mult))
            link(dve.tensor_tensor(self.r_m[:, :], self.r_cum[:, :], self.r_run[:, :], ALU.add))
            dve.wait_ge(self.cols_ready, 1)
            flat = lambda t: t[:, :, :].rearrange("p t n -> p (t n)")
            dve.tensor_copy(flat(self.aT), self.pav[:, 0:T])
            dve.tensor_copy(flat(self.emT), self.pav[:, T:2 * T])
            dve.wait_ge(self.run_stored, 16)
            dve.memset(self.ks[:, :, :, :], 0.0)
            dve.memset(self.vx[:, :, :, :, DH:DH + 1], 1.0).then_inc(self.cols_done, 1)

        def log_decay(b, u):
            dve.wait_ge(self.row_in[u], 8 * (b - u) + 16)
            need(dve, self.ct_done, NH * (b - 1))
            for h in range(NH):
                for t in range(TP):
                    a = self.aT[:, t, bass.ds(NH * b + h, 1)]
                    i = dve.scalar_tensor_tensor(out=self.logd[:, u, h, t * T:t * T + P],
                                                 in0=self.run_row[:, u, h, t * P:(t + 1) * P], scalar=a,
                                                 in1=self.mask[:, :], op0=ALU.add, op1=ALU.min)
            i.then_inc(self.logd_done, 1)

        def weights(b, u):
            dve.wait_ge(self.d_done, b + 1)
            need(dve, self.av_done, b - 1)
            for h in range(NH):
                dve.wait_ge(self.s_done, NH * b + h + 1)
                dve.tensor_tensor(self.ct[:, u, h, :], self.ps[h][:, 0:self.TRI], self.logd[:, u, h, :],
                                  ALU.mult).then_inc(self.ct_done, 1)

        def heads(b, u):
            ch, n8 = self.head, self.n8
            ch.begin(b)
            dve.wait_ge(self.avc_done, b + 1)
            total = self.av[:, u, :, DH]
            wide = lambda t: t.unsqueeze(2).to_broadcast([P, TP * NH, DH])
            by = lambda t: t[:, u, :, :].rearrange("p t (h d) -> p (t h) d", d=DH)
            ch.link(dve, dve.scalar_tensor_tensor(out=n8[:, u, 0, :], in0=total, scalar=-1.0, in1=total, op0=ALU.mult, op1=ALU.max))
            em = self.emT[:, :, bass.ds(NH * b, NH)]
            two = lambda t: t.rearrange("p (t h) -> p t h", t=TP)
            ch.link(dve, dve.tensor_tensor(two(n8[:, u, 1, :]), two(n8[:, u, 0, :]), em, ALU.max))
            ch.link(dve, dve.tensor_scalar(n8[:, u, 0, :], n8[:, u, 1, :], EPS_HEAD, None, ALU.add))
            ch.link(dve, dve.reciprocal(n8[:, u, 1, :], n8[:, u, 0, :]))
            need(dve, self.cen_done, b - 1)
            ch.link(dve, dve.tensor_tensor(by(self.hv), self.av[:, u, :, 0:DH], wide(n8[:, u, 1, :]), ALU.mult))
            ch.end()
            dve.tensor_reduce(n8[:, u, 2, :], by(self.hv), AX.X, ALU.add).then_inc(self.hsum, 1)

        def variance(b, u):
            dve.wait_ge(self.sq_done, b + 1)
            dve.tensor_reduce(self.n8[:, u, 3, :], self.sq[:, u, :, :].rearrange("p t (h d) -> p (t h) d", d=DH),
                              AX.X, ALU.add).then_inc(self.var_done, 1)

        def gate_out(b, u):
            dve.wait_ge(self.hn_done, b + 1)
            need(dve, self.hT_ready, b - 1)
            flat = lambda t: t[:, u, :, :].rearrange("p t c -> p (t c)")
            dve.scalar_tensor_tensor(out=flat(self.hg), in0=flat(self.th), scalar=1.0, in1=flat(self.hn), op0=ALU.add,
                                     op1=ALU.mult).then_inc(self.hg_done, 1)

        def update(b):
            dve.wait_ge(self.out_done, b + 1)
            x = X[:, bass.ds(TP * b, TP), :]
            dve.tensor_tensor(x, x, self.pm[:, 0:TP * C].rearrange("p (t c) -> p t c", t=TP), ALU.add).then_inc(sh.x_done, 1)

        def step(s, u):
            if inside(s - 1):
                heads(s - 1, 1 - u)
            if inside(s):
                weights(s, u)
            if inside(s - 1):
                variance(s - 1, 1 - u)
            if inside(s + 1):
                log_decay(s + 1, 1 - u)
            self.moments_next(dve, s - 3, 1 - u)
            if inside(s - 2):
                update(s - 2)
            if inside(s - 1):
                gate_out(s - 1, 1 - u)

        sh.start(dve, self.x0)
        dve.wait_ge(sh.consts, sh.N_CONSTS)
        dve.wait_ge(self.w_in, 16 * (len(self.LOADS) + 1))
        dve.memset(self.ones[:, :], 1.0)
        dve.tensor_scalar(self.wd[:, :], self.wd0[:, :], self.nw[:, 0:1], 0.5, ALU.mult, ALU.mult).then_inc(self.setup, 1)
        pipeline(dve, lambda b, u: self.norm.vector(dve, b, u, lambda: apart(dve, self.xT_ready, b - 1, sh.passed)), 0, B - 1, 2, B - 3)
        gate_math()
        row_math()
        log_decay(0, 0)
        self.steps(dve, step)
        self.moments_next(dve, B - 1, 1)

    def gpsimd(self, pool):
        sh = self.sh

        def again(b, u):
            apart(pool, self.yT_ready, b - 1, sh.passed)
            self.norm.spread(pool, b, u, self.xa_centred, self.xa_done)

        by = lambda t, u: t[:, u, :, :].rearrange("p t (h d) -> p (t h) d", d=DH)
        wide = lambda t: t.unsqueeze(2).to_broadcast([P, TP * NH, DH])

        def centre(b, u):
            n8 = self.n8
            apart(pool, self.hsum, b + 1, sh.passed)
            apart(pool, self.hn_done, b - 1, sh.passed)
            pool.tensor_scalar(n8[:, u, 4, :], n8[:, u, 2, :], -1.0 / DH, 0.0, ALU.mult, ALU.add).then_inc(self.mean_done, 1)
            pool.wait_ge(self.mean_done, b + 1)
            pool.tensor_tensor(by(self.d, u), by(self.hv, u), wide(n8[:, u, 4, :]), ALU.add).then_inc(self.cen_done, 1)

        def scale(b, u):
            n8, ch = self.n8, self.rstd
            ch.begin(b)
            apart(pool, self.var_done, b + 1, sh.passed)
            ch.link(pool, pool.tensor_scalar(n8[:, u, 4, :], n8[:, u, 3, :], 1.0 / DH, EPS_HEAD, ALU.mult, ALU.add))
            ch.link(pool, pool.tensor_tensor(n8[:, u, 5, :], n8[:, u, 4, :], sh.mhalf[:, 0:TP * NH], ALU.pow))
            ch.end()
            need(pool, self.hg_done, b - 1)
            pool.tensor_tensor(by(self.hn, u), by(self.d, u), wide(n8[:, u, 5, :]), ALU.mult).then_inc(self.hn_done, 1)

        def step(s, u):
            if inside(s - 1):
                centre(s - 1, 1 - u)
            if inside(s + 2):
                again(s + 2, u)
            if inside(s - 1):
                scale(s - 1, 1 - u)
            self.scale_next(pool, s - 3, 1 - u)

        sh.start(pool, self.x0)
        pool.memset(self.mask[:, :], 0.0).then_inc(self.mask_set, 1)
        pool.wait_ge(self.mask_set, 1)
        pool.affine_select(out=self.mask[:, :], in_=self.mask[:, :], compare_op=ALU.is_ge, fill=-BIG, base=0,
                           pattern=[[1, P]], channel_multiplier=-1).then_inc(self.setup, 1)
        pool.wait_ge(self.xT_ready, B)
        again(0, 0)
        again(1, 1)
        self.steps(pool, step)
        self.scale_next(pool, B - 1, 1)


class Split:

    def __init__(self, sh, tag, parts, stage_mem, after):
        self.sh, self.parts, self.after = sh, parts, after
        self.loaded, self.hi, self.lo = (sh.sem(f"{tag}_{n}") for n in ("loaded", "hi_done", "lo_done"))
        self.told = set()
        self.stage = [stage_mem.take(f"{tag}_stage{n}", [P, p[0].shape[1]]) for n, p in enumerate(parts)]

    def sync(self, sp):
        need(sp, self.sh.x_done, self.after)
        for (_, _, name), st in zip(self.parts, self.stage):
            sp.dma_start(st[:, :], self.sh.args[name]).then_inc(self.loaded, 16)

    def scalar(self, act):
        act.wait_ge(self.loaded, 16 * len(self.parts))
        for (hi, _, _), st in zip(self.parts, self.stage):
            act.activation(hi, st[:, :], ACT.Copy).then_inc(self.hi, 1)

    def rest(self, eng):
        for n, ((hi, lo, _), st) in enumerate(zip(self.parts, self.stage)):
            eng.wait_ge(self.hi, n + 1)
            eng.tensor_tensor(lo, st[:, :], hi.bitcast(F32), ALU.subtract).then_inc(self.lo, 1)

    def once(self, eng, part):
        if part not in self.told:
            self.told.add(part)
            part(eng)

    def sync_once(self, sp):
        self.once(sp, self.sync)

    def scalar_once(self, act):
        self.once(act, self.scalar)

    def rest_once(self, eng):
        self.once(eng, self.rest)

    def ready(self, eng):
        eng.wait_ge(self.lo, len(self.parts))


def build(nc, args, out):
    with ExitStack() as ctx:
        sh = Shared(nc, ctx, args)
        mem = sh.mem
        base = mem.at
        layers = []
        first = {}
        choice_w = ChoiceWeights(sh, mem) if "choice" in LAYERS else None
        above = mem.at
        for n, kind in enumerate(LAYERS):
            if kind in first:
                layers.append((first[kind], n, 1))
                continue
            if kind == "choice":
                mem.at = above
                layer = Choice(sh, "choice", choice_w, mem)
                mem.at = layer.big
                choice_w.split = Split(sh, "ec", choice_w.parts, mem, 0)
            elif kind == "top2":
                mem.at = base
                w = Top2Weights(sh, mem)
                above_top2 = mem.at
                layer = Top2(sh, "top2", w, mem)
                mem.at = layer.big
                w.split = Split(sh, "t2", w.parts, mem, n * B)
            elif kind == "rwkv":
                mem.at = first["choice"].first_end if "choice" in first else above
                layer = Rwkv(sh, "rwkv", mem)
            elif kind == "mlstm":
                mem.at = above_top2 if "top2" in LAYERS else base
                layer = Mlstm(sh, "mlstm", mem)
            first[kind] = layer
            layers.append((layer, n, 0))

        def stand(n):
            layer, place, run = layers[n]
            if LAYERS[n] == "rwkv" and n + 1 < len(layers) and LAYERS[n + 1] == "choice":
                layer.next = layers[n + 1][0]
                layer.next.stand(*layers[n + 1][1:])
            layer.stand(place, run)
            return layer

        block = ctx.enter_context(nc.Block())

        @block.sync
        def _(sp):
            part = [slice(c * NT // XC, (c + 1) * NT // XC) for c in range(XC)]
            for c in range(XC):
                sp.dma_start(sh.X[:, part[c], :], args["x"][:, part[c], :]).then_inc(sh.x_loaded[c], 16)
            if choice_w is not None:
                choice_w.sync(sp)
            for n in range(len(layers)):
                stand(n).sync(sp)
            for c in range(XC):
                sp.wait_ge(sh.x_done, (len(LAYERS) - 1) * B + (c + 1) * B // XC)
                sp.dma_start(out[:, part[c], :], sh.X[:, part[c], :]).then_inc(sh.stored, 16)
            sp.wait_ge(sh.stored, 16 * XC)

        @block.tensor
        def _(pe):
            for n in range(len(layers)):
                stand(n).tensor(pe)

        @block.scalar
        def _(act):
            for n in range(len(layers)):
                stand(n).scalar(act)

        @block.vector
        def _(dve):
            if LAYERS[0] != "choice":
                sh.moments.moments_first(dve)
            for n in range(len(layers)):
                stand(n).vector(dve)

        @block.gpsimd
        def _(pool):
            sh.constants(pool)
            sh.moments.scale_first(pool)
            for n in range(len(layers)):
                stand(n).gpsimd(pool)


def laid_out(i):
    import numpy as np
    a = {k: np.asarray(v) for k, v in i.items()}
    t = lambda v: np.ascontiguousarray(v)
    return {
        "x": t(a["L0_attn_x"].reshape(NT, P, C).transpose(1, 0, 2)),
        "rk_cols": t(np.stack([a[n].reshape(C) for n in (
            "L0_attn_time_decay", "L0_attn_time_mix_k", "L0_attn_time_mix_v", "L0_attn_time_mix_r",
            "L0_attn_ln_g", "L0_attn_ln_b")], 1)),
        "rk_w": t(np.concatenate([a[n].T for n in ("L0_attn_Wk", "L0_attn_Wv", "L0_attn_Wr", "L0_attn_Wo")], 1)),
        "ml_wq": t(a["L1_attn_Wq"]),
        "ml_wk": t(a["L1_attn_Wk"]),
        "ml_wvo": t(np.concatenate([a["L1_attn_Wv"], a["L1_attn_Wo"]], 1)),
        "ml_wdown": t(a["L1_attn_Wdown"]),
        "ml_wgate": t(np.concatenate([a["L1_attn_Wig"], a["L1_attn_Wfg"]], 1)),
        "ml_norm_w": t(a["L1_attn_norm_w"].reshape(C, 1)),
        "ml_bias": t(np.concatenate([a["L1_attn_big"], a["L1_attn_bfg"]]).reshape(1, 2 * NH)),
        "ec_gate": t(a["L0_ffn_gate_w"]),
        "ec_w1": t(a["L0_ffn_w1"].transpose(1, 0, 2).reshape(C, E * H0)),
        "ec_w2": t(a["L0_ffn_w2"].reshape(E, HC, P, C).transpose(2, 0, 1, 3).reshape(P, E * H0)),
        "t2_wg": t(a["L1_ffn_w_g"].transpose(1, 0, 2).reshape(C, HID)),
        "t2_wu": t(a["L1_ffn_w_u"].transpose(1, 0, 2).reshape(C, HID)),
        "t2_wd": t(a["L1_ffn_w_d"].reshape(NCH, P, C).transpose(1, 0, 2).reshape(P, HID)),
        "t2_gate": t(a["L1_ffn_w_gate"]),
        "t2_sel": t(np.tile(np.repeat(np.eye(E, dtype=np.float32), M1, axis=1), (2, 1))),
    }


def kernel(**inputs):
    import numpy as np
    import concourse.bacc as bacc
    from concourse.bass_utils import run_bass_kernel_spmd

    nc = bacc.Bacc("TRN2", target_bir_lowering=False, num_devices=1)
    arrays = laid_out(inputs)
    args = {n: nc.dram_tensor(f"in_{n}", a.shape, F32, kind="ExternalInput").ap() for n, a in arrays.items()}
    out = nc.dram_tensor("out_x", (P, NT, C), F32, kind="ExternalOutput").ap()
    build(nc, args, out)
    r = run_bass_kernel_spmd(nc, [{f"in_{n}": a for n, a in arrays.items()}], core_ids=[0])
    y = np.asarray(r.results[0]["out_x"])
    return np.ascontiguousarray(y.transpose(1, 0, 2)).reshape(B, T, C)
```
